# Optimizing a Trainium2 kernel written in Bass

```python
import numpy as np
import jax
import jax.numpy as jnp

def _softmax(x, axis=-1):
    return jax.nn.softmax(x, axis=axis)

def _gelu(x):
    return jax.nn.gelu(x, approximate=True)

def _silu(x):
    return jax.nn.silu(x)

def _sigmoid(x):
    return jax.nn.sigmoid(x)

def _layernorm(x, axis=-1, eps=1e-05):
    m = jnp.mean(x, axis=axis, keepdims=True)
    v = jnp.var(x, axis=axis, keepdims=True)
    return (x - m) / jnp.sqrt(v + eps)

def _scatter_add(tgt, idx, src, axis=0):
    return tgt.at[idx].add(src)

def _segment_sum(src, seg, n):
    return jax.ops.segment_sum(src, seg, n)
kernel_name = 'mk_audio_tower_d2_tok_audfeat2048_r4_04ae67'

def setup_inputs(seed: int=0):
    np.random.seed(seed)
    _w = jnp.asarray

    def _rec_inputs():
        import jax
        import jax.numpy as jnp
        _rk = jax.random.key(seed)
        x = -5.77387e-05 + 0.999872 * jax.random.normal(jax.random.fold_in(_rk, 1), (32, 256, 320), jnp.float32)
        return x
    x = _rec_inputs()

    def _L0_tok_setup():
        import jax, jax.numpy as jnp
        import numpy as np
        K = 4
        E = 4
        TOP_K = 2
        ENC_DIM = 320
        IN_DIM = ENC_DIM * K
        HID = 512
        OUT_DIM = 512
        EPS_NORM = 1e-06
        EPS_GATE = 1e-06

        def _rmsnorm(x, w):
            xf = x.astype(jnp.float32)
            var = jnp.mean(xf * xf, axis=-1, keepdims=True)
            return (w * (xf * jax.lax.rsqrt(var + EPS_NORM))).astype(x.dtype)
        key = jax.random.key(seed)
        ks = jax.random.split(key, 12)
        xav = (6.0 / (IN_DIM + HID)) ** 0.5
        return {'x': jax.random.normal(ks[0], (16, 375, ENC_DIM), dtype=jnp.float32), 'norm_w': jnp.ones((IN_DIM,), dtype=jnp.float32), 'router_w': jax.random.normal(ks[1], (E, IN_DIM), dtype=jnp.float32) * 0.02, 'w1': jax.random.uniform(ks[2], (E, HID, IN_DIM), jnp.float32, -xav, xav), 'b1': jnp.zeros((E, HID), dtype=jnp.float32), 'w2': jax.random.normal(ks[3], (E, OUT_DIM, HID), dtype=jnp.float32) * 0.01, 'b2': jnp.zeros((E, OUT_DIM), dtype=jnp.float32), 'sw1': jax.random.uniform(ks[4], (HID, IN_DIM), jnp.float32, -xav, xav), 'sb1': jnp.zeros((HID,), dtype=jnp.float32), 'sw2': jax.random.normal(ks[5], (OUT_DIM, HID), dtype=jnp.float32) * 0.01, 'sb2': jnp.zeros((OUT_DIM,), dtype=jnp.float32)}
    _L0_tok_all = _L0_tok_setup()
    _L0_tok_in = {k: v for k, v in _L0_tok_all.items() if k in ('norm_w', 'router_w', 'w1', 'b1', 'w2', 'b2', 'sw1', 'sb1', 'sw2', 'sb2')}
    del _L0_tok_all

    def _L0_attn_setup():
        import jax, jax.numpy as jnp
        import numpy as np
        N_EMBD = 512
        N_HEAD = 16
        HEAD_DIM = N_EMBD // N_HEAD
        key = jax.random.key(seed)
        ks = jax.random.split(key, 9)
        s = 0.02
        x = jax.random.normal(ks[0], (4, 512, N_EMBD), dtype=jnp.float32)
        Wq = jax.random.normal(ks[1], (N_EMBD, N_EMBD), dtype=jnp.float32) * s
        bq = jnp.zeros((N_EMBD,), dtype=jnp.float32)
        Wk = jax.random.normal(ks[2], (N_EMBD, N_EMBD), dtype=jnp.float32) * s
        bk = jnp.zeros((N_EMBD,), dtype=jnp.float32)
        Wv = jax.random.normal(ks[3], (N_EMBD, N_EMBD), dtype=jnp.float32) * s
        bv = jnp.zeros((N_EMBD,), dtype=jnp.float32)
        Wp = jax.random.normal(ks[4], (N_EMBD, N_EMBD), dtype=jnp.float32) * s
        bp = jnp.zeros((N_EMBD,), dtype=jnp.float32)
        return {'x': x, 'Wq': Wq, 'bq': bq, 'Wk': Wk, 'bk': bk, 'Wv': Wv, 'bv': bv, 'Wp': Wp, 'bp': bp}
    _L0_attn_all = _L0_attn_setup()
    _L0_attn_in = {k: v for k, v in _L0_attn_all.items() if k in ('Wq', 'bq', 'Wk', 'bk', 'Wv', 'bv', 'Wp', 'bp')}
    del _L0_attn_all

    def _L0_ffn_setup():
        import jax, jax.numpy as jnp
        import numpy as np
        HIDDEN = 512
        INTER = 2048
        RETRIEVAL = 128
        NUM_EXPERTS = 1024
        NUM_KEYS = 64
        TOP_K = 8
        B, S = (4, 512)
        key = jax.random.key(seed)
        ks = jax.random.split(key, 8)
        sc = 0.02
        return {'hidden_states': jax.random.normal(ks[0], (B, S, HIDDEN), jnp.float32), 'W_q': jax.random.normal(ks[1], (HIDDEN, RETRIEVAL), jnp.float32) * sc, 'keys': jax.random.normal(ks[2], (2, RETRIEVAL // 2, NUM_KEYS), jnp.float32) * sc, 'down_embed': jax.random.normal(ks[3], (NUM_EXPERTS, HIDDEN), jnp.float32) * sc, 'up_embed': jax.random.normal(ks[4], (NUM_EXPERTS, HIDDEN), jnp.float32) * sc, 'gate_w': jax.random.normal(ks[5], (HIDDEN, INTER), jnp.float32) * sc, 'up_w': jax.random.normal(ks[6], (HIDDEN, INTER), jnp.float32) * sc, 'down_w': jax.random.normal(ks[7], (INTER, HIDDEN), jnp.float32) * sc}
    _L0_ffn_all = _L0_ffn_setup()
    _L0_ffn_in = {k: v for k, v in _L0_ffn_all.items() if k in ('W_q', 'keys', 'down_embed', 'up_embed', 'gate_w', 'up_w', 'down_w')}
    del _L0_ffn_all

    def _L1_attn_setup():
        import jax, jax.numpy as jnp
        import numpy as np
        B, T, C = (2, 512, 512)
        NH, NKV, HD = (16, 8, 64)
        SOFTCAP = 50.0
        ROPE_BASE = 10000.0

        def _rotate_half(x):
            x1, x2 = (x[..., :x.shape[-1] // 2], x[..., x.shape[-1] // 2:])
            return jnp.concatenate((-x2, x1), axis=-1)

        def _rope_cos_sin(t, head_dim, dtype):
            inv_freq = 1.0 / ROPE_BASE ** (jnp.arange(0, head_dim, 2, dtype=jnp.int32).astype(jnp.float32) / head_dim)
            pos = jnp.arange(t, dtype=jnp.float32)
            freqs = pos[:, None] * inv_freq[None, :]
            emb = jnp.concatenate((freqs, freqs), axis=-1)
            return (jnp.cos(emb).astype(dtype)[None, None], jnp.sin(emb).astype(dtype)[None, None])
        key = jax.random.key(seed)
        ks = jax.random.split(key, 5)
        s = 0.02
        return {'X': jax.random.normal(ks[0], (B, T, C), dtype=jnp.float32), 'Wq': jax.random.normal(ks[1], (C, NH * HD), dtype=jnp.float32) * s, 'Wk': jax.random.normal(ks[2], (C, NKV * HD), dtype=jnp.float32) * s, 'Wv': jax.random.normal(ks[3], (C, NKV * HD), dtype=jnp.float32) * s, 'Wo': jax.random.normal(ks[4], (NH * HD, C), dtype=jnp.float32) * s}
    _L1_attn_all = _L1_attn_setup()
    _L1_attn_in = {k: v for k, v in _L1_attn_all.items() if k in ('Wq', 'Wk', 'Wv', 'Wo')}
    del _L1_attn_all

    def _L1_ffn_setup():
        import jax, jax.numpy as jnp
        import numpy as np
        EPS = 1e-08

        def _quantize(w):
            gamma = jnp.mean(jnp.abs(w))
            return jnp.clip(jnp.round(w / (gamma + EPS)), -1.0, 1.0)

        def _bitlinear(x, w):
            return jnp.matmul(x, _quantize(w).T)
        key = jax.random.key(seed)
        k1, k2, k3, k4 = jax.random.split(key, 4)
        d, h = (512, 1408)
        x = jax.random.normal(k1, (4, 512, d), dtype=jnp.float32)
        w1 = jax.random.normal(k2, (h, d), dtype=jnp.float32)
        w2 = jax.random.normal(k3, (h, d), dtype=jnp.float32)
        w3 = jax.random.normal(k4, (d, h), dtype=jnp.float32)
        return {'x': x, 'w1': w1, 'w2': w2, 'w3': w3}
    _L1_ffn_all = _L1_ffn_setup()
    _L1_ffn_in = {k: v for k, v in _L1_ffn_all.items() if k in ('w1', 'w2', 'w3')}
    del _L1_ffn_all
    return {'x': x, 'L0_tok_norm_w': _L0_tok_in['norm_w'], 'L0_tok_router_w': _L0_tok_in['router_w'], 'L0_tok_w1': _L0_tok_in['w1'], 'L0_tok_b1': _L0_tok_in['b1'], 'L0_tok_w2': _L0_tok_in['w2'], 'L0_tok_b2': _L0_tok_in['b2'], 'L0_tok_sw1': _L0_tok_in['sw1'], 'L0_tok_sb1': _L0_tok_in['sb1'], 'L0_tok_sw2': _L0_tok_in['sw2'], 'L0_tok_sb2': _L0_tok_in['sb2'], 'L0_attn_Wq': _L0_attn_in['Wq'], 'L0_attn_bq': _L0_attn_in['bq'], 'L0_attn_Wk': _L0_attn_in['Wk'], 'L0_attn_bk': _L0_attn_in['bk'], 'L0_attn_Wv': _L0_attn_in['Wv'], 'L0_attn_bv': _L0_attn_in['bv'], 'L0_attn_Wp': _L0_attn_in['Wp'], 'L0_attn_bp': _L0_attn_in['bp'], 'L0_ffn_W_q': _L0_ffn_in['W_q'], 'L0_ffn_keys': _L0_ffn_in['keys'], 'L0_ffn_down_embed': _L0_ffn_in['down_embed'], 'L0_ffn_up_embed': _L0_ffn_in['up_embed'], 'L0_ffn_gate_w': _L0_ffn_in['gate_w'], 'L0_ffn_up_w': _L0_ffn_in['up_w'], 'L0_ffn_down_w': _L0_ffn_in['down_w'], 'L1_attn_Wq': _L1_attn_in['Wq'], 'L1_attn_Wk': _L1_attn_in['Wk'], 'L1_attn_Wv': _L1_attn_in['Wv'], 'L1_attn_Wo': _L1_attn_in['Wo'], 'L1_ffn_w1': _L1_ffn_in['w1'], 'L1_ffn_w2': _L1_ffn_in['w2'], 'L1_ffn_w3': _L1_ffn_in['w3']}

def reference(x, L0_tok_norm_w, L0_tok_router_w, L0_tok_w1, L0_tok_b1, L0_tok_w2, L0_tok_b2, L0_tok_sw1, L0_tok_sb1, L0_tok_sw2, L0_tok_sb2, L0_attn_Wq, L0_attn_bq, L0_attn_Wk, L0_attn_bk, L0_attn_Wv, L0_attn_bv, L0_attn_Wp, L0_attn_bp, L0_ffn_W_q, L0_ffn_keys, L0_ffn_down_embed, L0_ffn_up_embed, L0_ffn_gate_w, L0_ffn_up_w, L0_ffn_down_w, L1_attn_Wq, L1_attn_Wk, L1_attn_Wv, L1_attn_Wo, L1_ffn_w1, L1_ffn_w2, L1_ffn_w3):
    import jax
    import jax.numpy as jnp

    def _L0_tok_ref(x, norm_w, router_w, w1, b1, w2, b2, sw1, sb1, sw2, sb2):
        import jax, jax.numpy as jnp
        import numpy as np
        K = 4
        E = 4
        TOP_K = 2
        ENC_DIM = 320
        IN_DIM = ENC_DIM * K
        HID = 512
        OUT_DIM = 512
        EPS_NORM = 1e-06
        EPS_GATE = 1e-06

        def _rmsnorm(x, w):
            xf = x.astype(jnp.float32)
            var = jnp.mean(xf * xf, axis=-1, keepdims=True)
            return (w * (xf * jax.lax.rsqrt(var + EPS_NORM))).astype(x.dtype)
        B, S, D = x.shape
        out_len = (S - K) // K + 1
        xs = x[:, :out_len * K, :].reshape(B, out_len, D * K)
        xs = _rmsnorm(xs, norm_w)
        flat = xs.reshape(-1, D * K)
        T = flat.shape[0]
        shared = jax.nn.gelu(flat @ sw1.T + sb1, approximate=False) @ sw2.T + sb2
        logits = flat @ router_w.T
        probs = jax.nn.softmax(logits.astype(jnp.float32), axis=-1).astype(flat.dtype)
        tw, ti = jax.lax.top_k(probs, TOP_K)
        tw = tw / (jnp.sum(tw, axis=-1, keepdims=True) + EPS_GATE)
        gates = jnp.zeros((T, E), dtype=flat.dtype).at[jnp.arange(T)[:, None], ti].add(tw)
        h = jax.nn.gelu(jnp.einsum('td,ehd->teh', flat, w1) + b1, approximate=False)
        eo = jnp.einsum('teh,eoh->teo', h, w2) + b2
        sparse = jnp.einsum('teo,te->to', eo, gates)
        return (shared + sparse).reshape(B, out_len, OUT_DIM)

    def _L0_attn_ref(x, Wq, bq, Wk, bk, Wv, bv, Wp, bp):
        import jax, jax.numpy as jnp
        import numpy as np
        N_EMBD = 512
        N_HEAD = 16
        HEAD_DIM = N_EMBD // N_HEAD
        B, T, C = x.shape
        H, HD = (N_HEAD, HEAD_DIM)
        scale = 1.0 / jnp.sqrt(jnp.asarray(HD, dtype=x.dtype))

        def split_heads(y):
            return y.reshape(B, T, H, HD).transpose(0, 2, 1, 3)
        q = split_heads(x @ Wq + bq)
        k = split_heads(x @ Wk + bk)
        v = split_heads(x @ Wv + bv)
        scores = jnp.einsum('bhqd,bhkd->bhqk', q, k) * scale
        causal = jnp.tril(jnp.ones((T, T), dtype=bool))
        float_min = jnp.finfo(x.dtype).min
        scores = jnp.where(causal, scores, float_min)
        attn_w = jax.nn.softmax(scores, axis=-1)
        attn = jnp.einsum('bhqk,bhkd->bhqd', attn_w, v)
        attn = attn.transpose(0, 2, 1, 3).reshape(B, T, C)
        return attn @ Wp + bp

    def _L0_ffn_ref(hidden_states, W_q, keys, down_embed, up_embed, gate_w, up_w, down_w):
        import jax, jax.numpy as jnp
        import numpy as np
        HIDDEN = 512
        INTER = 2048
        RETRIEVAL = 128
        NUM_EXPERTS = 1024
        NUM_KEYS = 64
        TOP_K = 8
        B, S = (4, 512)
        b, s, h = hidden_states.shape
        n = b * s
        queries = (hidden_states @ W_q).reshape(2, n, RETRIEVAL // 2)
        routing = jnp.einsum('tnd,tdk->tnk', queries, keys)
        scores2, idx2 = jax.lax.top_k(routing, TOP_K)
        sx, sy = (scores2[0], scores2[1])
        ix, iy = (idx2[0], idx2[1])
        all_scores = (sx[:, :, None] + sy[:, None, :]).reshape(n, TOP_K * TOP_K)
        all_idx = (ix[:, :, None] * NUM_KEYS + iy[:, None, :]).reshape(n, TOP_K * TOP_K)
        scores, pk = jax.lax.top_k(all_scores, TOP_K)
        indices = jnp.take_along_axis(all_idx, pk, axis=-1)
        de = down_embed[indices]
        ue = up_embed[indices]
        x = hidden_states.reshape(n, h)
        ew = jnp.einsum('nh,nkh->nk', x, de)
        ew = jax.nn.silu(ew) * jax.nn.softmax(scores, axis=-1)
        experts_states = jnp.einsum('nk,nkh->nh', ew, ue).reshape(b, s, h)
        mlp = jax.nn.silu(x @ gate_w) * (x @ up_w) @ down_w
        return mlp.reshape(b, s, h) + experts_states

    def _L1_attn_ref(X, Wq, Wk, Wv, Wo):
        import jax, jax.numpy as jnp
        import numpy as np
        B, T, C = (2, 512, 512)
        NH, NKV, HD = (16, 8, 64)
        SOFTCAP = 50.0
        ROPE_BASE = 10000.0

        def _rotate_half(x):
            x1, x2 = (x[..., :x.shape[-1] // 2], x[..., x.shape[-1] // 2:])
            return jnp.concatenate((-x2, x1), axis=-1)

        def _rope_cos_sin(t, head_dim, dtype):
            inv_freq = 1.0 / ROPE_BASE ** (jnp.arange(0, head_dim, 2, dtype=jnp.int32).astype(jnp.float32) / head_dim)
            pos = jnp.arange(t, dtype=jnp.float32)
            freqs = pos[:, None] * inv_freq[None, :]
            emb = jnp.concatenate((freqs, freqs), axis=-1)
            return (jnp.cos(emb).astype(dtype)[None, None], jnp.sin(emb).astype(dtype)[None, None])
        b, t, c = X.shape
        n_rep = NH // NKV
        q = (X @ Wq).reshape(b, t, NH, HD).transpose(0, 2, 1, 3)
        k = (X @ Wk).reshape(b, t, NKV, HD).transpose(0, 2, 1, 3)
        v = (X @ Wv).reshape(b, t, NKV, HD).transpose(0, 2, 1, 3)
        cos, sin = _rope_cos_sin(t, HD, X.dtype)
        q = q * cos + _rotate_half(q) * sin
        k = k * cos + _rotate_half(k) * sin
        k = jnp.repeat(k, n_rep, axis=1)
        v = jnp.repeat(v, n_rep, axis=1)
        scale = 256.0 ** (-0.5)
        att = jnp.einsum('bhqd,bhkd->bhqk', q, k) * scale
        att = SOFTCAP * jnp.tanh(att / SOFTCAP)
        causal = jnp.tril(jnp.ones((t, t), dtype=bool))
        att = jnp.where(causal[None, None], att, -jnp.inf)
        att = jax.nn.softmax(att, axis=-1)
        y = jnp.einsum('bhqk,bhkd->bhqd', att, v)
        y = y.transpose(0, 2, 1, 3).reshape(b, t, NH * HD)
        return y @ Wo

    def _L1_ffn_ref(x, w1, w2, w3):
        import jax, jax.numpy as jnp
        import numpy as np
        EPS = 1e-08

        def _quantize(w):
            gamma = jnp.mean(jnp.abs(w))
            return jnp.clip(jnp.round(w / (gamma + EPS)), -1.0, 1.0)

        def _bitlinear(x, w):
            return jnp.matmul(x, _quantize(w).T)
        x1 = _bitlinear(x, w1)
        x2 = _bitlinear(x, w2)
        hidden = jax.nn.sigmoid(x1) * x2
        return _bitlinear(hidden, w3)
    h = _L0_tok_ref(x, L0_tok_norm_w, L0_tok_router_w, L0_tok_w1, L0_tok_b1, L0_tok_w2, L0_tok_b2, L0_tok_sw1, L0_tok_sb1, L0_tok_sw2, L0_tok_sb2)
    h = h + _L0_attn_ref(_layernorm(h, axis=-1), L0_attn_Wq, L0_attn_bq, L0_attn_Wk, L0_attn_bk, L0_attn_Wv, L0_attn_bv, L0_attn_Wp, L0_attn_bp)
    h = h + _L0_ffn_ref(_layernorm(h, axis=-1), L0_ffn_W_q, L0_ffn_keys, L0_ffn_down_embed, L0_ffn_up_embed, L0_ffn_gate_w, L0_ffn_up_w, L0_ffn_down_w)
    h = h + _L1_attn_ref(_layernorm(h, axis=-1), L1_attn_Wq, L1_attn_Wk, L1_attn_Wv, L1_attn_Wo)
    h = h + _L1_ffn_ref(_layernorm(h, axis=-1), L1_ffn_w1, L1_ffn_w2, L1_ffn_w3)
    return h

_drawn_inputs = setup_inputs


def setup_inputs(seed=0):
    import zlib

    import numpy as np

    out = dict(_drawn_inputs(seed))
    spreads = {'L0_tok_norm_w': (1.0, 0.2),
     'L0_tok_b1': (0.0, 0.1),
     'L0_tok_b2': (0.0, 0.1),
     'L0_tok_sb1': (0.0, 0.1),
     'L0_tok_sb2': (0.0, 0.1),
     'L0_attn_bq': (0.0, 0.8),
     'L0_attn_bk': (0.0, 0.8),
     'L0_attn_bv': (0.0, 0.1),
     'L0_attn_bp': (0.0, 0.1)}
    factors = {'L0_ffn_W_q': 8.0,
     'L0_ffn_keys': 8.0,
     'L0_ffn_down_embed': 4.798,
     'L0_ffn_up_embed': 4.823,
     'L1_attn_Wq': 2.918,
     'L1_attn_Wk': 2.987}
    for name, (base, spread) in spreads.items():
        noise = np.random.default_rng([zlib.crc32(name.encode()), seed]).standard_normal(out[name].shape)
        drawn = base * np.exp(spread * noise) if base else spread * noise
        out[name] = jnp.asarray(drawn.astype(out[name].dtype))
    for name, factor in factors.items():
        out[name] = (out[name] * factor).astype(out[name].dtype)
    return out
```

```python
from contextlib import ExitStack

import numpy as np

import concourse.bass as bass
from concourse import mybir

F32 = mybir.dt.float32
F32R = mybir.dt.float32r
BF16 = mybir.dt.bfloat16
U32 = mybir.dt.uint32
ALU = mybir.AluOpType
ACT = mybir.ActivationFunctionType
AX = mybir.AxisListType

P = 128
CLIPS, CLIP = 32, 64
TOK = CLIPS * CLIP
TILES = TOK // P
D = 512
DC = D // P
BLK = 512
BT = BLK // P
NBLK = TOK // BLK
PACK = 1280
PC = PACK // P
EXPERTS = 4
MLPS = EXPERTS + 1
HID = 512
HC = HID // P
BIG = 1.0e30


class Stage:

    def __init__(self, nc, name):
        self.nc, self.name, self.ctx = nc, name, ExitStack()
        self.sems = []

    def __enter__(self):
        return self

    def __exit__(self, *a):
        self.nc.clear_and_free_semaphores(self.sems)
        self.nc.all_engine_barrier()
        self.ctx.close()

    def sb(self, name, shape, dt=F32):
        return self.ctx.enter_context(self.nc.sbuf_tensor(f"{self.name}_{name}", shape, dt))

    def ps(self, name, shape, dt=F32):
        return self.ctx.enter_context(self.nc.psum_tensor(f"{self.name}_{name}", shape, dt))

    def sem(self, name):
        self.sems.append(self.nc.alloc_semaphore(f"{self.name}_{name}"))
        return self.sems[-1]

    def block(self):
        return self.nc.Block()


def product(pe, out, left, right, start, stop):
    pe.matmul(out, left[0], right[0], start=start, stop=False)
    pe.matmul(out, left[0], right[1], start=False, stop=False)
    return pe.matmul(out, left[1], right[0], start=False, stop=stop)


class Norm:

    def __init__(self, s, nc, h, ident, turn, turns=NBLK):
        self.turns = turns
        self.nc, self.h, self.ident, self.turn = nc, h, ident, turn
        self.stat = s.sb("ln_stat", [P, BT, 6])
        self.moment = s.sb("ln_moment", [P, BT, 2])
        self.shifted = s.sb("ln_shifted", [P, BT])
        self.rstd = s.sb("ln_rstd", [P, BT])
        self.minus_half = s.sb("ln_minus_half", [P, BT])
        self.xn = s.sb("xn", [P, BT, D])
        self.xT = s.sb("xT", [P, 2, DC, BLK], F32R)
        self.const = s.sem("ln_const")
        self.passed = s.sem("ln_passed")
        self.stat_ready = s.sem("ln_stat_ready")
        self.moment_ready = s.sem("ln_moment_ready")
        self.pool_step = s.sem("ln_pool_step")
        self.rstd_ready = s.sem("ln_rstd_ready")
        self.xn_ready = s.sem("xn_ready")
        self.turned = s.sem("xn_turned")
        self.xT_high = s.sem("xT_high")
        self.xT_ready = s.sem("xT_ready")

    def pool_rstd(self, pool):
        pool.memset(self.minus_half[:], -0.5).then_inc(self.const, 1)
        pool.wait_ge(self.const, 1)
        for n in range(self.turns):
            pool.wait_ge(self.moment_ready, n * BT + BT)
            pool.tensor_scalar(self.shifted[:], self.moment[:, :, 1], 1e-5, None, ALU.add).then_inc(self.pool_step, 1)
            pool.wait_ge(self.pool_step, n + 1)
            if n:
                pool.wait_ge(self.xn_ready, n * BT)
            pool.tensor_tensor(self.rstd[:], self.shifted[:], self.minus_half[:], ALU.pow).then_inc(self.rstd_ready, 1)

    def dve_scale(self, dve, n, b, first=False):
        if not first:
            dve.wait_ge(self.xn_ready, n * BT)
            dve.wait_ge(self.moment_ready, n * BT)
            dve.wait_ge(self.turned, n * DC)
        for t in range(BT):
            dve.bn_stats(self.stat[:, t, :], self.h[:, b * BT + t, :]).then_inc(self.stat_ready, 1)
        dve.wait_ge(self.stat_ready, n * BT + BT)
        dve.sem_inc(self.passed, 1)
        for t in range(BT):
            dve.bn_aggr(self.moment[:, t, :], self.stat[:, t, :]).then_inc(self.moment_ready, 1)
        dve.wait_ge(self.rstd_ready, n + 1)
        for t in range(BT):
            dve.tensor_scalar(self.xn[:, t, :], self.h[:, b * BT + t, :], self.moment[:, t, 0:1], self.rstd[:, t:t + 1],
                              ALU.subtract, ALU.mult).then_inc(self.xn_ready, 1)

    def pe_turn_chunk(self, pe, n, k, first=False):
        if k == 0:
            pe.wait_ge(self.xn_ready, n * BT + BT)
        if not (first and k == 0):
            pe.wait_ge(self.xT_ready, n * DC + k)
        for t in range(BT):
            ins = pe.transpose(self.turn[:, t * P:(t + 1) * P], self.xn[:, t, k * P:(k + 1) * P], self.ident[:])
        ins.then_inc(self.turned, 1)

    def act_high_chunk(self, act, n, k):
        act.wait_ge(self.turned, n * DC + k + 1)
        self.nc.scalar.activation(self.xT[:, 0, k, :], self.turn[:], ACT.Copy).then_inc(self.xT_high, 1)

    def dve_low_chunk(self, dve, n, k):
        dve.wait_ge(self.xT_high, n * DC + k + 1)
        dve.tensor_tensor(self.xT[:, 1, k, :], self.turn[:], self.xT[:, 0, k, :].bitcast(F32),
                          ALU.subtract).then_inc(self.xT_ready, 1)

    def pe_turn(self, pe, n, first=False):
        for k in range(DC):
            self.pe_turn_chunk(pe, n, k, first)

    def act_high(self, act, n):
        for k in range(DC):
            self.act_high_chunk(act, n, k)

    def dve_low(self, dve, n):
        for k in range(DC):
            self.dve_low_chunk(dve, n, k)


class Resident:

    def __init__(self, s, nc, pieces):
        self.nc, self.pieces = nc, pieces
        self.raw = s.sb("w_raw", [P, 2, DC * D])
        self.w = s.sb("w", [P, pieces, 2, DC * D], F32R)
        self.loaded = [s.sem(f"w_loaded{i}") for i in range(2)]
        self.high = s.sem("w_high")
        self.ready = s.sem("w_ready")

    def load(self, sp, src):
        for n in range(self.pieces):
            if n >= 2:
                sp.wait_ge(self.ready, n - 1)
            sp.dma_start(self.raw[:, n % 2, :], src[n]).then_inc(self.loaded[n % 2], 16)

    def split_high(self, act):
        for n in range(self.pieces):
            act.wait_ge(self.loaded[n % 2], 16 * (n // 2 + 1))
            self.nc.scalar.activation(self.w[:, n, 0, :], self.raw[:, n % 2, :], ACT.Copy).then_inc(self.high, 1)

    def split_low(self, dve):
        for n in range(self.pieces):
            dve.wait_ge(self.high, n + 1)
            dve.tensor_tensor(self.w[:, n, 1, :], self.raw[:, n % 2, :], self.w[:, n, 0, :].bitcast(F32),
                              ALU.subtract).then_inc(self.ready, 1)

    def pair(self, n, k, c0, c1):
        return [self.w[:, n, i, k * D + c0:k * D + c1] for i in range(2)]


def token_blocks(eng, body):
    with eng.Fori(0, NBLK - 1) as b:
        body(b, False)
    body(NBLK - 1, True)


def token_stage(nc, h, ident, a):
    UNIT = PC * P + D
    with Stage(nc, "tok") as s:
        x_in = s.sb("x_in", [P, BT, PACK])
        square = s.sb("square", [P, PACK])
        sumsq = s.sb("sumsq", [P, BT])
        rstd = s.sb("rstd", [P, BT])
        meansq = s.sb("meansq", [P, BT])
        minus_half = s.sb("minus_half", [P, BT])
        norm_w = s.sb("norm_w", [P, PC])
        router = s.sb("router", [P, PC * EXPERTS])
        router_hl = s.sb("router_hl", [P, 2, PC, EXPERTS], F32R)
        b1 = s.sb("b1", [P, MLPS, HC])
        b2 = s.sb("b2", [MLPS, D])
        xT = s.sb("xT", [P, 2, PC, BLK], F32R)
        raw = s.sb("raw", [P, 2, UNIT])
        w = s.sb("w", [P, HC, 2, UNIT], F32R)
        hid = s.sb("hid", [P, 2, BLK])
        hidT = s.sb("hidT", [P, HC, 2, BLK], F32R)
        logit_max = s.sb("logit_max", [P, BT])
        logit = s.sb("logit", [P, BT, EXPERTS])
        prob = s.sb("prob", [P, BT, EXPERTS])
        total = s.sb("total", [P, BT])
        rank = s.sb("rank", [P, BT, EXPERTS])
        beats = s.sb("beats", [P, 3, BT, EXPERTS])
        top = s.sb("top", [P, BT, EXPERTS])
        top_sum = s.sb("top_sum", [P, BT])
        gate = s.sb("gate", [P, BT, MLPS])
        gateT = s.sb("gateT", [MLPS, BLK])

        turn = [s.ps(f"turn{i}", [P, BLK]) for i in range(2)]
        ps1 = [s.ps(f"ps1_{i}", [P, BLK]) for i in range(2)]
        ps2 = [s.ps(f"ps2_{i}", [P, D]) for i in range(BT)]

        small_in = s.sem("small_in")
        x_loaded = s.sem("x_loaded")
        raw_loaded = [s.sem(f"raw_loaded{i}") for i in range(2)]
        raw_free = s.sem("raw_free")
        consts = s.sem("consts")
        sumsq_ready = s.sem("sumsq_ready")
        rstd_ready = s.sem("rstd_ready")
        pool_step = s.sem("pool_step")
        router_high = s.sem("router_high")
        router_ready = s.sem("router_ready")
        xn_ready = s.sem("xn_ready")
        turned = s.sem("turned")
        turn_free = s.sem("turn_free")
        xT_high = s.sem("xT_high")
        w_high = s.sem("w_high")
        w_ready = s.sem("w_ready")
        unit_used = s.sem("unit_used")
        l1_done = s.sem("l1_done")
        hid_ready = s.sem("hid_ready")
        hid_step = s.sem("hid_step")
        hidT_ready = s.sem("hidT_ready")
        max_ready = s.sem("max_ready")
        exp_ready = s.sem("exp_ready")
        gate_step = s.sem("gate_step")
        gate_ready = s.sem("gate_ready")
        gateT_ready = s.sem("gateT_ready")
        bias_done = s.sem("bias_done")
        l2_done = s.sem("l2_done")
        ps2_free = s.sem("ps2_free")

        UB = MLPS * HC
        TURNS = PC + 2
        AHEAD = HC - 1
        GATE_STEPS = 12
        START = 1

        def blocks(eng, body):
            with eng.Fori(0, NBLK - 1) as b:
                body(b, False)
            body(NBLK - 1, True)

        def mlps(eng, body):
            body(0, True, False)
            with eng.Fori(1, MLPS - 1) as e:
                body(e, False, False)
            body(MLPS - 1, False, True)

        with s.block() as block:

            @block.sync
            def _(sp):
                for dst, src in ((norm_w, a["norm_w"]), (router, a["router"]), (b2, a["b2"])):
                    sp.dma_start(dst[:], src).then_inc(small_in, 16)
                sp.dma_start(b1[:], a["b1"]).then_inc(small_in, 16)
                sp.dma_start(x_in[:], a["x"][0]).then_inc(x_loaded, 16)

                def of_block(b, last):
                    def of_mlp(e, first, last_mlp):
                        for m in range(HC):
                            sp.wait_ge(raw_free, (b * MLPS + e) * HC + m + 1)
                            sp.dma_start(raw[:, m % 2, :], a["w_units"][e * HC + m]).then_inc(raw_loaded[m % 2], 16)
                        if first and not last:
                            sp.wait_ge(turned, b * TURNS + PC)
                            sp.dma_start(x_in[:], a["x"][b + 1]).then_inc(x_loaded, 16)
                    mlps(sp, of_mlp)
                blocks(sp, of_block)

            @block.gpsimd
            def _(pool):
                pool.memset(minus_half[:], -0.5).then_inc(consts, 1)
                pool.wait_ge(consts, 1)
                for b in range(NBLK):
                    pool.wait_ge(sumsq_ready, b * BT + BT)
                    pool.tensor_scalar(meansq[:], sumsq[:], 1.0 / PACK, 1e-6, ALU.mult, ALU.add).then_inc(pool_step, 1)
                    pool.wait_ge(pool_step, b + 1)
                    if b:
                        pool.wait_ge(xn_ready, b * BT)
                    pool.tensor_tensor(rstd[:], meansq[:], minus_half[:], ALU.pow).then_inc(rstd_ready, 1)

            @block.scalar
            def _(act):
                act.sem_inc(hid_ready, START)
                act.wait_ge(small_in, 64)
                nc.scalar.activation(router_hl[:, 0].rearrange("p c e -> p (c e)"), router[:], ACT.Copy).then_inc(router_high, 1)

                def squares(nb):
                    act.wait_ge(x_loaded, nb * 16 + 16)
                    for t in range(BT):
                        if t:
                            act.wait_ge(sumsq_ready, nb * BT + t)
                        nc.scalar.activation(square[:], x_in[:, t, :], ACT.Square,
                                             accum_out=sumsq[:, t:t + 1]).then_inc(sumsq_ready, 1)

                def split_high(b, e, m):
                    n = b * MLPS + e
                    act.wait_ge(raw_loaded[m % 2], 16 * (n * 2 + m // 2 + 1))
                    act.wait_ge(unit_used, n * HC + m + 1)
                    nc.scalar.activation(w[:, m, 0, :], raw[:, m % 2, :], ACT.Copy).then_inc(w_high, 1)

                squares(0)
                for m in range(AHEAD):
                    split_high(0, 0, m)

                def of_block(b, last):
                    for kc in range(PC):
                        act.wait_ge(turned, b * TURNS + kc + 1)
                        if kc == 0:
                            act.wait_ge(l1_done, START + b * UB)
                        nc.scalar.activation(xT[:, 0, kc, :], turn[kc % 2][:], ACT.Copy,
                                             scale=norm_w[:, kc:kc + 1]).then_inc(xT_high, 1)
                    act.wait_ge(max_ready, b + 1)
                    nc.scalar.activation(prob[:], logit[:], ACT.Exp).then_inc(exp_ready, 1)

                    def of_mlp(e, first, last_mlp):
                        n = b * MLPS + e
                        for m in range(HC):
                            act.wait_ge(l1_done, START + n * HC + m + 1)
                            act.wait_ge(hidT_ready, START + n * HC + m)
                            nc.scalar.activation(hid[:, m % 2, :], ps1[m % 2][:], ACT.Gelu,
                                                 bias=b1[:, bass.ds(e, 1), m]).then_inc(hid_ready, 1)
                            if m == 0:
                                split_high(b, e, AHEAD)
                            elif not last_mlp:
                                split_high(b, e + 1, m - 1)
                            elif not last:
                                split_high(b + 1, 0, m - 1)
                        if last_mlp and not last:
                            act.wait_ge(rstd_ready, b + 1)
                            act.wait_ge(sumsq_ready, (b + 1) * BT)
                            squares(b + 1)
                    mlps(act, of_mlp)
                blocks(act, of_block)

            @block.vector
            def _(dve):
                dve.sem_inc(hidT_ready, START)
                dve.memset(gate[:, :, EXPERTS:], 1.0).then_inc(gate_step, 1)
                dve.wait_ge(router_high, 1)
                dve.tensor_tensor(router_hl[:, 1].rearrange("p c e -> p (c e)"), router[:],
                                  router_hl[:, 0].rearrange("p c e -> p (c e)").bitcast(F32),
                                  ALU.subtract).then_inc(router_ready, 1)

                def normalise(nb):
                    dve.wait_ge(rstd_ready, nb + 1)
                    for t in range(BT):
                        dve.tensor_scalar(x_in[:, t, :], x_in[:, t, :], rstd[:, t:t + 1], None,
                                          ALU.mult).then_inc(xn_ready, 1)

                def split_low(b, e, m):
                    n = b * MLPS + e
                    dve.wait_ge(w_high, n * HC + m + 1)
                    dve.tensor_tensor(w[:, m, 1, :], raw[:, m % 2, :], w[:, m, 0, :].bitcast(F32),
                                      ALU.subtract).then_inc(w_ready, 1)
                    dve.wait_ge(w_ready, n * HC + m + 1)
                    dve.sem_inc(raw_free, 1)

                dve.sem_inc(raw_free, 2)
                normalise(0)
                for m in range(AHEAD):
                    split_low(0, 0, m)

                def gates(b):
                    G = 1 + b * GATE_STEPS
                    step = [0]

                    def chain(ins):
                        step[0] += 1
                        ins.then_inc(gate_step, 1)
                        dve.wait_ge(gate_step, G + step[0])

                    dve.wait_ge(turned, b * TURNS + PC + 1)
                    lg = turn[0][:, 0:BT * EXPERTS].rearrange("p (t e) -> p t e", t=BT)
                    chain(dve.tensor_reduce(logit_max[:], lg, AX.X, ALU.max))
                    dve.tensor_tensor(logit[:], lg, logit_max[:].rearrange("p (t o) -> p t o", o=1).broadcast_to([P, BT, EXPERTS]),
                                      ALU.subtract).then_inc(max_ready, 1)
                    dve.wait_ge(max_ready, b + 1)
                    dve.sem_inc(turn_free, 1)
                    dve.wait_ge(exp_ready, b + 1)
                    chain(dve.tensor_reduce(total[:], prob[:], AX.X, ALU.add))
                    for e in range(EXPERTS):
                        mine = prob[:, :, e:e + 1]
                        k = 0
                        for o in range(EXPERTS):
                            if o != e:
                                ins = dve.tensor_tensor(beats[:, k, :, e:e + 1], prob[:, :, o:o + 1], mine,
                                                        ALU.is_ge if o < e else ALU.is_gt)
                                k += 1
                    chain(ins)
                    chain(dve.tensor_tensor(rank[:], beats[:, 0], beats[:, 1], ALU.add))
                    chain(dve.tensor_tensor(rank[:], rank[:], beats[:, 2], ALU.add))
                    chain(dve.tensor_scalar(rank[:], rank[:], 2.0, None, ALU.is_lt))
                    chain(dve.reciprocal(total[:], total[:]))
                    chain(dve.tensor_tensor(prob[:], prob[:], total[:].rearrange("p (t o) -> p t o", o=1).broadcast_to([P, BT, EXPERTS]), ALU.mult))
                    chain(dve.tensor_tensor(top[:], prob[:], rank[:], ALU.mult))
                    chain(dve.tensor_reduce(top_sum[:], top[:], AX.X, ALU.add))
                    chain(dve.tensor_scalar(top_sum[:], top_sum[:], 1e-6, None, ALU.add))
                    chain(dve.reciprocal(top_sum[:], top_sum[:]))
                    dve.tensor_tensor(gate[:, :, 0:EXPERTS], top[:], top_sum[:].rearrange("p (t o) -> p t o", o=1).broadcast_to([P, BT, EXPERTS]),
                                      ALU.mult).then_inc(gate_ready, 1)

                def of_block(b, last):
                    for kc in range(PC):
                        dve.wait_ge(xT_high, b * PC + kc + 1)
                        dve.scalar_tensor_tensor(out=xT[:, 1, kc, :], in0=turn[kc % 2][:], scalar=norm_w[:, kc:kc + 1],
                                                 in1=xT[:, 0, kc, :].bitcast(F32), op0=ALU.mult,
                                                 op1=ALU.subtract).then_inc(turn_free, 1)
                    gates(b)
                    dve.wait_ge(turned, b * TURNS + PC + 2)
                    dve.tensor_copy(gateT[:], turn[1][0:MLPS, :]).then_inc(gateT_ready, 1)
                    dve.wait_ge(gateT_ready, b + 1)
                    dve.sem_inc(turn_free, 1)

                    def take(e, t):
                        n = b * MLPS + e
                        if t < BT - 1:
                            dve.wait_ge(l2_done, n * (BT - 1) + t + 1)
                        else:
                            dve.wait_ge(unit_used, HC + (n + 1) * HC)
                        dve.scalar_tensor_tensor(out=h[:, b * BT + t, :], in0=ps2[t][:], scalar=gate[:, t, bass.ds(e, 1)],
                                                 in1=h[:, b * BT + t, :], op0=ALU.mult,
                                                 op1=ALU.add).then_inc(ps2_free, 1)

                    def of_mlp(e, first, last_mlp):
                        n = b * MLPS + e
                        for m in range(HC):
                            dve.wait_ge(hid_ready, START + n * HC + m + 1)
                            dve.tensor_copy(hidT[:, m, 0, :], hid[:, m % 2, :]).then_inc(hid_step, 1)
                            dve.wait_ge(hid_step, n * HC + m + 1)
                            dve.tensor_tensor(hidT[:, m, 1, :], hid[:, m % 2, :], hidT[:, m, 0, :].bitcast(F32),
                                              ALU.subtract).then_inc(hidT_ready, 1)
                            if m == 1 and first:
                                for t in range(BT):
                                    dve.wait_ge(bias_done, b * BT + t + 1)
                                    dve.tensor_copy(h[:, b * BT + t, :], ps2[t][:]).then_inc(ps2_free, 1)
                            if m == 0 and not first:
                                for t in range(BT):
                                    take(e - 1, t)
                            if m == 0:
                                split_low(b, e, AHEAD)
                            elif not last_mlp:
                                split_low(b, e + 1, m - 1)
                            elif not last:
                                split_low(b + 1, 0, m - 1)
                        if last_mlp:
                            for t in range(BT):
                                take(e, t)
                            if not last:
                                normalise(b + 1)
                    mlps(dve, of_mlp)
                blocks(dve, of_block)

            @block.tensor
            def _(pe):
                pe.sem_inc(l1_done, START)
                pe.sem_inc(unit_used, HC)
                pe.sem_inc(turn_free, 2)
                pe.sem_inc(ps2_free, BT)
                pe.wait_ge(router_ready, 1)

                def of_block(b, last):
                    NB = b * (MLPS + 1) * BT
                    pe.wait_ge(xn_ready, b * BT + BT)
                    for kc in range(PC):
                        pe.wait_ge(turn_free, b * TURNS + kc + 1)
                        for t in range(BT):
                            ins = pe.transpose(turn[kc % 2][:, t * P:(t + 1) * P],
                                               x_in[:, t, kc * P:(kc + 1) * P], ident[:])
                        ins.then_inc(turned, 1)
                    pe.wait_ge(turn_free, b * TURNS + PC + 2)
                    for t in range(BT):
                        for kc in range(PC):
                            ins = product(pe, turn[0][:, t * EXPERTS:(t + 1) * EXPERTS],
                                          [xT[:, i, kc, t * P:(t + 1) * P] for i in range(2)],
                                          [router_hl[:, i, kc, :] for i in range(2)],
                                          kc == 0, kc == PC - 1)
                    ins.then_inc(turned, 1)

                    def layer1(e, m):
                        n = b * MLPS + e
                        pe.wait_ge(w_ready, n * HC + m + 1)
                        pe.wait_ge(hid_ready, START + n * HC + max(m - 1, 0))
                        for kc in range(PC):
                            ins = product(pe, ps1[m % 2][:],
                                          [w[:, m, i, kc * P:(kc + 1) * P] for i in range(2)],
                                          [xT[:, i, kc, :] for i in range(2)], kc == 0, kc == PC - 1)
                        ins.then_inc(l1_done, 1)

                    def layer2(e, m):
                        n = b * MLPS + e
                        pe.wait_ge(hidT_ready, START + n * HC + m + 1)
                        for t in range(BT):
                            if m == 0:
                                pe.wait_ge(ps2_free, NB + (e + 1) * BT + t + 1)
                            ins = product(pe, ps2[t][:],
                                          [hidT[:, m, i, t * P:(t + 1) * P] for i in range(2)],
                                          [w[:, m, i, PC * P:] for i in range(2)], m == 0, m == HC - 1)
                            if t == BT - 1:
                                ins.then_inc(unit_used, 1)
                            elif m == HC - 1:
                                ins.then_inc(l2_done, 1)

                    def of_mlp(e, first, last_mlp):
                        layer1(e, 0)
                        if first:
                            pe.wait_ge(gate_ready, b + 1)
                            pe.wait_ge(turn_free, b * TURNS + PC + 2)
                            for t in range(BT):
                                ins = pe.transpose(turn[1][0:MLPS, t * P:(t + 1) * P], gate[:, t, :], ident[:])
                            ins.then_inc(turned, 1)
                        else:
                            layer2(e - 1, HC - 1)
                        layer1(e, 1)
                        if first:
                            pe.wait_ge(gateT_ready, b + 1)
                            for t in range(BT):
                                pe.wait_ge(ps2_free, NB + t + 1)
                                pe.matmul(ps2[t][:], gateT[:, t * P:(t + 1) * P], b2[:], start=True,
                                          stop=True).then_inc(bias_done, 1)
                        layer2(e, 0)
                        layer1(e, 2)
                        layer2(e, 1)
                        layer1(e, 3)
                        layer2(e, 2)
                        if last_mlp:
                            layer2(e, 3)
                    mlps(pe, of_mlp)
                blocks(pe, of_block)


def attention_stage(nc, h, ident, a):
    HEADS, HD = 16, 32
    SCALE = float(np.float32(1.0) / np.sqrt(np.float32(HD)))
    GROUP = P // HD
    UNITS = HEADS
    SLOTS = 4
    SUMS = 2 * SLOTS
    with Stage(nc, "at0") as s:
        turn = s.ps("turn", [P, BLK])
        mm = [s.ps(f"mm{i}", [P, BLK]) for i in range(2)]
        score = [s.ps(f"score{i}", [P, BT, P]) for i in range(GROUP)]
        probT_ps = s.ps("probT_ps", [P, BT, P])
        o_ps = [mm[i][:, 0:BT * HD].rearrange("p (t d) -> p t d", t=BT) for i in range(2)]
        oT_ps = turn[:].rearrange("p (c q) -> p c q", c=DC)
        ln = Norm(s, nc, h, ident, turn)
        w = Resident(s, nc, 4)
        WQ, WK, WV, WP = range(4)
        bq = s.sb("bq", [P, DC])
        bq_negated = s.sb("bq_negated", [P, DC])
        bk = s.sb("bk", [P, DC])
        bv = s.sb("bv", [P, D])
        bp = s.sb("bp", [P, D])
        mask = s.sb("mask", [P, P])
        qT = s.sb("qT", [P, DC, BLK])
        kT = s.sb("kT", [P, DC, BLK])
        v = s.sb("v", [P, BT, D])
        masked = s.sb("masked", [P, SLOTS, BT, P])
        least = s.sb("least", [P, SLOTS, BT])
        prob = w.raw[:, 0, :].rearrange("p (s t k) -> p s t k", s=SLOTS, t=BT)
        o = w.raw[:, 1, :].rearrange("p (t n) -> p t n", t=BT)
        psum_ = s.sb("prob_sum", [P, SUMS, BT])
        inv_sum = s.sb("inv_sum", [P, 2, BT])
        probT = s.sb("probT", [P, SLOTS, BT, P])
        oT = s.sb("oT", [P, 2, BT, DC, P], F32R)
        biased = s.sb("biased", [P, D])

        small_in = s.sem("small_in")
        bias_ready = s.sem("bias_ready")
        mm_done = s.sem("mm_done")
        mm_free = [s.sem(f"mm_free{i}") for i in range(2)]
        qk_ready = s.sem("qk_ready")
        v_ready = s.sem("v_ready")
        score_done = s.sem("score_done")
        masked_ready = s.sem("masked_ready")
        least_ready = s.sem("least_ready")
        prob_ready = s.sem("prob_ready")
        prob_turned = s.sem("prob_turned")
        probT_ready = s.sem("probT_ready")
        o_done = s.sem("o_done")
        inv_ready = s.sem("inv_ready")
        o_ready = s.sem("o_ready")
        o_turned = s.sem("o_turned")
        oT_high = s.sem("oT_high")
        oT_ready = s.sem("oT_ready")
        biased_ready = s.sem("biased_ready")
        h_ready = s.sem("h_ready")

        MM = 4 * DC
        with s.block() as block:

            @block.sync
            def _(sp):
                for dst, src in ((bq, "bq"), (bk, "bk"), (mask, "mask")):
                    sp.dma_start(dst[:], a[src]).then_inc(small_in, 16)
                for dst, src in ((bv, "bv"), (bp, "bp")):
                    sp.dma_start(dst[:], a[src].partition_broadcast(P)).then_inc(small_in, 16)
                w.load(sp, a["w_at0"])

            @block.gpsimd
            def _(pool):
                ln.pool_rstd(pool)

            @block.scalar
            def _(act):
                act.wait_ge(small_in, 80)
                nc.scalar.activation(bq_negated[:], bq[:], ACT.Copy, scale=-SCALE).then_inc(bias_ready, 1)
                w.split_high(act)
                ln.act_high(act, 0)
                act.wait_ge(bias_ready, 1)

                def of_block(b, last):
                    for c in range(DC):
                        act.wait_ge(mm_done, b * MM + 2 * c + 1)
                        nc.scalar.activation(qT[:, c, :], mm[0][:], ACT.Identity, bias=bq_negated[:, c:c + 1],
                                             scale=-SCALE).then_inc(qk_ready, 1)
                        act.wait_ge(qk_ready, b * 2 * DC + 2 * c + 1)
                        act.sem_inc(mm_free[0], 1)
                        act.wait_ge(mm_done, b * MM + 2 * c + 2)
                        nc.scalar.activation(kT[:, c, :], mm[1][:], ACT.Identity, bias=bk[:, c:c + 1]).then_inc(qk_ready, 1)
                        act.wait_ge(qk_ready, b * 2 * DC + 2 * c + 2)
                        act.sem_inc(mm_free[1], 1)
                    if not last:
                        ln.act_high(act, b + 1)

                    def copy_probT(u):
                        n = b * UNITS + u
                        act.wait_ge(prob_turned, n + 1)
                        if u >= SLOTS:
                            act.wait_ge(o_done, n - SLOTS + 1)
                        nc.scalar.activation(probT[:, u % SLOTS], probT_ps[:], ACT.Copy).then_inc(probT_ready, 1)

                    for u in range(UNITS):
                        n = b * UNITS + u
                        act.wait_ge(least_ready, n + 1)
                        if u >= SLOTS:
                            act.wait_ge(prob_turned, n - SLOTS + 1)
                        if u >= SUMS:
                            act.wait_ge(o_ready, n - SUMS + 1)
                        for t in range(BT):
                            nc.scalar.activation(prob[:, u % SLOTS, t, :], masked[:, u % SLOTS, t, :], ACT.Exp,
                                                 bias=least[:, u % SLOTS, t:t + 1], scale=-1.0,
                                                 accum_out=psum_[:, u % SUMS, t:t + 1]).then_inc(prob_ready, 1)
                        if u:
                            copy_probT(u - 1)
                    copy_probT(UNITS - 1)
                    for t in range(BT):
                        act.wait_ge(o_turned, b * BT + t + 1)
                        nc.scalar.activation(oT[:, 0, t], oT_ps[:], ACT.Copy).then_inc(oT_high, 1)
                token_blocks(act, of_block)

            @block.vector
            def _(dve):
                ln.dve_scale(dve, 0, 0, first=True)
                w.split_low(dve)
                ln.dve_low(dve, 0)
                dve.sem_inc(h_ready, BT)

                def of_block(b, last):
                    if not last:
                        ln.dve_scale(dve, b + 1, b + 1)
                    for t in range(BT):
                        j = 2 * DC + t
                        dve.wait_ge(mm_done, b * MM + j + 1)
                        dve.tensor_tensor(v[:, t, :], mm[j % 2][:], bv[:], ALU.add).then_inc(v_ready, 1)
                        dve.wait_ge(v_ready, b * BT + t + 1)
                        dve.sem_inc(mm_free[j % 2], 1)
                    if not last:
                        ln.dve_low(dve, b + 1)

                    def masked_scores(u):
                        n = b * UNITS + u
                        dve.wait_ge(score_done, n + 1)
                        if u >= SLOTS:
                            dve.wait_ge(prob_ready, (n - SLOTS + 1) * BT)
                        dve.tensor_tensor(masked[:, u % SLOTS], score[u % GROUP][:],
                                          mask[:].rearrange("p (o k) -> p o k", o=1).broadcast_to([P, BT, P]),
                                          ALU.add).then_inc(masked_ready, 1)
                        dve.wait_ge(masked_ready, n + 1)
                        dve.tensor_reduce(least[:, u % SLOTS], masked[:, u % SLOTS], AX.X, ALU.min).then_inc(least_ready, 1)

                    def take_o(u):
                        n = b * UNITS + u
                        dve.wait_ge(o_done, n + 1)
                        dve.reciprocal(inv_sum[:, u % 2], psum_[:, u % SUMS]).then_inc(inv_ready, 1)
                        dve.wait_ge(inv_ready, n + 1)
                        dve.tensor_tensor(o[:, :, u * HD:(u + 1) * HD], o_ps[u % 2],
                                          inv_sum[:, u % 2].rearrange("p (t o) -> p t o", o=1).broadcast_to([P, BT, HD]),
                                          ALU.mult).then_inc(o_ready, 1)

                    for u in range(UNITS):
                        masked_scores(u)
                        if u >= SLOTS:
                            take_o(u - SLOTS)
                    for u in range(UNITS - SLOTS, UNITS):
                        take_o(u)
                    for t in range(BT):
                        dve.wait_ge(oT_high, b * BT + t + 1)
                        dve.tensor_tensor(oT[:, 1, t], oT_ps[:], oT[:, 0, t].bitcast(F32),
                                          ALU.subtract).then_inc(oT_ready, 1)
                    for t in range(BT):
                        j = 3 * DC + t
                        dve.wait_ge(mm_done, b * MM + j + 1)
                        dve.wait_ge(h_ready, b * BT + BT + t)
                        dve.tensor_tensor(biased[:], mm[j % 2][:], bp[:], ALU.add).then_inc(biased_ready, 1)
                        dve.wait_ge(biased_ready, b * BT + t + 1)
                        dve.sem_inc(mm_free[j % 2], 1)
                        dve.tensor_tensor(h[:, b * BT + t, :], h[:, b * BT + t, :], biased[:],
                                          ALU.add).then_inc(h_ready, 1)
                token_blocks(dve, of_block)
                dve.wait_ge(h_ready, NBLK * BT + BT)

            @block.tensor
            def _(pe):
                pe.sem_inc(mm_free[0], 1)
                pe.sem_inc(mm_free[1], 1)
                ln.pe_turn(pe, 0, first=True)
                for n in range(4):
                    pe.wait_ge(w.ready, n + 1)

                def of_block(b, last):
                    pe.wait_ge(ln.xT_ready, b * DC + DC)

                    def take_mm(j):
                        pe.wait_ge(mm_free[j % 2], b * (MM // 2) + j // 2 + 1)
                        return mm[j % 2][:]

                    for c in range(DC):
                        for i, piece in enumerate((WQ, WK)):
                            out = take_mm(2 * c + i)
                            for k in range(DC):
                                ins = product(pe, out, w.pair(piece, k, c * P, (c + 1) * P),
                                              [ln.xT[:, x, k, :] for x in range(2)], k == 0, k == DC - 1)
                            ins.then_inc(mm_done, 1)
                    for t in range(BT):
                        out = take_mm(2 * DC + t)
                        for k in range(DC):
                            ins = product(pe, out, [ln.xT[:, x, k, t * P:(t + 1) * P] for x in range(2)],
                                          w.pair(WV, k, 0, D), k == 0, k == DC - 1)
                        ins.then_inc(mm_done, 1)
                    if not last:
                        ln.pe_turn(pe, b + 1)

                    def scores(u):
                        n = b * UNITS + u
                        c, j = u // GROUP, u % GROUP
                        rows = slice(j * HD, (j + 1) * HD)
                        if j == 0:
                            pe.wait_ge(qk_ready, b * 2 * DC + 2 * c + 2)
                        if u >= GROUP:
                            pe.wait_ge(masked_ready, n - GROUP + 1)
                        for t in range(BT):
                            ins = pe.matmul(score[j][:, t, :], qT[rows, c, t * P:(t + 1) * P],
                                            kT[rows, c, t * P:(t + 1) * P], start=True, stop=True)
                        ins.then_inc(score_done, 1)

                    def turn_prob(u):
                        n = b * UNITS + u
                        pe.wait_ge(prob_ready, (n + 1) * BT)
                        if u:
                            pe.wait_ge(probT_ready, n)
                        for t in range(BT):
                            ins = pe.transpose(probT_ps[:, t, :], prob[:, u % SLOTS, t, :], ident[:])
                        ins.then_inc(prob_turned, 1)

                    def heads(u):
                        n = b * UNITS + u
                        if u == 0:
                            pe.wait_ge(v_ready, b * BT + BT)
                        pe.wait_ge(probT_ready, n + 1)
                        if u >= 2:
                            pe.wait_ge(o_ready, n - 1)
                        for t in range(BT):
                            ins = pe.matmul(o_ps[u % 2][:, t, :], probT[:, u % SLOTS, t, :], v[:, t, u * HD:(u + 1) * HD],
                                            start=True, stop=True)
                        ins.then_inc(o_done, 1)

                    for u in range(SLOTS - 1):
                        scores(u)
                    for u in range(UNITS):
                        if u + SLOTS - 1 < UNITS:
                            scores(u + SLOTS - 1)
                        turn_prob(u)
                        if u >= 2:
                            heads(u - 2)
                    heads(UNITS - 2)
                    heads(UNITS - 1)
                    pe.wait_ge(o_ready, (b + 1) * UNITS)
                    for t in range(BT):
                        if t:
                            pe.wait_ge(oT_ready, b * BT + t)
                        for c in range(DC):
                            ins = pe.transpose(oT_ps[:, c, :], o[:, t, c * P:(c + 1) * P], ident[:])
                        ins.then_inc(o_turned, 1)
                    for t in range(BT):
                        out = take_mm(3 * DC + t)
                        pe.wait_ge(oT_ready, b * BT + t + 1)
                        for c in range(DC):
                            ins = product(pe, out, [oT[:, x, t, c, :] for x in range(2)], w.pair(WP, c, 0, D),
                                          c == 0, c == DC - 1)
                        ins.then_inc(mm_done, 1)
                token_blocks(pe, of_block)


def memory_mlp_stage(nc, h, ident, a):
    INTER = 2048
    UM = INTER // P
    KEYS, TOP, EXP = 64, 8, 1024
    UE = EXP // P
    XK = EXP // KEYS
    U = UM + UE
    RD = 64
    WM, WE = DC * 2 * P + D, DC * P + D
    SLOTS = 4
    AHEAD = SLOTS - 1
    ROWS = KEYS + XK + 1
    TSTEPS, BSTEPS = 16, 6
    START = 2
    with Stage(nc, "mem") as s:
        turn = s.ps("turn", [P, BLK])
        gu = [s.ps(f"gu{i}", [P, BLK]) for i in range(3)]
        out_ps = [s.ps(f"out{i}", [P, D]) for i in range(BT)]
        ln = Norm(s, nc, h, ident, turn, 2 * NBLK)
        wq_raw = s.sb("wq_raw", [P, DC * P])
        wq = s.sb("wq", [P, 2, DC * P], F32R)
        keys = s.sb("keys", [RD, 2, KEYS])
        iota = s.sb("iota", [P, KEYS])
        ysteps = s.sb("ysteps", [P, TOP])
        select_raw = s.sb("select_raw", [ROWS, EXP + P])
        select = s.sb("select", [ROWS, EXP + P], F32R)
        query = s.sb("query", [RD, TOK, 2])
        tile_query = s.sb("tile_query", [RD, 2, P])
        raw = s.sb("raw", [P, 2, WM])
        w = s.sb("w", [P, SLOTS, 2, WM], F32R)
        act_out = s.sb("act_out", [P, 2, BLK])
        hid = s.sb("hid", [P, BLK])
        hidT = s.sb("hidT", [P, 2, 2, BLK], F32R)
        route = s.sb("route", [P, 2, KEYS])
        best = s.sb("best", [P, 2, TOP])
        best_at = s.sb("best_at", [P, 2, TOP], U32)
        best_pos = s.sb("best_pos", [P, BT, 2, TOP])
        pair = s.sb("pair", [P, BT, TOP, TOP])
        pair_now = s.sb("pair_now", [P, TOP, TOP])
        pair_best = s.sb("pair_best", [P, TOP])
        marked = s.sb("marked", [P, TOP, TOP])
        chosen = s.sb("chosen", [P, BT, TOP, TOP])
        count = s.sb("count", [P, TOP])
        hit = s.sb("hit", [P, TOP, KEYS])
        pair_exp = s.sb("pair_exp", [P, BT, TOP * TOP])
        row_sum = s.sb("row_sum", [P, BT, TOP])
        clamped = s.sb("clamped", [P, BT, TOP])
        inv_total = s.sb("inv_total", [P, BT])
        rows = s.sb("rows", [P, BT, 2, ROWS])
        rowsT = s.sb("rowsT", [ROWS, 2, BLK], F32R)
        rankT = s.sb("rankT", [ROWS, BLK], F32R)
        expo = s.sb("expo", [P, 2, BLK])
        mix = s.sb("mix", [P, UE, BLK])

        small_in = s.sem("small_in")
        q_high = s.sem("q_high")
        q_split = s.sem("q_split")
        q_done = s.sem("q_done")
        query_ready = s.sem("query_ready")
        raw_loaded = [s.sem(f"raw_loaded{i}") for i in range(2)]
        raw_free = s.sem("raw_free")
        w_high = s.sem("w_high")
        w_ready = s.sem("w_ready")
        unit_used = s.sem("unit_used")
        g_done = s.sem("g_done")
        u_done = s.sem("u_done")
        silu_ready = s.sem("silu_ready")
        hid_step = s.sem("hid_step")
        hid_high = s.sem("hid_high")
        hid_ready = s.sem("hid_ready")
        out_done = s.sem("out_done")
        out_free = s.sem("out_free")
        route_done = s.sem("route_done")
        route_step = s.sem("route_step")
        pair_in = s.sem("pair_in")
        pair_exp_ready = s.sem("pair_exp_ready")
        block_step = s.sem("block_step")
        rows_ready = s.sem("rows_ready")
        rows_turned = s.sem("rows_turned")
        rows_high = s.sem("rows_high")
        rows_low = s.sem("rows_low")
        rank_ready = s.sem("rank_ready")
        mix_done = s.sem("mix_done")
        expo_ready = s.sem("expo_ready")
        mix_ready = s.sem("mix_ready")
        extra_done = s.sem("extra_done")
        mix_whole = s.sem("mix_whole")
        passed = s.sem("passed")
        queries_ready = s.sem("queries_ready")

        expo_ps = [gu[1], gu[0]]
        rank_ps = [gu[2], turn]

        def mlp_groups(eng, body):
            body(0)
            with eng.Fori(1, UM // SLOTS - 1) as g:
                body(g)
            body(UM // SLOTS - 1)

        def units_ahead(b, g, m, last):
            i = g * SLOTS + m + AHEAD
            slot = (m + AHEAD) % SLOTS
            if isinstance(i, int) and i >= U:
                return None if last else ((b + 1) * U + i - U, slot, WM)
            return b * U + i, slot, WE if isinstance(i, int) and i >= UM else WM

        with s.block() as block:

            @block.sync
            def _(sp):
                for dst, src in ((wq_raw, "w_ret"), (keys, "keys"), (iota, "iota"), (ysteps, "ysteps"),
                                 (select_raw, "select")):
                    sp.dma_start(dst[:], a[src]).then_inc(small_in, 16)

                def of_block(b, last):
                    def of_group(g):
                        for m in range(SLOTS):
                            sp.wait_ge(raw_free, b * U + g * SLOTS + m + 1)
                            sp.dma_start(raw[:, m % 2, :], a["w_mlp"][g * SLOTS + m]).then_inc(raw_loaded[m % 2], 16)
                    mlp_groups(sp, of_group)
                    for e in range(UE):
                        sp.wait_ge(raw_free, b * U + UM + e + 1)
                        sp.dma_start(raw[:, e % 2, 0:WE], a["w_exp"][e]).then_inc(raw_loaded[e % 2], 16)
                token_blocks(sp, of_block)

            @block.gpsimd
            def _(pool):
                ln.pool_rstd(pool)

            @block.scalar
            def _(act):
                act.sem_inc(silu_ready, START)
                act.sem_inc(route_done, 1)
                act.wait_ge(small_in, 80)
                nc.scalar.activation(wq[:, 0], wq_raw[:], ACT.Copy).then_inc(q_high, 1)
                nc.scalar.activation(select[:], select_raw[:], ACT.Copy).then_inc(q_high, 1)
                ln.act_high(act, 0)

                def of_query(b):
                    for half in range(2):
                        act.wait_ge(q_done, b * 2 + half + 1)
                        nc.scalar.activation(query[:, bass.ds(b * BLK, BLK), half], gu[half][0:RD, :],
                                             ACT.Copy).then_inc(query_ready, 1)
                    ln.act_high(act, b + 1)
                with act.Fori(0, NBLK) as b:
                    of_query(b)
                for m in range(AHEAD):
                    act.wait_ge(raw_loaded[m % 2], 16 * (m // 2 + 1))
                    nc.scalar.activation(w[:, m, 0, :], raw[:, m % 2, :], ACT.Copy).then_inc(w_high, 1)

                def of_block(b, last):
                    def of_unit(g, m):
                        n = b * U + g * SLOTS + m
                        act.wait_ge(g_done, n + 1)
                        act.wait_ge(hid_step, START + n - 1)
                        nc.scalar.activation(act_out[:, m % 2, :], gu[0][:], ACT.Silu).then_inc(silu_ready, 1)
                        unit = units_ahead(b, g, m, last)
                        if unit is not None:
                            nn, slot, cols = unit
                            par = slot % 2
                            base = b * (U // 2) + g * (SLOTS // 2) + (m + AHEAD) // 2 + 1
                            act.wait_ge(raw_loaded[par], base * 16)
                            act.wait_ge(unit_used, nn + 1)
                            nc.scalar.activation(w[:, slot, 0, 0:cols], raw[:, par, 0:cols], ACT.Copy).then_inc(w_high, 1)

                    def of_group(g):
                        for m in range(SLOTS):
                            of_unit(g, m)

                    def of_mlp_group(g):
                        act.wait_ge(route_done, b * BT + g + 1)
                        flat = query[:].rearrange("p t s -> p (t s)").rearrange("p (i n) -> p i n", i=2)
                        nc.scalar.activation(tile_query[:], flat[:, :, bass.ds((b * BT + g) * P, P)],
                                             ACT.Copy).then_inc(queries_ready, 1)
                        of_group(g)
                    mlp_groups(act, of_mlp_group)
                    act.wait_ge(pair_in, b + 1)
                    nc.scalar.activation(pair_exp[:], pair[:].rearrange("p t x y -> p t (x y)"),
                                         ACT.Exp).then_inc(pair_exp_ready, 1)
                    act.wait_ge(rows_turned, b * 2 + 1)
                    nc.scalar.activation(rowsT[:, 0], turn[0:ROWS, :], ACT.Copy).then_inc(rows_high, 1)
                    act.wait_ge(rows_turned, b * 2 + 2)
                    nc.scalar.activation(rankT[:], gu[2][0:ROWS, :], ACT.Copy).then_inc(rank_ready, 1)
                    for e in range(UE):
                        act.wait_ge(mix_done, b * UE + e + 1)
                        if e >= 2:
                            act.wait_ge(mix_ready, b * UE + e - 1)
                        nc.scalar.activation(expo[:, e % 2, :], expo_ps[e % 2][:], ACT.Exp).then_inc(expo_ready, 1)
                    for g in range(UM // SLOTS, U // SLOTS):
                        of_group(g)
                    if not last:
                        ln.act_high(act, NBLK + 1 + b)
                token_blocks(act, of_block)

            @block.vector
            def _(dve):
                dve.sem_inc(hid_step, START)
                dve.sem_inc(raw_free, 2)
                dve.memset(rows[:], 0.0).then_inc(q_split, 1)
                ln.dve_scale(dve, 0, 0, first=True)
                dve.wait_ge(q_high, 1)
                dve.tensor_tensor(wq[:, 1], wq_raw[:], wq[:, 0].bitcast(F32), ALU.subtract).then_inc(q_split, 1)
                ln.dve_low(dve, 0)
                with dve.Fori(0, NBLK - 1) as b:
                    ln.dve_scale(dve, b + 1, b + 1)
                    ln.dve_low(dve, b + 1)
                ln.dve_scale(dve, NBLK, 0)
                ln.dve_low(dve, NBLK)

                def split_low(n, slot, cols):
                    dve.wait_ge(w_high, n + 1)
                    dve.tensor_tensor(w[:, slot, 1, 0:cols], raw[:, slot % 2, 0:cols], w[:, slot, 0, 0:cols].bitcast(F32),
                                      ALU.subtract).then_inc(w_ready, 1)
                    dve.wait_ge(w_ready, n + 1)
                    dve.sem_inc(raw_free, 1)

                for m in range(AHEAD):
                    split_low(m, m, WM)

                def last_steps(b):
                    step = [0]

                    def chain(ins):
                        step[0] += 1
                        ins.then_inc(block_step, 1)
                        dve.wait_ge(block_step, b * BSTEPS + step[0])

                    dve.wait_ge(pair_exp_ready, b + 1)
                    e4 = pair_exp[:].rearrange("p t (x y) -> p t x y", x=TOP)
                    chain(dve.tensor_tensor(pair_exp[:].rearrange("p t q -> p (t q)"), pair_exp[:].rearrange("p t q -> p (t q)"),
                                            chosen[:].rearrange("p t x y -> p (t x y)"), ALU.mult))
                    chain(dve.tensor_reduce(row_sum[:], e4, AX.X, ALU.add))
                    chain(dve.tensor_reduce(inv_total[:], row_sum[:], AX.X, ALU.add))
                    chain(dve.reciprocal(inv_total[:], inv_total[:]))
                    chain(dve.tensor_scalar(clamped[:], best_pos[:, :, 0, :], XK - 0.5, None, ALU.is_gt))
                    chain(dve.tensor_tensor(clamped[:], clamped[:], row_sum[:], ALU.mult))
                    dve.tensor_reduce(rows[:, :, 0, ROWS - 1], clamped[:], AX.X, ALU.add).then_inc(rows_ready, 1)

                def route_part(b, g, m):
                    base = (b * BT + g) * TSTEPS
                    step = [(0, 4, 10, 13)[m]]

                    def chain(ins, wait=True):
                        step[0] += 1
                        ins.then_inc(route_step, 1)
                        if wait:
                            dve.wait_ge(route_step, base + step[0])

                    def alone():
                        dve.sem_inc(passed, 1)

                    t = bass.ds(g, 1) if not isinstance(g, int) else slice(g, g + 1)

                    def tile(x, pattern):
                        return x.rearrange(pattern)
                    if m == 0:
                        dve.wait_ge(route_done, b * BT + g + 2)
                        chain(dve.tensor_copy(route[:].rearrange("p s k -> p (s k)"), gu[2][:, 0:2 * KEYS]))
                        alone()
                        for i in range(2):
                            chain(dve.max(best[:, i, :], route[:, i, :]), wait=i == 1)
                        alone()
                        chain(dve.max_index(best_at[:, 0, :], best[:, 0, :], route[:, 0, :]))
                    if m == 1:
                        alone()
                        chain(dve.max_index(best_at[:, 1, :], best[:, 1, :], route[:, 1, :]))
                        chain(dve.tensor_copy(tile(best_pos[:, t], "p o s k -> p (o s k)"), best_at[:].rearrange("p s k -> p (s k)")), wait=False)
                        chain(dve.tensor_tensor(pair_now[:],
                                                best[:, 0, :].rearrange("p (k o) -> p k o", o=1).broadcast_to([P, TOP, TOP]),
                                                best[:, 1, :].rearrange("p (o k) -> p o k", o=1).broadcast_to([P, TOP, TOP]), ALU.add))
                        flat = pair_now[:].rearrange("p x y -> p (x y)")
                        alone()
                        chain(dve.max(pair_best[:], flat))
                        alone()
                        chain(dve.match_replace(marked[:].rearrange("p x y -> p (x y)"), pair_best[:], flat, -3.0e38))
                        chain(dve.tensor_tensor(tile(chosen[:, t], "p o x y -> p (o x y)"), marked[:].rearrange("p x y -> p (x y)"),
                                                flat, ALU.not_equal))
                    if m == 2:
                        chain(dve.tensor_reduce(count[:], tile(chosen[:, t], "p o x y -> p (o x) y"), AX.X, ALU.add), wait=False)
                        chain(dve.tensor_tensor(hit[:, :, 0:XK], iota[:, 0:XK].rearrange("p (o k) -> p o k", o=1).broadcast_to([P, TOP, XK]),
                                                tile(best_pos[:, t, 0, :], "p o k -> p k o").broadcast_to([P, TOP, XK]), ALU.is_equal))
                        chain(dve.tensor_tensor(hit[:, :, 0:XK], hit[:, :, 0:XK],
                                                count[:].rearrange("p (k o) -> p k o", o=1).broadcast_to([P, TOP, XK]), ALU.mult))
                        dve.tensor_reduce(tile(rows[:, t, 1, KEYS:KEYS + XK], "p o k -> p (o k)"),
                                          hit[:, :, 0:XK].rearrange("p k x -> p x k"), AX.X, ALU.add)
                        for i, (c0, n) in enumerate(((KEYS, XK), (0, KEYS))):
                            dve.tensor_scalar(tile(rows[:, t, 0, c0:c0 + n], "p o k -> p (o k)"), route[:, i, 0:n],
                                              best[:, i, 0:1], None, ALU.subtract)
                    if m == 3:
                        chain(dve.tensor_tensor(hit[:], iota[:].rearrange("p (o k) -> p o k", o=1).broadcast_to([P, TOP, KEYS]),
                                                tile(best_pos[:, t, 1, :], "p o k -> p k o").broadcast_to([P, TOP, KEYS]), ALU.is_equal))
                        chain(dve.tensor_tensor(hit[:], hit[:], ysteps[:].rearrange("p (k o) -> p k o", o=1).broadcast_to([P, TOP, KEYS]),
                                                ALU.mult))
                        dve.tensor_reduce(tile(rows[:, t, 1, 0:KEYS], "p o k -> p (o k)"), hit[:].rearrange("p k y -> p y k"), AX.X,
                                          ALU.add)
                        chain(dve.tensor_scalar(tile(pair[:, t], "p o x y -> p (o x y)"), pair_now[:].rearrange("p x y -> p (x y)"),
                                                pair_best[:, 0:1], None, ALU.subtract))

                def of_block(b, last):
                    def of_unit(g, m, mlp):
                        n = b * U + g * SLOTS + m
                        dve.wait_ge(silu_ready, START + n + 1)
                        if mlp:
                            dve.wait_ge(u_done, b * UM + g * SLOTS + m + 1)
                        dve.wait_ge(hid_ready, START + n)
                        other = gu[1][:] if mlp else mix[:, g * SLOTS + m - UM, :]
                        dve.tensor_tensor(hid[:], act_out[:, m % 2, :], other, ALU.mult).then_inc(hid_step, 1)
                        dve.wait_ge(hid_step, START + n + 1)
                        dve.wait_ge(unit_used, SLOTS + n - 1)
                        dve.tensor_copy(hidT[:, m % 2, 0], hid[:]).then_inc(hid_high, 1)
                        dve.wait_ge(hid_high, n + 1)
                        dve.tensor_tensor(hidT[:, m % 2, 1], hid[:], hidT[:, m % 2, 0].bitcast(F32),
                                          ALU.subtract).then_inc(hid_ready, 1)
                        unit = units_ahead(b, g, m, last)
                        if unit is not None:
                            split_low(*unit)

                    def of_group(g):
                        for m in range(SLOTS):
                            of_unit(g, m, True)
                            route_part(b, g, m)
                            if m == SLOTS - 1 and isinstance(g, int) and g == 0 and not last:
                                ln.dve_scale(dve, NBLK + 1 + b, b + 1)
                    mlp_groups(dve, of_group)
                    dve.wait_ge(route_step, (b + 1) * BT * TSTEPS)
                    dve.sem_inc(pair_in, 1)
                    last_steps(b)
                    for t in range(BT):
                        if t < BT - 1:
                            dve.wait_ge(out_done, b * 2 * (BT - 1) + t + 1)
                        else:
                            dve.wait_ge(unit_used, SLOTS + b * U + UM)
                        dve.tensor_tensor(h[:, b * BT + t, :], h[:, b * BT + t, :], out_ps[t][:],
                                          ALU.add).then_inc(out_free, 1)
                    dve.wait_ge(rows_high, b + 1)
                    dve.tensor_tensor(rowsT[:, 1], turn[0:ROWS, :], rowsT[:, 0].bitcast(F32), ALU.subtract).then_inc(rows_low, 1)
                    for e in range(UE):
                        dve.wait_ge(expo_ready, b * UE + e + 1)
                        dve.scalar_tensor_tensor(out=mix[:, e, :], in0=rank_ps[e % 2][:], scalar=TOP + 0.5, in1=expo[:, e % 2, :],
                                                 op0=ALU.is_gt, op1=ALU.mult).then_inc(mix_ready, 1)
                    dve.wait_ge(extra_done, b + 1)
                    dve.wait_ge(mix_ready, (b + 1) * UE)
                    dve.tensor_tensor(mix[:, UE - 1, :], mix[:, UE - 1, :], gu[1][:], ALU.add).then_inc(mix_whole, 1)
                    dve.wait_ge(mix_whole, b + 1)
                    for g in range(UM // SLOTS, U // SLOTS):
                        for m in range(SLOTS):
                            of_unit(g, m, False)
                    if not last:
                        ln.dve_low(dve, NBLK + 1 + b)
                    for t in range(BT):
                        if t < BT - 1:
                            dve.wait_ge(out_done, (b * 2 + 1) * (BT - 1) + t + 1)
                        else:
                            dve.wait_ge(unit_used, SLOTS + (b + 1) * U)
                        dve.wait_ge(out_free, BT + b * 2 * BT + t + 1)
                        dve.scalar_tensor_tensor(out=h[:, b * BT + t, :], in0=out_ps[t][:], scalar=inv_total[:, t:t + 1],
                                                 in1=h[:, b * BT + t, :], op0=ALU.mult, op1=ALU.add).then_inc(out_free, 1)
                token_blocks(dve, of_block)

            @block.tensor
            def _(pe):
                pe.sem_inc(unit_used, SLOTS)
                pe.sem_inc(hid_ready, START)
                pe.sem_inc(out_free, BT)
                ln.pe_turn(pe, 0, first=True)
                pe.wait_ge(q_split, 2)
                pe.wait_ge(q_high, 2)
                with pe.Fori(0, NBLK) as b:
                    pe.wait_ge(ln.xT_ready, (b + 1) * DC)
                    for half in range(2):
                        for k in range(DC):
                            ins = product(pe, gu[half][0:RD, :], [wq[:, i, k * P + half * RD:k * P + half * RD + RD] for i in range(2)],
                                          [ln.xT[:, i, k, :] for i in range(2)], k == 0, k == DC - 1)
                        ins.then_inc(q_done, 1)
                    ln.pe_turn(pe, b + 1)
                    pe.wait_ge(query_ready, (b + 1) * 2)

                def of_block(b, last):
                    pe.wait_ge(ln.xT_ready, (NBLK + 1 + b) * DC)

                    def first_product(g, m, mlp):
                        n = b * U + g * SLOTS + m
                        pe.wait_ge(w_ready, n + 1)
                        pe.wait_ge(silu_ready, START + n)
                        for k in range(DC):
                            ins = product(pe, gu[0][:], [w[:, m, i, k * P:(k + 1) * P] for i in range(2)],
                                          [ln.xT[:, i, k, :] for i in range(2)], k == 0, k == DC - 1)
                        ins.then_inc(g_done, 1)
                        if mlp:
                            pe.wait_ge(hid_step, START + n)
                            for k in range(DC):
                                ins = product(pe, gu[1][:], [w[:, m, i, (DC + k) * P:(DC + k + 1) * P] for i in range(2)],
                                              [ln.xT[:, i, k, :] for i in range(2)], k == 0, k == DC - 1)
                            ins.then_inc(u_done, 1)

                    def second_product(g, m, mlp, start, stop):
                        n = b * U + g * SLOTS + m
                        pe.wait_ge(hid_ready, START + n + 1)
                        c0 = 2 * DC * P if mlp else DC * P
                        for t in range(BT):
                            if start:
                                pe.wait_ge(out_free, (b * 2 + (0 if mlp else 1)) * BT + t + 1)
                            ins = product(pe, out_ps[t][:], [hidT[:, m % 2, i, t * P:(t + 1) * P] for i in range(2)],
                                          [w[:, m, i, c0:c0 + D] for i in range(2)], start, stop)
                            if t == BT - 1:
                                ins.then_inc(unit_used, 1)
                            elif stop:
                                ins.then_inc(out_done, 1)

                    def of_group(g):
                        if not isinstance(g, int) or g:
                            pe.wait_ge(route_step, (b * BT + g) * TSTEPS - TSTEPS + 1)
                        pe.wait_ge(queries_ready, b * BT + g + 1)
                        for i in range(2):
                            ins = pe.matmul(gu[2][:, i * KEYS:(i + 1) * KEYS], tile_query[:, i, :], keys[:, i, :],
                                            start=True, stop=True)
                        ins.then_inc(route_done, 1)
                        for m in range(SLOTS):
                            first_product(g, m, True)
                            if m:
                                second_product(g, m - 1, True, isinstance(g, int) and g == 0 and m == 1, False)
                            elif not (isinstance(g, int) and g == 0):
                                second_product(g - 1, SLOTS - 1, True, False, False)
                    mlp_groups(pe, of_group)
                    second_product(UM // SLOTS - 1, SLOTS - 1, True, False, True)

                    pe.wait_ge(rows_ready, b + 1)
                    for i, out in enumerate((turn, gu[2])):
                        for t in range(BT):
                            ins = pe.transpose(out[0:ROWS, t * P:(t + 1) * P], rows[:, t, i, :], ident[:])
                        ins.then_inc(rows_turned, 1)
                    pe.wait_ge(rows_low, b + 1)
                    pe.wait_ge(rank_ready, b + 1)
                    pe.wait_ge(silu_ready, START + b * U + UM)
                    for e in range(UE):
                        if e >= 2:
                            pe.wait_ge(expo_ready, b * UE + e - 1)
                            pe.wait_ge(mix_ready, b * UE + e - 1)
                        lhs = select[:, e * P:(e + 1) * P]
                        for i in range(2):
                            pe.matmul(expo_ps[e % 2][:], lhs, rowsT[:, i], start=i == 0, stop=i == 1)
                        pe.matmul(rank_ps[e % 2][:], lhs, rankT[:], start=True, stop=True).then_inc(mix_done, 1)
                    pe.wait_ge(expo_ready, b * UE + UE)
                    pe.wait_ge(mix_ready, b * UE + UE)
                    for i in range(2):
                        ins = pe.matmul(gu[1][:], select[:, EXP:EXP + P], rowsT[:, i], start=i == 0, stop=i == 1)
                    ins.then_inc(extra_done, 1)

                    for g in range(UM // SLOTS, U // SLOTS):
                        for m in range(SLOTS):
                            first_product(g, m, False)
                            if (g, m) != (UM // SLOTS, 0):
                                pg, pm = (g, m - 1) if m else (g - 1, SLOTS - 1)
                                second_product(pg, pm, False, (pg, pm) == (UM // SLOTS, 0), False)
                    if not last:
                        ln.pe_turn(pe, NBLK + 1 + b)
                    second_product(U // SLOTS - 1, SLOTS - 1, False, False, True)
                    pe.wait_ge(mix_whole, b + 1)
                token_blocks(pe, of_block)


def rotary_attention_stage(nc, h, ident, a):
    HD, KV = 64, 8
    CAP, SCALE = 50.0, 256.0 ** -0.5
    UNITS = 16
    PAIR = 2
    DENSE = 3
    MM = BT + DC * DENSE + BT
    PARTS = 2 * BT
    WQ, WK, WV, WO = 0, 2, 3, 4
    START = 2
    with Stage(nc, "at1") as s:
        mm = [s.ps(f"mm{i}", [P, BLK]) for i in range(2)]
        score = [s.ps(f"score{i}", [P, PAIR, 2, P]) for i in range(4)]
        spare = [s.ps(f"spare{i}", [P, BLK]) for i in range(2)]
        o_ps = [x[:, 0:PAIR * 2 * (HD + 1)].rearrange("p (t i d) -> p t i d", t=PAIR, i=2) for x in spare]
        ln = Norm(s, nc, h, ident, mm[0])
        w = Resident(s, nc, 6)
        cos = s.sb("cos", [P, CLIP])
        sin = s.sb("sin", [P, CLIP])
        mask = s.sb("mask", [P, P])
        qT = s.sb("qT", [P, 2, 2, BLK])
        kT = s.sb("kT", [P, 2, BLK])
        swapped = s.sb("swapped", [P, 2, BLK])
        v = s.sb("v", [P, BT, KV, HD + 1])
        probT = s.sb("probT", [P, 2, PAIR, 2, P])
        inv_sum = s.sb("inv_sum", [P, 2, PAIR, 2])
        o = w.raw[:].rearrange("p a (b n) -> p (a b) n", b=2)
        oT = s.sb("oT", [P, 2, 2, DC, P], F32R)

        small_in = s.sem("small_in")
        ones_ready = s.sem("ones_ready")
        mm_done = s.sem("mm_done")
        mm_taken = [s.sem(f"mm_taken{i}") for i in range(2)]
        swap_loaded = [s.sem(f"swap_loaded{i}") for i in range(2)]
        rope_step = s.sem("rope_step")
        rope_ready = s.sem("rope_ready")
        score_done = s.sem("score_done")
        tanh_ready = s.sem("tanh_ready")
        exp_ready = s.sem("exp_ready")
        probT_ready = s.sem("probT_ready")
        o_done = s.sem("o_done")
        inv_ready = s.sem("inv_ready")
        o_ready = s.sem("o_ready")
        o_turned = s.sem("o_turned")
        oT_high = s.sem("oT_high")
        oT_ready = s.sem("oT_ready")
        part_half = s.sem("part_half")
        passed = s.sem("passed")

        def task(c, i):
            return BT + c * DENSE + i

        def where(c, i):
            return kT[:, c % 2, :] if i == 0 else qT[:, c % 2, i - 1, :]

        with s.block() as block:

            @block.sync
            def _(sp):
                for dst, src in ((cos, "cos"), (sin, "sin"), (mask, "maskT")):
                    sp.dma_start(dst[:], a[src]).then_inc(small_in, 16)
                w.load(sp, a["w_at1"])

                def of_block(b, last):
                    for c in range(DC):
                        for i in range(DENSE):
                            j, d = task(c, i), c * DENSE + i
                            sp.wait_ge(mm_taken[j % 2], b * (MM // 2) + j // 2 + 2)
                            sp.sem_inc(passed, 1)
                            sp.wait_ge(rope_ready, START + b * DC * DENSE + d - 1)
                            for r in range(4):
                                src = slice((r ^ 1) * 32, (r ^ 1) * 32 + 32)
                                sp.dma_start(swapped[r * 32:r * 32 + 32, d % 2, :],
                                             where(c, i)[src]).then_inc(swap_loaded[d % 2], 16)
                token_blocks(sp, of_block)

            @block.gpsimd
            def _(pool):
                ln.pool_rstd(pool)

            @block.scalar
            def _(act):
                w.split_high(act)
                ln.act_high(act, 0)

                def of_block(b, last):
                    act.wait_ge(ones_ready, 1)
                    for t in range(BT):
                        act.wait_ge(mm_done, b * MM + t + 1)
                        nc.scalar.activation(v[:, t, :, 0:HD], mm[t % 2][:].rearrange("p (j d) -> p j d", j=KV),
                                             ACT.Copy).then_inc(mm_taken[t % 2], 1)

                    def take(c, i):
                        j = task(c, i)
                        act.wait_ge(mm_done, b * MM + j + 1)
                        if c >= 2:
                            act.wait_ge(score_done, b * UNITS + (c - 1) * 4)
                        nc.scalar.activation(where(c, i), mm[j % 2][:], ACT.Copy).then_inc(mm_taken[j % 2], 1)

                    for i in range(DENSE):
                        take(0, i)
                    for u in range(UNITS):
                        n = b * UNITS + u
                        act.wait_ge(score_done, n + 1)
                        if u >= 2:
                            act.wait_ge(o_done, n - 1)
                        bank = score[2 * (u % 4 // 2) + u % 2]
                        nc.scalar.activation(probT[:, u % 2], bank[:], ACT.Tanh, scale=SCALE / CAP).then_inc(tanh_ready, 1)
                        act.wait_ge(tanh_ready, n + 1)
                        nc.scalar.activation(probT[:, u % 2], probT[:, u % 2], ACT.Exp, scale=CAP).then_inc(exp_ready, 1)
                        if u < UNITS - 4 and u % 4 < DENSE:
                            take(u // 4 + 1, u % 4)
                        if u >= UNITS - 4 and not last:
                            ln.act_high_chunk(act, b + 1, u - UNITS + 4)
                    for i in range(PARTS):
                        act.wait_ge(o_turned, b * PARTS + i + 1)
                        if i >= 2:
                            if i % 2 == 0:
                                act.wait_ge(part_half, b * BT + i // 2)
                            else:
                                act.wait_ge(mm_done, b * MM + MM - BT + i // 2)
                        nc.scalar.activation(oT[:, i % 2, 0], spare[i % 2][:].rearrange("p (c q) -> p c q", c=DC),
                                             ACT.Copy).then_inc(oT_high, 1)
                token_blocks(act, of_block)

            @block.vector
            def _(dve):
                dve.sem_inc(rope_ready, START)
                dve.memset(v[:, :, :, HD:], 1.0).then_inc(ones_ready, 1)
                ln.dve_scale(dve, 0, 0, first=True)
                w.split_low(dve)
                ln.dve_low(dve, 0)
                dve.wait_ge(small_in, 48)

                def of_block(b, last):
                    def rope(c, i):
                        d = c * DENSE + i
                        n = b * DC * DENSE + d
                        dve.wait_ge(swap_loaded[d % 2], (b * (DC * DENSE // 2) + d // 2 + 1) * 64)
                        clips = BLK // CLIP
                        x = where(c, i).rearrange("p (n t) -> p n t", n=clips)
                        y = swapped[:, d % 2, :].rearrange("p (n t) -> p n t", n=clips)
                        table = [z[:].rearrange("p (o t) -> p o t", o=1).broadcast_to([P, clips, CLIP]) for z in (cos, sin)]
                        dve.tensor_tensor(x, x, table[0], ALU.mult).then_inc(rope_step, 1)
                        dve.tensor_tensor(y, y, table[1], ALU.mult).then_inc(rope_step, 1)
                        dve.wait_ge(rope_step, n * 2 + 2)
                        dve.tensor_tensor(x, x, y, ALU.add).then_inc(rope_ready, 1)

                    for i in range(DENSE):
                        rope(0, i)

                    def take_o(u):
                        n = b * UNITS + u
                        t0 = u % 2 * PAIR
                        c0 = u // 2 * P
                        dve.wait_ge(o_done, n + 1)
                        dve.reciprocal(inv_sum[:, u % 2], o_ps[u % 2][:, :, :, HD]).then_inc(inv_ready, 1)
                        dve.wait_ge(inv_ready, n + 1)
                        dve.tensor_tensor(o[:, t0:t0 + PAIR, c0:c0 + P].rearrange("p t (i d) -> p t i d", i=2),
                                          o_ps[u % 2][:, :, :, 0:HD],
                                          inv_sum[:, u % 2].rearrange("p t (i o) -> p t i o", o=1).broadcast_to([P, PAIR, 2, HD]),
                                          ALU.mult).then_inc(o_ready, 1)

                    for u in range(UNITS):
                        n = b * UNITS + u
                        dve.wait_ge(exp_ready, n + 1)
                        dve.tensor_tensor(probT[:, u % 2].rearrange("p t i q -> p (t i) q"),
                                          probT[:, u % 2].rearrange("p t i q -> p (t i) q"),
                                          mask[:].rearrange("p (o q) -> p o q", o=1).broadcast_to([P, PAIR * 2, P]),
                                          ALU.mult).then_inc(probT_ready, 1)
                        if u:
                            take_o(u - 1)
                        if u < UNITS - 4 and u % 4 < DENSE:
                            rope(u // 4 + 1, u % 4)
                        if u == 3 and not last:
                            ln.dve_scale(dve, b + 1, b + 1)
                        if u >= UNITS - 4 and not last:
                            ln.dve_low_chunk(dve, b + 1, u - UNITS + 4)
                    take_o(UNITS - 1)

                    def low(i):
                        dve.wait_ge(oT_high, b * PARTS + i + 1)
                        dve.tensor_tensor(oT[:, i % 2, 1], spare[i % 2][:].rearrange("p (c q) -> p c q", c=DC),
                                          oT[:, i % 2, 0].bitcast(F32), ALU.subtract).then_inc(oT_ready, 1)

                    def add(t):
                        j = MM - BT + t
                        dve.wait_ge(mm_done, b * MM + j + 1)
                        dve.tensor_tensor(h[:, b * BT + t, :], h[:, b * BT + t, :], mm[j % 2][:],
                                          ALU.add).then_inc(mm_taken[j % 2], 1)
                    for i in range(PARTS):
                        low(i)
                        if i >= 3 and i % 2:
                            add(i // 2 - 1)
                    add(BT - 1)
                token_blocks(dve, of_block)

            @block.tensor
            def _(pe):
                pe.sem_inc(mm_taken[0], 1)
                pe.sem_inc(mm_taken[1], 1)
                ln.pe_turn(pe, 0, first=True)
                for n in range(6):
                    pe.wait_ge(w.ready, n + 1)

                def of_block(b, last):
                    pe.wait_ge(ln.xT_ready, b * DC + DC)

                    def take_mm(j):
                        pe.wait_ge(mm_taken[j % 2], b * (MM // 2) + j // 2 + 1)
                        return mm[j % 2][:]

                    def dense(c, i):
                        out = take_mm(task(c, i))
                        piece, col = (WK, c * P) if i == 0 else (WQ + (2 * c + i - 1) // DC, (2 * c + i - 1) % DC * P)
                        for k in range(DC):
                            ins = product(pe, out, w.pair(piece, k, col, col + P),
                                          [ln.xT[:, x, k, :] for x in range(2)], k == 0, k == DC - 1)
                        ins.then_inc(mm_done, 1)

                    for t in range(BT):
                        out = take_mm(t)
                        for k in range(DC):
                            ins = product(pe, out, [ln.xT[:, x, k, t * P:(t + 1) * P] for x in range(2)],
                                          w.pair(WV, k, 0, D), k == 0, k == DC - 1)
                        ins.then_inc(mm_done, 1)
                    for i in range(DENSE):
                        dense(0, i)

                    def scores(u):
                        n = b * UNITS + u
                        c, r, t0 = u // 4, u % 4 // 2, u % 2 * PAIR
                        if u % 4 == 0:
                            pe.wait_ge(rope_ready, START + b * DC * DENSE + (c + 1) * DENSE)
                        if u >= 4:
                            pe.wait_ge(tanh_ready, n - 3)
                        rows = slice(r * HD, (r + 1) * HD)
                        for t in range(PAIR):
                            cols = slice((t0 + t) * P, (t0 + t + 1) * P)
                            ins = pe.matmul(score[2 * r + u % 2][:, t, :, :], kT[rows, c % 2, cols], qT[rows, c % 2, :, cols],
                                            start=True, stop=True)
                        ins.then_inc(score_done, 1)

                    def heads(u):
                        n = b * UNITS + u
                        t0 = u % 2 * PAIR
                        if u == 0:
                            for i in range(2):
                                pe.wait_ge(mm_taken[i], b * (MM // 2) + BT // 2 + 1)
                        pe.wait_ge(probT_ready, n + 1)
                        if u >= 2:
                            pe.wait_ge(o_ready, n - 1)
                        for t in range(PAIR):
                            for i in range(2):
                                ins = pe.matmul(o_ps[u % 2][:, t, i, :], probT[:, u % 2, t, i, :], v[:, t0 + t, u // 2, :],
                                                start=True, stop=True)
                        ins.then_inc(o_done, 1)

                    scores(0)
                    scores(1)
                    for u in range(UNITS):
                        if u < UNITS - 4 and u % 4 < DENSE:
                            dense(u // 4 + 1, u % 4)
                        if u >= UNITS - 4 and not last:
                            if u == UNITS - 4:
                                pe.wait_ge(mm_taken[0], b * (MM // 2) + (MM - BT) // 2 + 1)
                            ln.pe_turn_chunk(pe, b + 1, u - UNITS + 4)
                        if u + 2 < UNITS:
                            scores(u + 2)
                        heads(u)

                    def turn_part(i):
                        t, half = i // 2, i % 2
                        if i == 0:
                            pe.wait_ge(o_ready, (b + 1) * UNITS)
                        if i >= 2:
                            pe.wait_ge(oT_ready, b * PARTS + i - 1)
                        for c in range(DC):
                            col = (half * DC + c) * P
                            ins = pe.transpose(spare[i % 2][:, c * P:(c + 1) * P], o[:, t, col:col + P], ident[:])
                        ins.then_inc(o_turned, 1)

                    def project(i):
                        t, half = i // 2, i % 2
                        j = MM - BT + t
                        if half == 0:
                            take_mm(j)
                        pe.wait_ge(oT_ready, b * PARTS + i + 1)
                        for c in range(DC):
                            ins = product(pe, mm[j % 2][:], [oT[:, i % 2, x, c, :] for x in range(2)],
                                          w.pair(WO + half, c, 0, D), i % 2 == 0 and c == 0, i % 2 == 1 and c == DC - 1)
                        ins.then_inc(mm_done if half else part_half, 1)

                    turn_part(0)
                    turn_part(1)
                    if not last:
                        pe.wait_ge(ln.xT_ready, (b + 2) * DC)
                    for i in range(PARTS):
                        project(i)
                        if i + 2 < PARTS:
                            turn_part(i + 2)
                token_blocks(pe, of_block)


def ternary_mlp_stage(nc, h, ident, a, out):
    INNER = 1408
    FC = INNER // P
    COLS = FC * D
    W1, W2, W3 = range(3)
    with Stage(nc, "ter") as s:
        turn = s.ps("turn", [P, BLK])
        x1_ps = [s.ps(f"x1_{i}", [P, BLK]) for i in range(2)]
        x2_ps = [s.ps(f"x2_{i}", [P, BLK]) for i in range(2)]
        out_ps = [s.ps(f"out{i}", [P, D]) for i in range(2)]
        ln = Norm(s, nc, h, ident, turn)
        raw = s.sb("raw", [P, COLS])
        w = s.sb("w", [P, 3, COLS], F32R)
        size = s.sb("size", [P, D])
        size_sum = s.sb("size_sum", [P, 3, FC])
        size_total = s.sb("size_total", [P, 3])
        ones = s.sb("ones", [P, P])
        bound = s.sb("bound", [P, 3, 2])
        sig = s.sb("sig", [P, 2, BLK])
        hid = s.sb("hid", [P, 2, BLK])
        hidT = s.sb("hidT", [P, FC, 2, BLK], F32R)

        raw_loaded = s.sem("raw_loaded")
        ones_ready = s.sem("ones_ready")
        size_ready = s.sem("size_ready")
        total_ready = s.sem("total_ready")
        mean_done = s.sem("mean_done")
        bound_ready = s.sem("bound_ready")
        above_ready = s.sem("above_ready")
        w_ready = s.sem("w_ready")
        x1_done = s.sem("x1_done")
        x2_done = s.sem("x2_done")
        sig_ready = s.sem("sig_ready")
        hid_step = s.sem("hid_step")
        hid_high = s.sem("hid_high")
        hid_ready = s.sem("hid_ready")
        out_done = s.sem("out_done")
        h_ready = s.sem("h_ready")
        stored = s.sem("stored")
        START = 2

        with s.block() as block:

            @block.sync
            def _(sp):
                for n in range(3):
                    if n:
                        sp.wait_ge(w_ready, n)
                    sp.dma_start(raw[:], a["w_ter"][n]).then_inc(raw_loaded, 16)
                with sp.Fori(0, TILES) as t:
                    sp.wait_ge(h_ready, START + t + 1)
                    sp.dma_start(out[t], h[:, t, :]).then_inc(stored, 16)
                sp.wait_ge(stored, TILES * 16)

            @block.gpsimd
            def _(pool):
                pool.memset(ones[:], 1.0).then_inc(ones_ready, 1)
                ln.pool_rstd(pool)

            @block.scalar
            def _(act):
                act.sem_inc(sig_ready, START)
                for n in range(3):
                    act.wait_ge(raw_loaded, 16 * n + 16)
                    for f in range(FC):
                        if n or f:
                            act.wait_ge(size_ready, n * FC + f)
                        nc.scalar.activation(size[:], raw[:, f * D:(f + 1) * D], ACT.Abs,
                                             accum_out=size_sum[:, n, f:f + 1]).then_inc(size_ready, 1)
                    if n == 0:
                        ln.act_high(act, 0)

                def of_block(b, last):
                    for f in range(FC):
                        n = b * FC + f
                        act.wait_ge(x1_done, n + 1)
                        act.wait_ge(hid_step, START + n - (1 if f else 0))
                        nc.scalar.activation(sig[:, f % 2, :], x1_ps[f % 2][:], ACT.Sigmoid,
                                             scale=-1.0).then_inc(sig_ready, 1)
                    if not last:
                        ln.act_high(act, b + 1)
                token_blocks(act, of_block)

            @block.vector
            def _(dve):
                dve.sem_inc(hid_step, START)
                dve.sem_inc(h_ready, START)
                ln.dve_scale(dve, 0, 0, first=True)
                for n in range(3):
                    dve.wait_ge(size_ready, (n + 1) * FC)
                    dve.tensor_reduce(size_total[:, n:n + 1], size_sum[:, n, :], AX.X, ALU.add).then_inc(total_ready, 1)
                    if n == 0:
                        ln.dve_low(dve, 0)
                    dve.wait_ge(mean_done, n + 1)
                    for i, sign in enumerate((0.5, -0.5)):
                        dve.tensor_scalar(bound[:, n, i:i + 1], out_ps[0][:, 0:1], sign / (INNER * D), sign * 1e-8,
                                          ALU.mult, ALU.add).then_inc(bound_ready, 1)
                    dve.wait_ge(bound_ready, 2 * n + 2)
                    dve.tensor_scalar(w[:, n, :], raw[:], bound[:, n, 0:1], None, ALU.is_gt).then_inc(above_ready, 1)
                    dve.wait_ge(above_ready, n + 1)
                    dve.scalar_tensor_tensor(out=w[:, n, :], in0=raw[:], scalar=bound[:, n, 1:2], in1=w[:, n, :].bitcast(F32),
                                             op0=ALU.is_lt, op1=ALU.subtract).then_inc(w_ready, 1)

                def of_block(b, last):
                    for f in range(FC):
                        n = b * FC + f
                        dve.wait_ge(x2_done, n + 1)
                        dve.wait_ge(sig_ready, START + n + 1)
                        dve.tensor_tensor(hid[:, f % 2, :], sig[:, f % 2, :], x2_ps[f % 2][:],
                                          ALU.mult).then_inc(hid_step, 1)
                        dve.wait_ge(hid_step, START + n + 1)
                        dve.tensor_copy(hidT[:, f, 0, :], hid[:, f % 2, :]).then_inc(hid_high, 1)
                        dve.wait_ge(hid_high, n + 1)
                        dve.tensor_tensor(hidT[:, f, 1, :], hid[:, f % 2, :], hidT[:, f, 0, :].bitcast(F32),
                                          ALU.subtract).then_inc(hid_ready, 1)
                        if f == 1 and not last:
                            ln.dve_scale(dve, b + 1, b + 1)
                    if not last:
                        ln.dve_low(dve, b + 1)
                    for t in range(BT):
                        dve.wait_ge(out_done, b * BT + t + 1)
                        dve.tensor_tensor(h[:, b * BT + t, :], h[:, b * BT + t, :], out_ps[t % 2][:],
                                          ALU.add).then_inc(h_ready, 1)
                token_blocks(dve, of_block)

            @block.tensor
            def _(pe):
                pe.sem_inc(hid_ready, START)
                pe.wait_ge(ones_ready, 1)
                ln.pe_turn(pe, 0, first=True)
                for n in range(3):
                    pe.wait_ge(total_ready, n + 1)
                    if n:
                        pe.wait_ge(bound_ready, 2 * n)
                    pe.matmul(out_ps[0][:, 0:1], ones[:], size_total[:, n:n + 1], start=True, stop=True).then_inc(mean_done, 1)

                def of_block(b, last):
                    pe.wait_ge(ln.xT_ready, b * DC + DC)
                    for f in range(FC):
                        n = b * FC + f
                        for m, bank, done in ((W1, x1_ps, x1_done), (W2, x2_ps, x2_done)):
                            pe.wait_ge(w_ready, m + 1)
                            pe.wait_ge(sig_ready if m == W1 else hid_step, START + n - (1 if f else 0))
                            for k in range(DC):
                                lhs = w[:, m, (f * DC + k) * P:(f * DC + k + 1) * P]
                                for x in range(2):
                                    ins = pe.matmul(bank[f % 2][:], lhs, ln.xT[:, x, k, :], start=k == 0 and x == 0,
                                                    stop=k == DC - 1 and x == 1)
                            ins.then_inc(done, 1)
                    if not last:
                        ln.pe_turn(pe, b + 1)
                    pe.wait_ge(w_ready, 3)
                    pe.wait_ge(hid_ready, START + (b + 1) * FC)
                    for t in range(BT):
                        pe.wait_ge(h_ready, START + b * BT + t - 1)
                        for f in range(FC):
                            for x in range(2):
                                ins = pe.matmul(out_ps[t % 2][:], hidT[:, f, x, t * P:(t + 1) * P], w[:, W3, f * D:(f + 1) * D],
                                                start=f == 0 and x == 0, stop=f == FC - 1 and x == 1)
                        ins.then_inc(out_done, 1)
                token_blocks(pe, of_block)


def program(nc, a, out):
    with ExitStack() as ctx:
        h = ctx.enter_context(nc.sbuf_tensor("h", [P, TILES, D], F32))
        ident = ctx.enter_context(nc.sbuf_tensor("ident", [P, P], F32))
        ident_loaded = ctx.enter_context(nc.semaphore("ident_loaded"))
        with nc.Block() as block:

            @block.sync
            def _(sp):
                sp.dma_start(ident[:], a["ident"]).then_inc(ident_loaded, 16)
                sp.wait_ge(ident_loaded, 16)
        token_stage(nc, h, ident, a)
        attention_stage(nc, h, ident, a)
        memory_mlp_stage(nc, h, ident, a)
        rotary_attention_stage(nc, h, ident, a)
        ternary_mlp_stage(nc, h, ident, a, out)



def lay_token(lay, f):
    lay["x"] = f["x"].reshape(NBLK, BT, P, PACK).transpose(0, 2, 1, 3)
    lay["norm_w"] = f["L0_tok_norm_w"].reshape(PC, P).T
    lay["router"] = f["L0_tok_router_w"].reshape(EXPERTS, PC, P).transpose(2, 1, 0).reshape(P, PC * EXPERTS)
    w1 = np.concatenate([f["L0_tok_w1"], f["L0_tok_sw1"][None]])
    w2 = np.concatenate([f["L0_tok_w2"], f["L0_tok_sw2"][None]])
    w1 = w1.reshape(MLPS, HC, P, PC, P).transpose(0, 1, 4, 3, 2).reshape(MLPS * HC, P, PC * P)
    w2 = w2.reshape(MLPS, D, HC, P).transpose(0, 2, 3, 1).reshape(MLPS * HC, P, D)
    lay["w_units"] = np.concatenate([w1, w2], axis=2)
    lay["b1"] = np.concatenate([f["L0_tok_b1"], f["L0_tok_sb1"][None]]).reshape(MLPS, HC, P).transpose(2, 0, 1)
    lay["b2"] = np.concatenate([f["L0_tok_b2"], f["L0_tok_sb2"][None]])


def lay_attention(lay, f):
    def rows(w):
        return w.reshape(DC, P, -1).transpose(1, 0, 2).reshape(P, -1)
    lay["w_at0"] = np.stack([rows(f[f"L0_attn_{k}"]) for k in ("Wq", "Wk", "Wv", "Wp")])
    for k in ("bq", "bk"):
        lay[k] = f[f"L0_attn_{k}"].reshape(DC, P).T
    for k in ("bv", "bp"):
        lay[k] = f[f"L0_attn_{k}"]
    q, k = np.arange(P)[:, None], np.arange(P)[None, :]
    lay["mask"] = np.where((q // CLIP == k // CLIP) & (k <= q), 0.0, BIG).astype(np.float32)


def lay_memory_mlp(lay, f):
    DM, KEYS, XK = 512, 64, 16
    lay["w_ret"] = f["L0_ffn_W_q"].reshape(DC, P, P).transpose(1, 0, 2).reshape(P, -1)
    lay["keys"] = f["L0_ffn_keys"].transpose(1, 0, 2)

    def chunks(w):
        return w.reshape(DC, P, -1, P).transpose(2, 1, 0, 3).reshape(-1, P, DC * P)
    lay["w_mlp"] = np.concatenate([chunks(f["L0_ffn_gate_w"]), chunks(f["L0_ffn_up_w"]),
                                   f["L0_ffn_down_w"].reshape(-1, P, D)], axis=2)
    lay["w_exp"] = np.concatenate([chunks(f["L0_ffn_down_embed"].T), f["L0_ffn_up_embed"].reshape(-1, P, D)], axis=2)
    lay["iota"] = np.tile(np.arange(KEYS, dtype=np.float32), (P, 1))
    lay["ysteps"] = np.tile(np.arange(8, 0, -1, dtype=np.float32), (P, 1))
    e = np.arange(1024)
    select = np.zeros((KEYS + XK + 1, 1024 + P), np.float32)
    select[e % KEYS, e] = 1.0
    select[KEYS + e // KEYS, e] = 1.0
    select[KEYS + XK, 1024 + P - 1] = 1.0
    lay["select"] = select


def lay_rotary_attention(lay, f):
    HD, KV = 64, 8

    def rows(w):
        return w.reshape(-1, P, D).transpose(1, 0, 2).reshape(P, -1)
    order = [4 * c + i + 2 * r for c in range(4) for i in range(2) for r in range(2)]
    wq = f["L1_attn_Wq"].reshape(D, 16, HD)[:, order].reshape(D, 16 * HD)
    wo = f["L1_attn_Wo"]
    lay["w_at1"] = np.stack([rows(wq[:, :D]), rows(wq[:, D:]), rows(f["L1_attn_Wk"]), rows(f["L1_attn_Wv"]),
                             rows(wo[:D]), rows(wo[D:])])
    freq = np.float32(1.0) / np.power(np.float32(10000.0), np.arange(0, HD, 2).astype(np.float32) / np.float32(HD))
    angle = np.tile(freq, 4)[:, None].astype(np.float32) * np.arange(CLIP, dtype=np.float32)[None, :]
    sign = np.where(np.arange(P) % HD < HD // 2, -1.0, 1.0).astype(np.float32)[:, None]
    lay["cos"] = np.cos(angle).astype(np.float32)
    lay["sin"] = (sign * np.sin(angle)).astype(np.float32)
    k, q = np.arange(P)[:, None], np.arange(P)[None, :]
    lay["maskT"] = ((q // CLIP == k // CLIP) & (k <= q)).astype(np.float32)


def lay_ternary_mlp(lay, f):
    def left(w):
        return w.reshape(-1, P, DC, P).transpose(3, 0, 2, 1).reshape(P, -1)
    lay["w_ter"] = np.stack([left(f["L1_ffn_w1"]), left(f["L1_ffn_w2"]),
                             f["L1_ffn_w3"].T.reshape(-1, P, D).transpose(1, 0, 2).reshape(P, -1)])


def kernel(**inputs):
    import concourse.bacc as bacc
    from concourse.bass_utils import run_bass_kernel_spmd

    f = {k: np.ascontiguousarray(v) for k, v in inputs.items()}
    lay = {"ident": np.eye(P, dtype=np.float32)}
    for fill in (lay_token, lay_attention, lay_memory_mlp, lay_rotary_attention, lay_ternary_mlp):
        fill(lay, f)
    lay = {k: np.ascontiguousarray(v) for k, v in lay.items()}
    nc = bacc.Bacc("TRN2", target_bir_lowering=False, num_devices=1)
    a = {k: nc.dram_tensor(f"in_{k}", v.shape, F32, kind="ExternalInput").ap() for k, v in lay.items()}
    out = nc.dram_tensor("out", (TILES, P, D), F32, kind="ExternalOutput").ap()
    program(nc, a, out)
    r = run_bass_kernel_spmd(nc, [{f"in_{k}": v for k, v in lay.items()}], core_ids=[0])
    return r.results[0]["out"].reshape(CLIPS, CLIP, D)
```

```python
from contextlib import ExitStack

import numpy as np

import concourse.bass as bass
from concourse import mybir

F32 = mybir.dt.float32
F32R = mybir.dt.float32r
BF16 = mybir.dt.bfloat16
U32 = mybir.dt.uint32
ALU = mybir.AluOpType
ACT = mybir.ActivationFunctionType
AX = mybir.AxisListType

P = 128
CLIPS, CLIP = 32, 64
TOK = CLIPS * CLIP
TILES = TOK // P
D = 512
DC = D // P
BLK = 512
BT = BLK // P
NBLK = TOK // BLK
PACK = 1280
PC = PACK // P
EXPERTS = 4
MLPS = EXPERTS + 1
HID = 512
HC = HID // P
BIG = 1.0e30


class Stage:

    def __init__(self, nc, name):
        self.nc, self.name, self.ctx = nc, name, ExitStack()
        self.sems = []

    def __enter__(self):
        return self

    def __exit__(self, *a):
        self.nc.clear_and_free_semaphores(self.sems)
        self.nc.all_engine_barrier()
        self.ctx.close()

    def sb(self, name, shape, dt=F32):
        return self.ctx.enter_context(self.nc.sbuf_tensor(f"{self.name}_{name}", shape, dt))

    def ps(self, name, shape, dt=F32):
        return self.ctx.enter_context(self.nc.psum_tensor(f"{self.name}_{name}", shape, dt))

    def sem(self, name):
        self.sems.append(self.nc.alloc_semaphore(f"{self.name}_{name}"))
        return self.sems[-1]

    def block(self):
        return self.nc.Block()


def product(pe, out, left, right, start, stop):
    pe.matmul(out, left[0], right[0], start=start, stop=False)
    pe.matmul(out, left[0], right[1], start=False, stop=False)
    return pe.matmul(out, left[1], right[0], start=False, stop=stop)


class Norm:

    def __init__(self, s, nc, h, ident, turn, turns=NBLK):
        self.turns = turns
        self.nc, self.h, self.ident, self.banks = nc, h, ident, turn if isinstance(turn, list) else [turn]
        self.stat = s.sb("ln_stat", [P, BT, 6])
        self.moment = s.sb("ln_moment", [P, BT, 2])
        self.shifted = s.sb("ln_shifted", [P, BT])
        self.rstd = s.sb("ln_rstd", [P, BT])
        self.minus_half = s.sb("ln_minus_half", [P, BT])
        self.xn = s.sb("xn", [P, BT, D])
        self.xT = s.sb("xT", [P, 2, DC, BLK], F32R)
        self.const = s.sem("ln_const")
        self.passed = s.sem("ln_passed")
        self.passed_pool = s.sem("ln_passed_pool")
        self.stat_ready = s.sem("ln_stat_ready")
        self.moment_ready = s.sem("ln_moment_ready")
        self.pool_step = s.sem("ln_pool_step")
        self.rstd_ready = s.sem("ln_rstd_ready")
        self.xn_ready = s.sem("xn_ready")
        self.turned = s.sem("xn_turned")
        self.xT_high = s.sem("xT_high")
        self.xT_ready = s.sem("xT_ready")

    def bank(self, k):
        return self.banks[k % len(self.banks)]

    def pool_start(self, pool):
        pool.memset(self.minus_half[:], -0.5).then_inc(self.const, 1)
        pool.wait_ge(self.const, 1)

    def pool_rstd_block(self, pool, n, first=False):
        pool.wait_ge(self.moment_ready, n * BT + BT)
        pool.sem_inc(self.passed_pool, 1)
        pool.tensor_scalar(self.shifted[:], self.moment[:, :, 1], 1e-5, None, ALU.add).then_inc(self.pool_step, 1)
        pool.wait_ge(self.pool_step, n + 1)
        if not first:
            pool.wait_ge(self.xn_ready, n * BT)
        pool.sem_inc(self.passed_pool, 1)
        pool.tensor_tensor(self.rstd[:], self.shifted[:], self.minus_half[:], ALU.pow).then_inc(self.rstd_ready, 1)

    def pool_rstd(self, pool):
        self.pool_start(pool)
        for n in range(self.turns):
            self.pool_rstd_block(pool, n, first=n == 0)

    def dve_scale(self, dve, n, b, first=False):
        if not first:
            dve.wait_ge(self.xn_ready, n * BT)
            dve.wait_ge(self.moment_ready, n * BT)
            dve.wait_ge(self.turned, n * DC)
        for t in range(BT):
            dve.bn_stats(self.stat[:, t, :], self.h[:, b * BT + t, :]).then_inc(self.stat_ready, 1)
        dve.wait_ge(self.stat_ready, n * BT + BT)
        dve.sem_inc(self.passed, 1)
        for t in range(BT):
            dve.bn_aggr(self.moment[:, t, :], self.stat[:, t, :]).then_inc(self.moment_ready, 1)
        dve.wait_ge(self.rstd_ready, n + 1)
        for t in range(BT):
            dve.tensor_scalar(self.xn[:, t, :], self.h[:, b * BT + t, :], self.moment[:, t, 0:1], self.rstd[:, t:t + 1],
                              ALU.subtract, ALU.mult).then_inc(self.xn_ready, 1)

    def pe_turn_chunk(self, pe, n, k, first=False):
        if k == 0:
            pe.wait_ge(self.xn_ready, n * BT + BT)
        if not first or k >= len(self.banks):
            pe.wait_ge(self.xT_ready, n * DC + k + 1 - len(self.banks))
        for t in range(BT):
            ins = pe.transpose(self.bank(k)[:, t * P:(t + 1) * P], self.xn[:, t, k * P:(k + 1) * P], self.ident[:])
        ins.then_inc(self.turned, 1)

    def act_high_chunk(self, act, n, k):
        act.wait_ge(self.turned, n * DC + k + 1)
        self.nc.scalar.activation(self.xT[:, 0, k, :], self.bank(k)[:], ACT.Copy).then_inc(self.xT_high, 1)

    def dve_low_chunk(self, dve, n, k):
        dve.wait_ge(self.xT_high, n * DC + k + 1)
        dve.tensor_tensor(self.xT[:, 1, k, :], self.bank(k)[:], self.xT[:, 0, k, :].bitcast(F32),
                          ALU.subtract).then_inc(self.xT_ready, 1)

    def pe_turn(self, pe, n, first=False):
        for k in range(DC):
            self.pe_turn_chunk(pe, n, k, first)

    def act_high(self, act, n):
        for k in range(DC):
            self.act_high_chunk(act, n, k)

    def dve_low(self, dve, n):
        for k in range(DC):
            self.dve_low_chunk(dve, n, k)


class Resident:

    def __init__(self, s, nc, pieces, late):
        self.nc, self.pieces, self.early = nc, pieces, pieces - late
        self.late_high = s.sem("w_late_high")
        self.late_ready = s.sem("w_late_ready")
        self.raw = s.sb("w_raw", [P, 2, DC * D])
        self.w = s.sb("w", [P, pieces, 2, DC * D], F32R)
        self.loaded = [s.sem(f"w_loaded{i}") for i in range(2)]
        self.high = s.sem("w_high")
        self.ready = s.sem("w_ready")

    def load(self, sp, src):
        for n in range(self.pieces):
            if n >= 2:
                sp.wait_ge(self.ready, n - 1)
            sp.dma_start(self.raw[:, n % 2, :], src[n]).then_inc(self.loaded[n % 2], 16)

    def split_high(self, act, pieces):
        for n in pieces:
            act.wait_ge(self.loaded[n % 2], 16 * (n // 2 + 1))
            self.nc.scalar.activation(self.w[:, n, 0, :], self.raw[:, n % 2, :], ACT.Copy).then_inc(self.high, 1)

    def split_late(self, pool):
        for i, n in enumerate(range(self.early, self.pieces)):
            pool.wait_ge(self.loaded[n % 2], 16 * (n // 2 + 1))
            pool.tensor_copy(self.w[:, n, 0, :], self.raw[:, n % 2, :]).then_inc(self.late_high, 1)
            pool.wait_ge(self.late_high, i + 1)
            pool.tensor_tensor(self.w[:, n, 1, :], self.raw[:, n % 2, :], self.w[:, n, 0, :].bitcast(F32),
                               ALU.subtract).then_inc(self.late_ready, 1)

    def split_low(self, dve, pieces):
        for n in pieces:
            dve.wait_ge(self.high, n + 1)
            dve.tensor_tensor(self.w[:, n, 1, :], self.raw[:, n % 2, :], self.w[:, n, 0, :].bitcast(F32),
                              ALU.subtract).then_inc(self.ready, 1)

    def pair(self, n, k, c0, c1):
        return [self.w[:, n, i, k * D + c0:k * D + c1] for i in range(2)]


def token_blocks(eng, body):
    with eng.Fori(0, NBLK - 1) as b:
        body(b, False)
    body(NBLK - 1, True)


def token_stage(nc, h, ident, a):
    UNIT = PC * P + D
    with Stage(nc, "tok") as s:
        x_in = s.sb("x_in", [P, BT, PACK])
        square = s.sb("square", [P, PACK])
        sumsq = s.sb("sumsq", [P, BT])
        rstd = s.sb("rstd", [P, BT])
        meansq = s.sb("meansq", [P, BT])
        minus_half = s.sb("minus_half", [P, BT])
        norm_w = s.sb("norm_w", [P, PC])
        router = s.sb("router", [P, PC * EXPERTS])
        router_hl = s.sb("router_hl", [P, 2, PC, EXPERTS], F32R)
        b1 = s.sb("b1", [P, MLPS, HC])
        b2 = s.sb("b2", [MLPS, D])
        xT = s.sb("xT", [P, 2, PC, BLK], F32R)
        raw = s.sb("raw", [P, 2, UNIT])
        w = s.sb("w", [P, HC, 2, UNIT], F32R)
        hid = s.sb("hid", [P, 2, BLK])
        hidT = s.sb("hidT", [P, HC, 2, BLK], F32R)
        logit_max = s.sb("logit_max", [P, BT])
        logit = s.sb("logit", [P, BT, EXPERTS])
        prob = s.sb("prob", [P, BT, EXPERTS])
        total = s.sb("total", [P, BT])
        rank = s.sb("rank", [P, BT, EXPERTS])
        beats = s.sb("beats", [P, 3, BT, EXPERTS])
        top = s.sb("top", [P, BT, EXPERTS])
        top_sum = s.sb("top_sum", [P, BT])
        gate = s.sb("gate", [P, BT, MLPS])
        gateT = s.sb("gateT", [MLPS, BLK])
        logitT = gateT[0:EXPERTS, :]

        turn = [s.ps(f"turn{i}", [P, BLK]) for i in range(2)]
        ps1 = [s.ps(f"ps1_{i}", [P, BLK]) for i in range(2)]
        ps2 = [s.ps(f"ps2_{i}", [P, D]) for i in range(BT)]

        small_in = s.sem("small_in")
        x_loaded = s.sem("x_loaded")
        raw_loaded = [s.sem(f"raw_loaded{i}") for i in range(2)]
        raw_free = s.sem("raw_free")
        consts = s.sem("consts")
        sumsq_ready = s.sem("sumsq_ready")
        rstd_ready = s.sem("rstd_ready")
        pool_step = s.sem("pool_step")
        router_high = s.sem("router_high")
        router_ready = s.sem("router_ready")
        xn_ready = s.sem("xn_ready")
        turned = s.sem("turned")
        turn_free = s.sem("turn_free")
        xT_high = s.sem("xT_high")
        w_high = s.sem("w_high")
        w_ready = s.sem("w_ready")
        unit_used = s.sem("unit_used")
        l1_done = s.sem("l1_done")
        hid_ready = s.sem("hid_ready")
        hid_step = s.sem("hid_step")
        hidT_ready = s.sem("hidT_ready")
        max_ready = s.sem("max_ready")
        logitT_ready = s.sem("logitT_ready")
        passed = s.sem("passed")
        exp_ready = s.sem("exp_ready")
        gate_step = s.sem("gate_step")
        gate_ready = s.sem("gate_ready")
        gateT_ready = s.sem("gateT_ready")
        bias_done = s.sem("bias_done")
        l2_done = s.sem("l2_done")
        ps2_free = s.sem("ps2_free")

        UB = MLPS * HC
        TURNS = PC + 3
        AHEAD = HC - 1
        GATE_STEPS = 12
        START = 1

        def blocks(eng, body):
            with eng.Fori(0, NBLK - 1) as b:
                body(b, False)
            body(NBLK - 1, True)

        def mlps(eng, body):
            body(0, True, False)
            with eng.Fori(1, MLPS - 1) as e:
                body(e, False, False)
            body(MLPS - 1, False, True)

        with s.block() as block:

            @block.sync
            def _(sp):
                for dst, src in ((norm_w, a["norm_w"]), (router, a["router"]), (b2, a["b2"])):
                    sp.dma_start(dst[:], src).then_inc(small_in, 16)
                sp.dma_start(b1[:], a["b1"]).then_inc(small_in, 16)
                sp.dma_start(x_in[:], a["x"][0]).then_inc(x_loaded, 16)

                def of_block(b, last):
                    def of_mlp(e, first, last_mlp):
                        for m in range(HC):
                            sp.wait_ge(raw_free, (b * MLPS + e) * HC + m + 1)
                            sp.dma_start(raw[:, m % 2, :], a["w_units"][e * HC + m]).then_inc(raw_loaded[m % 2], 16)
                        if first and not last:
                            sp.wait_ge(turned, b * TURNS + PC)
                            sp.dma_start(x_in[:], a["x"][b + 1]).then_inc(x_loaded, 16)
                    mlps(sp, of_mlp)
                blocks(sp, of_block)

            @block.gpsimd
            def _(pool):
                pool.memset(minus_half[:], -0.5).then_inc(consts, 1)
                pool.wait_ge(consts, 1)
                for b in range(NBLK):
                    pool.wait_ge(sumsq_ready, b * BT + BT)
                    pool.tensor_scalar(meansq[:], sumsq[:], 1.0 / PACK, 1e-6, ALU.mult, ALU.add).then_inc(pool_step, 1)
                    pool.wait_ge(pool_step, b + 1)
                    if b:
                        pool.wait_ge(xn_ready, b * BT)
                    pool.tensor_tensor(rstd[:], meansq[:], minus_half[:], ALU.pow).then_inc(rstd_ready, 1)

            @block.scalar
            def _(act):
                act.sem_inc(hid_ready, START)
                act.wait_ge(small_in, 64)
                nc.scalar.activation(router_hl[:, 0].rearrange("p c e -> p (c e)"), router[:], ACT.Copy).then_inc(router_high, 1)

                def squares(nb, tiles):
                    act.wait_ge(x_loaded, nb * 16 + 16)
                    for t in tiles:
                        if t:
                            act.wait_ge(sumsq_ready, nb * BT + t)
                        nc.scalar.activation(square[:], x_in[:, t, :], ACT.Square,
                                             accum_out=sumsq[:, t:t + 1]).then_inc(sumsq_ready, 1)

                def split_high(b, e, m):
                    n = b * MLPS + e
                    act.wait_ge(raw_loaded[m % 2], 16 * (n * 2 + m // 2 + 1))
                    act.wait_ge(unit_used, n * HC + m + 1)
                    nc.scalar.activation(w[:, m, 0, :], raw[:, m % 2, :], ACT.Copy).then_inc(w_high, 1)

                def high_chunks(nb):
                    for kc in range(PC):
                        act.wait_ge(turned, nb * TURNS + kc + 1)
                        if kc == 0:
                            act.wait_ge(l1_done, START + nb * UB)
                        nc.scalar.activation(xT[:, 0, kc, :], turn[kc % 2][:], ACT.Copy,
                                             scale=norm_w[:, kc:kc + 1]).then_inc(xT_high, 1)

                squares(0, range(BT))
                high_chunks(0)
                for m in range(AHEAD):
                    split_high(0, 0, m)

                def of_block(b, last):
                    act.wait_ge(max_ready, b + 1)
                    nc.scalar.activation(prob[:], logit[:], ACT.Exp).then_inc(exp_ready, 1)

                    def of_mlp(e, first, last_mlp):
                        n = b * MLPS + e
                        for m in range(HC):
                            act.wait_ge(l1_done, START + n * HC + m + 1)
                            act.wait_ge(hidT_ready, START + n * HC + m)
                            nc.scalar.activation(hid[:, m % 2, :], ps1[m % 2][:], ACT.Gelu,
                                                 bias=b1[:, bass.ds(e, 1), m]).then_inc(hid_ready, 1)
                            if m == 0:
                                split_high(b, e, AHEAD)
                            elif not last_mlp:
                                split_high(b, e + 1, m - 1)
                            elif not last and m < HC - 1:
                                split_high(b + 1, 0, m - 1)
                            if last_mlp and not last and m < 2:
                                if m == 0:
                                    act.wait_ge(rstd_ready, b + 1)
                                    act.wait_ge(sumsq_ready, (b + 1) * BT)
                                squares(b + 1, (2 * m, 2 * m + 1))
                        if last_mlp and not last:
                            high_chunks(b + 1)
                            split_high(b + 1, 0, HC - 2)
                    mlps(act, of_mlp)
                blocks(act, of_block)

            @block.vector
            def _(dve):
                dve.sem_inc(hidT_ready, START)
                dve.memset(gate[:, :, EXPERTS:], 1.0).then_inc(gate_step, 1)
                dve.wait_ge(router_high, 1)
                dve.tensor_tensor(router_hl[:, 1].rearrange("p c e -> p (c e)"), router[:],
                                  router_hl[:, 0].rearrange("p c e -> p (c e)").bitcast(F32),
                                  ALU.subtract).then_inc(router_ready, 1)

                def normalise(nb, tiles):
                    dve.wait_ge(rstd_ready, nb + 1)
                    for t in tiles:
                        dve.tensor_scalar(x_in[:, t, :], x_in[:, t, :], rstd[:, t:t + 1], None,
                                          ALU.mult).then_inc(xn_ready, 1)

                def split_low(b, e, m):
                    n = b * MLPS + e
                    dve.wait_ge(w_high, n * HC + m + 1)
                    dve.tensor_tensor(w[:, m, 1, :], raw[:, m % 2, :], w[:, m, 0, :].bitcast(F32),
                                      ALU.subtract).then_inc(w_ready, 1)
                    dve.wait_ge(w_ready, n * HC + m + 1)
                    dve.sem_inc(raw_free, 1)

                dve.sem_inc(raw_free, 2)
                def low_chunks(nb):
                    for kc in range(PC):
                        dve.wait_ge(xT_high, nb * PC + kc + 1)
                        dve.scalar_tensor_tensor(out=xT[:, 1, kc, :], in0=turn[kc % 2][:], scalar=norm_w[:, kc:kc + 1],
                                                 in1=xT[:, 0, kc, :].bitcast(F32), op0=ALU.mult,
                                                 op1=ALU.subtract).then_inc(turn_free, 1)

                normalise(0, range(BT))
                low_chunks(0)
                for m in range(AHEAD):
                    split_low(0, 0, m)

                def gates(b):
                    G = 1 + b * GATE_STEPS
                    step = [0]

                    def chain(ins):
                        step[0] += 1
                        ins.then_inc(gate_step, 1)
                        dve.wait_ge(gate_step, G + step[0])

                    dve.wait_ge(turned, b * TURNS + PC + 1)
                    dve.tensor_copy(logitT, turn[0][0:EXPERTS, :]).then_inc(logitT_ready, 1)
                    dve.wait_ge(logitT_ready, b + 1)
                    dve.sem_inc(turn_free, 1)
                    dve.wait_ge(turned, b * TURNS + PC + 2)
                    lg = turn[1][:, 0:BT * EXPERTS].rearrange("p (t e) -> p t e", t=BT)
                    chain(dve.tensor_reduce(logit_max[:], lg, AX.X, ALU.max))
                    dve.tensor_tensor(logit[:], lg, logit_max[:].rearrange("p (t o) -> p t o", o=1).broadcast_to([P, BT, EXPERTS]),
                                      ALU.subtract).then_inc(max_ready, 1)
                    dve.wait_ge(max_ready, b + 1)
                    dve.sem_inc(turn_free, 1)
                    dve.wait_ge(exp_ready, b + 1)
                    chain(dve.tensor_reduce(total[:], prob[:], AX.X, ALU.add))
                    for e in range(EXPERTS):
                        mine = prob[:, :, e:e + 1]
                        k = 0
                        for o in range(EXPERTS):
                            if o != e:
                                ins = dve.tensor_tensor(beats[:, k, :, e:e + 1], prob[:, :, o:o + 1], mine,
                                                        ALU.is_ge if o < e else ALU.is_gt)
                                k += 1
                    chain(ins)
                    chain(dve.tensor_tensor(rank[:], beats[:, 0], beats[:, 1], ALU.add))
                    chain(dve.tensor_tensor(rank[:], rank[:], beats[:, 2], ALU.add))
                    chain(dve.tensor_scalar(rank[:], rank[:], 2.0, None, ALU.is_lt))
                    chain(dve.reciprocal(total[:], total[:]))
                    chain(dve.tensor_tensor(prob[:], prob[:], total[:].rearrange("p (t o) -> p t o", o=1).broadcast_to([P, BT, EXPERTS]), ALU.mult))
                    chain(dve.tensor_tensor(top[:], prob[:], rank[:], ALU.mult))
                    chain(dve.tensor_reduce(top_sum[:], top[:], AX.X, ALU.add))
                    chain(dve.tensor_scalar(top_sum[:], top_sum[:], 1e-6, None, ALU.add))
                    chain(dve.reciprocal(top_sum[:], top_sum[:]))
                    dve.tensor_tensor(gate[:, :, 0:EXPERTS], top[:], top_sum[:].rearrange("p (t o) -> p t o", o=1).broadcast_to([P, BT, EXPERTS]),
                                      ALU.mult).then_inc(gate_ready, 1)

                def of_block(b, last):
                    gates(b)
                    dve.wait_ge(turned, b * TURNS + PC + 3)
                    dve.tensor_copy(gateT[:], turn[0][0:MLPS, :]).then_inc(gateT_ready, 1)
                    dve.wait_ge(gateT_ready, b + 1)
                    dve.sem_inc(turn_free, 1)

                    def take(e, t):
                        n = b * MLPS + e
                        if t < BT - 1:
                            dve.wait_ge(l2_done, n * (BT - 1) + t + 1)
                        else:
                            dve.wait_ge(unit_used, HC + (n + 1) * HC)
                        dve.scalar_tensor_tensor(out=h[:, b * BT + t, :], in0=ps2[t][:], scalar=gate[:, t, bass.ds(e, 1)],
                                                 in1=h[:, b * BT + t, :], op0=ALU.mult,
                                                 op1=ALU.add).then_inc(ps2_free, 1)

                    def of_mlp(e, first, last_mlp):
                        n = b * MLPS + e
                        for m in range(HC):
                            dve.wait_ge(hid_ready, START + n * HC + m + 1)
                            dve.tensor_copy(hidT[:, m, 0, :], hid[:, m % 2, :]).then_inc(hid_step, 1)
                            dve.wait_ge(hid_step, n * HC + m + 1)
                            dve.tensor_tensor(hidT[:, m, 1, :], hid[:, m % 2, :], hidT[:, m, 0, :].bitcast(F32),
                                              ALU.subtract).then_inc(hidT_ready, 1)
                            if m == 1 and first:
                                for t in range(BT):
                                    dve.wait_ge(bias_done, b * BT + t + 1)
                                    dve.tensor_copy(h[:, b * BT + t, :], ps2[t][:]).then_inc(ps2_free, 1)
                            if m == 0 and not first:
                                for t in range(BT):
                                    take(e - 1, t)
                            if m == 0:
                                split_low(b, e, AHEAD)
                            elif not last_mlp:
                                split_low(b, e + 1, m - 1)
                            elif not last and m < HC - 1:
                                split_low(b + 1, 0, m - 1)
                            if last_mlp and not last and m >= 2:
                                normalise(b + 1, (2 * m - 4, 2 * m - 3))
                        if last_mlp:
                            if not last:
                                low_chunks(b + 1)
                                split_low(b + 1, 0, HC - 2)
                            for t in range(BT):
                                take(e, t)
                    mlps(dve, of_mlp)
                blocks(dve, of_block)

            @block.tensor
            def _(pe):
                pe.sem_inc(l1_done, START)
                pe.sem_inc(unit_used, HC)
                pe.sem_inc(turn_free, 2)
                pe.sem_inc(ps2_free, BT)
                pe.wait_ge(router_ready, 1)

                def turn_chunk(nb, kc):
                    if kc == 0:
                        pe.wait_ge(xn_ready, nb * BT + BT)
                    pe.wait_ge(turn_free, nb * TURNS + max(kc + 1, 2))
                    for t in range(BT):
                        ins = pe.transpose(turn[kc % 2][:, t * P:(t + 1) * P], x_in[:, t, kc * P:(kc + 1) * P], ident[:])
                    ins.then_inc(turned, 1)

                for kc in range(PC):
                    turn_chunk(0, kc)

                def of_block(b, last):
                    NB = b * (MLPS + 1) * BT
                    pe.wait_ge(turn_free, b * TURNS + PC + 2)
                    for kc in range(PC):
                        ins = product(pe, turn[0][0:EXPERTS, :], [router_hl[:, i, kc, :] for i in range(2)],
                                      [xT[:, i, kc, :] for i in range(2)], kc == 0, kc == PC - 1)
                    ins.then_inc(turned, 1)

                    def layer1(e, m):
                        n = b * MLPS + e
                        pe.wait_ge(w_ready, n * HC + m + 1)
                        pe.wait_ge(hid_ready, START + n * HC + max(m - 1, 0))
                        for kc in range(PC):
                            ins = product(pe, ps1[m % 2][:],
                                          [w[:, m, i, kc * P:(kc + 1) * P] for i in range(2)],
                                          [xT[:, i, kc, :] for i in range(2)], kc == 0, kc == PC - 1)
                        ins.then_inc(l1_done, 1)

                    def layer2(e, m, chunks=()):
                        n = b * MLPS + e
                        pe.wait_ge(hidT_ready, START + n * HC + m + 1)
                        for t in range(BT):
                            if m == 0:
                                pe.wait_ge(ps2_free, NB + (e + 1) * BT + t + 1)
                            ins = product(pe, ps2[t][:],
                                          [hidT[:, m, i, t * P:(t + 1) * P] for i in range(2)],
                                          [w[:, m, i, PC * P:] for i in range(2)], m == 0, m == HC - 1)
                            if t == BT - 1:
                                ins.then_inc(unit_used, 1)
                            elif m == HC - 1:
                                ins.then_inc(l2_done, 1)
                            if chunks:
                                turn_chunk(b + 1, chunks[t])

                    def of_mlp(e, first, last_mlp):
                        layer1(e, 0)
                        if first:
                            pe.wait_ge(logitT_ready, b + 1)
                            pe.sem_inc(passed, 1)
                            for t in range(BT):
                                ins = pe.transpose(turn[1][:, t * EXPERTS:(t + 1) * EXPERTS],
                                                   logitT[:, t * P:(t + 1) * P], ident[0:EXPERTS, 0:EXPERTS])
                            ins.then_inc(turned, 1)
                        else:
                            layer2(e - 1, HC - 1)
                        layer1(e, 1)
                        if first:
                            pe.wait_ge(gate_ready, b + 1)
                            pe.wait_ge(turn_free, b * TURNS + PC + 3)
                            for t in range(BT):
                                ins = pe.transpose(turn[0][0:MLPS, t * P:(t + 1) * P], gate[:, t, :], ident[:])
                            ins.then_inc(turned, 1)
                            pe.wait_ge(gateT_ready, b + 1)
                            for t in range(BT):
                                pe.wait_ge(ps2_free, NB + t + 1)
                                pe.matmul(ps2[t][:], gateT[:, t * P:(t + 1) * P], b2[:], start=True,
                                          stop=True).then_inc(bias_done, 1)
                        layer2(e, 0)
                        layer1(e, 2)
                        layer2(e, 1)
                        layer1(e, 3)
                        turning = last_mlp and not last
                        layer2(e, 2, range(0, BT) if turning else ())
                        if last_mlp:
                            layer2(e, 3, range(BT, 2 * BT) if turning else ())
                        if turning:
                            for kc in range(2 * BT, PC):
                                turn_chunk(b + 1, kc)
                    mlps(pe, of_mlp)
                blocks(pe, of_block)


def attention_stage(nc, h, ident, a):
    HEADS, HD = 16, 32
    SCALE = float(np.float32(1.0) / np.sqrt(np.float32(HD)))
    GROUP = P // HD
    UNITS = DC * BT
    SLOTS = 4
    with Stage(nc, "at0") as s:
        turn = s.ps("turn", [P, BLK])
        mm = [s.ps(f"mm{i}", [P, BLK]) for i in range(2)]
        score = [s.ps(f"score{i}", [P, GROUP, P]) for i in range(2)]
        probT_ps = s.ps("probT_ps", [P, GROUP, P])
        oT_ps = [s.ps(f"oT_ps{i}", [P, P]) for i in range(2)]
        ln = Norm(s, nc, h, ident, turn)
        w = Resident(s, nc, 4, 1)
        WQ, WK, WV, WP = range(4)
        bq = s.sb("bq", [P, DC])
        bk = s.sb("bk", [P, DC])
        bv = s.sb("bv", [P, D])
        bp = s.sb("bp", [P, D])
        mask = s.sb("mask", [P, P])
        qT = s.sb("qT", [P, 2, 2, BLK], F32R)
        k_wide = s.sb("k_wide", [P, 2, 2, GROUP, BLK], F32R)
        v = s.sb("v", [P, BT, D])
        least = s.sb("least", [P, SLOTS, GROUP])
        prob_sum = s.sb("prob_sum", [P, SLOTS, GROUP])
        inv_sum = s.sb("inv_sum", [P, SLOTS, GROUP])
        biased = s.sb("biased", [P, D])
        prob, probT = [w.raw[:, i, :].rearrange("p (s j k) -> p s j k", s=SLOTS, j=GROUP) for i in range(2)]
        oT = s.sb("oT", [P, 2, BT, DC, P], F32R)

        small_in = s.sem("small_in")
        zeros_ready = s.sem("zeros_ready")
        wide_ready = s.sem("wide_ready")
        mm_done = s.sem("mm_done")
        mm_free = [s.sem(f"mm_free{i}") for i in range(2)]
        q_high = s.sem("q_high")
        k_high = s.sem("k_high")
        k_low = s.sem("k_low")
        score_done = s.sem("score_done")
        masked_ready = s.sem("masked_ready")
        least_ready = s.sem("least_ready")
        exp_ready = s.sem("exp_ready")
        inv_ready = s.sem("inv_ready")
        prob_ready = s.sem("prob_ready")
        prob_turned = s.sem("prob_turned")
        probT_ready = s.sem("probT_ready")
        o_done = s.sem("o_done")
        oT_high = s.sem("oT_high")
        oT_ready = s.sem("oT_ready")
        passed = s.sem("passed")
        h_ready = s.sem("h_ready")
        out_done = s.sem("out_done")
        out_free = s.sem("out_free")

        MM = 3 * DC
        PE_AT = {-1: (1, 0), 0: (1, 1), 3: (2, 0), 4: (2, 1), 7: (3, 0), 8: (3, 1)}
        ACT_AT = {u + 1: x for u, x in PE_AT.items()}
        DVE_AT = {u + 2: x for u, x in PE_AT.items()}
        PE_OUT = {1: 0, 2: 1, 5: 2, 6: 3}
        DVE_OUT = {u + 2: t for u, t in PE_OUT.items()}
        LN_UNIT = UNITS - DC

        def bank_free(j):
            return j // 2 + 2

        def blocks(eng, body):
            body(0, True, False)
            with eng.Fori(1, NBLK - 1) as b:
                body(b, False, False)
            body(NBLK - 1, False, True)

        with s.block() as block:

            @block.sync
            def _(sp):
                for dst, src in ((bq, "bq"), (bk, "bk"), (mask, "mask")):
                    sp.dma_start(dst[:], a[src]).then_inc(small_in, 16)
                for dst, src in ((bv, "bv"), (bp, "bp")):
                    sp.dma_start(dst[:], a[src].partition_broadcast(P)).then_inc(small_in, 16)
                w.load(sp, a["w_at0"])

            @block.gpsimd
            def _(pool):
                pool.memset(v[:], 0.0).then_inc(zeros_ready, 1)
                ln.pool_start(pool)
                ln.pool_rstd_block(pool, 0, first=True)
                w.split_late(pool)

                def of_block(b, first, last):
                    if not last:
                        ln.pool_rstd_block(pool, b + 1)
                    for u in range(UNITS):
                        n = b * UNITS + u
                        pool.wait_ge(inv_ready, n + 1)
                        pool.sem_inc(passed, 1)
                        pool.tensor_tensor(prob[:, u % SLOTS], prob[:, u % SLOTS],
                                           inv_sum[:, u % SLOTS].rearrange("p (j o) -> p j o", o=1).broadcast_to([P, GROUP, P]),
                                           ALU.mult).then_inc(prob_ready, 1)
                blocks(pool, of_block)

            @block.scalar
            def _(act):
                act.wait_ge(small_in, 80)
                w.split_high(act, range(2))
                ln.act_high(act, 0)
                w.split_high(act, range(2, w.early))
                act.wait_ge(wide_ready, 4)

                def of_block(b, first, last):
                    def high_q(c):
                        act.wait_ge(mm_done, b * MM + BT + 2 * c + 2)
                        if c >= 2:
                            act.wait_ge(score_done, b * UNITS + (c - 1) * BT)
                        nc.scalar.activation(qT[:, c % 2, 0, :], mm[1][:], ACT.Identity,
                                             bias=bq[:, c:c + 1]).then_inc(q_high, 1)

                    def high_k(c):
                        act.wait_ge(mm_done, b * MM + BT + 2 * c + 1)
                        if c >= 2:
                            act.wait_ge(score_done, b * UNITS + (c - 1) * BT)
                        for j in range(GROUP):
                            rows = slice(j * HD, (j + 1) * HD)
                            nc.scalar.activation(k_wide[rows, c % 2, 0, j, :], mm[0][rows, :], ACT.Identity,
                                                 bias=bk[rows, c:c + 1]).then_inc(k_high, 1)

                    def exponentials(u):
                        act.wait_ge(least_ready, b * UNITS + u + 1)
                        for j in range(GROUP):
                            nc.scalar.activation(prob[:, u % SLOTS, j, :], prob[:, u % SLOTS, j, :], ACT.Exp,
                                                 bias=least[:, u % SLOTS, j:j + 1], scale=-1.0,
                                                 accum_out=prob_sum[:, u % SLOTS, j:j + 1]).then_inc(exp_ready, 1)

                    def copy_probT(u):
                        n = b * UNITS + u
                        act.wait_ge(prob_turned, n + 1)
                        if u >= SLOTS:
                            act.wait_ge(o_done, n - SLOTS + 1)
                        nc.scalar.activation(probT[:, u % SLOTS], probT_ps[:], ACT.Copy).then_inc(probT_ready, 1)

                    def take_oT(u):
                        if u < BT and not first:
                            act.wait_ge(out_done, b * BT + (u + 1 - BT))
                        act.wait_ge(o_done, b * UNITS + u + 1)
                        nc.scalar.activation(oT[:, 0, u % BT, u // BT, :], oT_ps[u % 2][:], ACT.Copy).then_inc(oT_high, 1)

                    high_k(0)
                    high_q(0)
                    act.wait_ge(w.late_ready, 1)
                    for u in range(UNITS + 5):
                        if 3 <= u < UNITS + 3:
                            copy_probT(u - 3)
                        if u >= 5:
                            take_oT(u - 5)
                        if u < UNITS:
                            exponentials(u)
                        if u in ACT_AT:
                            c, i = ACT_AT[u]
                            (high_k, high_q)[i](c)
                        if LN_UNIT <= u < UNITS and not last:
                            ln.act_high_chunk(act, b + 1, u - LN_UNIT)
                blocks(act, of_block)

            @block.vector
            def _(dve):
                ln.dve_scale(dve, 0, 0, first=True)
                dve.wait_ge(zeros_ready, 1)
                for i in range(2):
                    for x in range(2):
                        dve.tensor_copy(k_wide[:, i, x], v[:]).then_inc(wide_ready, 1)
                w.split_low(dve, range(2))
                ln.dve_low(dve, 0)
                w.split_low(dve, range(2, w.early))
                dve.sem_inc(h_ready, BT)
                dve.wait_ge(small_in, 80)

                def add_out(b, t):
                    n = b * BT + (t - BT)
                    dve.wait_ge(out_done, n + 1)
                    dve.wait_ge(h_ready, n + BT)
                    dve.tensor_tensor(biased[:], mm[t % 2][:], bp[:], ALU.add).then_inc(out_free, 1)
                    dve.wait_ge(out_free, n + 1)
                    dve.tensor_tensor(h[:, n, :], h[:, n, :], biased[:], ALU.add).then_inc(h_ready, 1)

                def of_block(b, first, last):
                    if not last:
                        ln.dve_scale(dve, b + 1, b + 1)
                    for t in range(BT):
                        dve.wait_ge(mm_done, b * MM + t + 1)
                        dve.tensor_tensor(v[:, t, :], mm[t % 2][:], bv[:], ALU.add).then_inc(mm_free[t % 2], 1)

                    def low_q(c):
                        n = b * DC + c
                        dve.wait_ge(q_high, n + 1)
                        dve.sem_inc(passed, 1)
                        dve.scalar_tensor_tensor(out=qT[:, c % 2, 1, :], in0=mm[1][:], scalar=bq[:, c:c + 1],
                                                 in1=qT[:, c % 2, 0, :].bitcast(F32),
                                                 op0=ALU.add, op1=ALU.subtract).then_inc(mm_free[1], 1)

                    def low_k(c):
                        n = b * DC + c
                        dve.wait_ge(k_high, (n + 1) * GROUP)
                        dve.sem_inc(passed, 1)
                        for j in range(GROUP):
                            rows = slice(j * HD, (j + 1) * HD)
                            dve.scalar_tensor_tensor(out=k_wide[rows, c % 2, 1, j, :], in0=mm[0][rows, :], scalar=bk[rows, c:c + 1],
                                                     in1=k_wide[rows, c % 2, 0, j, :].bitcast(F32),
                                                     op0=ALU.add, op1=ALU.subtract).then_inc(mm_free[0] if j == GROUP - 1 else k_low, 1)

                    def masked_scores(u):
                        n = b * UNITS + u
                        dve.wait_ge(score_done, n + 1)
                        if u >= SLOTS:
                            dve.wait_ge(prob_turned, n - SLOTS + 1)
                        dve.sem_inc(passed, 1)
                        dve.scalar_tensor_tensor(out=prob[:, u % SLOTS], in0=score[u % 2][:], scalar=-SCALE,
                                                 in1=mask[:].rearrange("p (o k) -> p o k", o=1).broadcast_to([P, GROUP, P]),
                                                 op0=ALU.mult, op1=ALU.add).then_inc(masked_ready, 1)
                        dve.wait_ge(masked_ready, n + 1)
                        dve.tensor_reduce(least[:, u % SLOTS], prob[:, u % SLOTS], AX.X, ALU.min).then_inc(least_ready, 1)

                    def inverse_sums(u):
                        n = b * UNITS + u
                        dve.wait_ge(exp_ready, (n + 1) * GROUP)
                        dve.reciprocal(inv_sum[:, u % SLOTS], prob_sum[:, u % SLOTS]).then_inc(inv_ready, 1)

                    def low_oT(u):
                        dve.wait_ge(oT_high, b * UNITS + u + 1)
                        dve.tensor_tensor(oT[:, 1, u % BT, u // BT, :], oT_ps[u % 2][:],
                                          oT[:, 0, u % BT, u // BT, :].bitcast(F32), ALU.subtract).then_inc(oT_ready, 1)

                    low_k(0)
                    low_q(0)
                    for u in range(UNITS + 5):
                        if u >= 5:
                            low_oT(u - 5)
                        if u < UNITS:
                            masked_scores(u)
                        if 1 <= u <= UNITS:
                            inverse_sums(u - 1)
                        if u in DVE_AT:
                            c, i = DVE_AT[u]
                            (low_k, low_q)[i](c)
                        if u in DVE_OUT and not first:
                            add_out(b, DVE_OUT[u])
                        if LN_UNIT <= u < UNITS and not last:
                            ln.dve_low_chunk(dve, b + 1, u - LN_UNIT)
                    if last:
                        for t in range(BT):
                            add_out(NBLK, t)
                blocks(dve, of_block)
                dve.wait_ge(h_ready, NBLK * BT + BT)

            @block.tensor
            def _(pe):
                pe.sem_inc(mm_free[0], 1)
                pe.sem_inc(mm_free[1], 1)
                ln.pe_turn(pe, 0, first=True)
                pe.wait_ge(w.ready, w.early)

                def project_out(b, t, free):
                    pe.wait_ge(mm_free[t % 2], free)
                    pe.wait_ge(oT_ready, b * UNITS - BT + t + 1)
                    pe.wait_ge(w.late_ready, 1)
                    if isinstance(b, int) and t >= 2:
                        pe.wait_ge(out_free, (b - 1) * BT + t - 1)
                    for c in range(DC):
                        ins = product(pe, mm[t % 2][:], [oT[:, x, t, c, :] for x in range(2)], w.pair(WP, c, 0, D),
                                      c == 0, c == DC - 1)
                    ins.then_inc(out_done, 1)

                def of_block(b, first, last):
                    pe.wait_ge(ln.xT_ready, b * DC + DC)

                    def take_mm(j):
                        pe.wait_ge(mm_free[j % 2], b * (MM // 2) + j // 2 + 1)
                        return mm[j % 2][:]

                    def project_in(c, i):
                        out = take_mm(BT + 2 * c + i)
                        if c >= 2 and not first:
                            pe.wait_ge(out_free, b * BT + (2 * c - 3 + i - BT))
                        for k in range(DC):
                            ins = product(pe, out, w.pair((WK, WQ)[i], k, c * P, (c + 1) * P),
                                          [ln.xT[:, x, k, :] for x in range(2)], k == 0, k == DC - 1)
                        ins.then_inc(mm_done, 1)

                    for t in range(BT):
                        out = take_mm(t)
                        for k in range(DC):
                            ins = product(pe, out, [ln.xT[:, x, k, t * P:(t + 1) * P] for x in range(2)],
                                          w.pair(WV, k, 0, D), k == 0, k == DC - 1)
                        ins.then_inc(mm_done, 1)
                    project_in(0, 0)
                    project_in(0, 1)

                    def scores(u):
                        n = b * UNITS + u
                        c, t = u // BT, u % BT
                        if t == 0:
                            for i in range(2):
                                pe.wait_ge(mm_free[i], b * (MM // 2) + bank_free(BT + 2 * c))
                        if u >= 2:
                            pe.wait_ge(masked_ready, n - 1)
                        cols = slice(t * P, (t + 1) * P)
                        product(pe, score[u % 2][:], [qT[:, c % 2, x, cols] for x in range(2)],
                                [k_wide[:, c % 2, x, :, cols] for x in range(2)], True, True).then_inc(score_done, 1)

                    def turn_prob(u):
                        n = b * UNITS + u
                        pe.wait_ge(prob_ready, n + 1)
                        if u:
                            pe.wait_ge(probT_ready, n)
                        for j in range(GROUP):
                            ins = pe.transpose(probT_ps[:, j, :], prob[:, u % SLOTS, j, :], ident[:])
                        ins.then_inc(prob_turned, 1)

                    def heads(u):
                        n = b * UNITS + u
                        c, t = u // BT, u % BT
                        pe.wait_ge(probT_ready, n + 1)
                        if u >= 2:
                            pe.wait_ge(oT_ready, n - 1)
                        for j in range(GROUP):
                            ins = pe.matmul(oT_ps[u % 2][j * HD:(j + 1) * HD, :], v[:, t, c * P + j * HD:c * P + (j + 1) * HD],
                                            probT[:, u % SLOTS, j, :], start=True, stop=True)
                        ins.then_inc(o_done, 1)

                    for u in range(-1, UNITS + 3):
                        if u + 1 < UNITS:
                            scores(u + 1)
                        if 2 <= u < UNITS + 2:
                            turn_prob(u - 2)
                        if u in PE_AT:
                            project_in(*PE_AT[u])
                        if u in PE_OUT and not first:
                            project_out(b, PE_OUT[u], b * (MM // 2) + bank_free(BT + 2 * (1 + PE_OUT[u] // 2)))
                        if LN_UNIT - 1 <= u < UNITS - 1 and not last:
                            ln.pe_turn_chunk(pe, b + 1, u - LN_UNIT + 1)
                        if u >= 3:
                            heads(u - 3)
                    if last:
                        for t in range(BT):
                            project_out(NBLK, t, NBLK * (MM // 2) + 1)
                blocks(pe, of_block)


def memory_mlp_stage(nc, h, ident, a):
    INTER = 2048
    UM = INTER // P
    KEYS, TOP, EXP = 64, 8, 1024
    UE = EXP // P
    XK = EXP // KEYS
    U = UM + UE
    RD = 64
    WM, WE = DC * 2 * P + D, DC * P + D
    SLOTS = 4
    AHEAD = SLOTS - 1
    ROWS = KEYS + XK + 1
    TSTEPS, BSTEPS = 16, 6
    START = 2
    with Stage(nc, "mem") as s:
        turn = s.ps("turn", [P, BLK])
        gu = [s.ps(f"gu{i}", [P, BLK]) for i in range(3)]
        out_ps = [s.ps(f"out{i}", [P, D]) for i in range(BT)]
        ln = Norm(s, nc, h, ident, [turn, gu[2]], 2 * NBLK)
        wq_raw = s.sb("wq_raw", [P, DC * P])
        wq = s.sb("wq", [P, 2, DC * P], F32R)
        keys = s.sb("keys", [RD, 2, KEYS])
        iota = s.sb("iota", [P, KEYS])
        ysteps = s.sb("ysteps", [P, TOP])
        select_raw = s.sb("select_raw", [ROWS, EXP + P])
        select = s.sb("select", [ROWS, EXP + P], F32R)
        query = s.sb("query", [RD, TOK, 2])
        tile_query = s.sb("tile_query", [RD, 2, P])
        raw = s.sb("raw", [P, 2, WM])
        w = s.sb("w", [P, SLOTS, 2, WM], F32R)
        act_out = s.sb("act_out", [P, 2, BLK])
        hid = s.sb("hid", [P, BLK])
        hidT = s.sb("hidT", [P, 2, 2, BLK], F32R)
        route = s.sb("route", [P, 2, KEYS])
        best = s.sb("best", [P, 2, TOP])
        best_at = s.sb("best_at", [P, 2, TOP], U32)
        best_pos = s.sb("best_pos", [P, BT, 2, TOP])
        pair = s.sb("pair", [P, BT, TOP, TOP])
        pair_now = s.sb("pair_now", [P, TOP, TOP])
        pair_best = s.sb("pair_best", [P, TOP])
        marked = s.sb("marked", [P, TOP, TOP])
        chosen = s.sb("chosen", [P, BT, TOP, TOP])
        count = s.sb("count", [P, TOP])
        hit = s.sb("hit", [P, TOP, KEYS])
        pair_exp = s.sb("pair_exp", [P, BT, TOP * TOP])
        row_sum = s.sb("row_sum", [P, BT, TOP])
        clamped = s.sb("clamped", [P, BT, TOP])
        inv_total = s.sb("inv_total", [P, BT])
        rows = s.sb("rows", [P, BT, 2, ROWS])
        rowsT = s.sb("rowsT", [ROWS, 2, BLK], F32R)
        rankT = s.sb("rankT", [ROWS, BLK], F32R)
        expo = s.sb("expo", [P, 2, BLK])
        mix = s.sb("mix", [P, UE, BLK])

        small_in = s.sem("small_in")
        q_high = s.sem("q_high")
        q_split = s.sem("q_split")
        q_done = s.sem("q_done")
        query_ready = s.sem("query_ready")
        raw_loaded = [s.sem(f"raw_loaded{i}") for i in range(2)]
        raw_free = s.sem("raw_free")
        w_high = s.sem("w_high")
        w_ready = s.sem("w_ready")
        unit_used = s.sem("unit_used")
        g_done = s.sem("g_done")
        u_done = s.sem("u_done")
        silu_ready = s.sem("silu_ready")
        hid_step = s.sem("hid_step")
        hid_high = s.sem("hid_high")
        hid_ready = s.sem("hid_ready")
        out_done = s.sem("out_done")
        out_free = s.sem("out_free")
        route_done = s.sem("route_done")
        route_step = s.sem("route_step")
        pair_in = s.sem("pair_in")
        pair_exp_ready = s.sem("pair_exp_ready")
        block_step = s.sem("block_step")
        rows_ready = s.sem("rows_ready")
        rows_turned = s.sem("rows_turned")
        rows_high = s.sem("rows_high")
        rows_low = s.sem("rows_low")
        rank_ready = s.sem("rank_ready")
        mix_done = s.sem("mix_done")
        expo_ready = s.sem("expo_ready")
        mix_ready = s.sem("mix_ready")
        extra_done = s.sem("extra_done")
        mix_whole = s.sem("mix_whole")
        passed = s.sem("passed")
        queries_ready = s.sem("queries_ready")

        expo_ps = [gu[1], gu[0]]
        rank_ps = [gu[2], turn]

        def mlp_groups(eng, body):
            body(0)
            with eng.Fori(1, UM // SLOTS - 1) as g:
                body(g)
            body(UM // SLOTS - 1)

        def units_ahead(b, g, m, last):
            i = g * SLOTS + m + AHEAD
            slot = (m + AHEAD) % SLOTS
            if isinstance(i, int) and i >= U:
                return None if last else ((b + 1) * U + i - U, slot, WM)
            return b * U + i, slot, WE if isinstance(i, int) and i >= UM else WM

        with s.block() as block:

            @block.sync
            def _(sp):
                for dst, src in ((wq_raw, "w_ret"), (keys, "keys"), (iota, "iota"), (ysteps, "ysteps"),
                                 (select_raw, "select")):
                    sp.dma_start(dst[:], a[src]).then_inc(small_in, 16)

                def of_block(b, last):
                    def of_group(g):
                        for m in range(SLOTS):
                            sp.wait_ge(raw_free, b * U + g * SLOTS + m + 1)
                            sp.dma_start(raw[:, m % 2, :], a["w_mlp"][g * SLOTS + m]).then_inc(raw_loaded[m % 2], 16)
                    mlp_groups(sp, of_group)
                    for e in range(UE):
                        sp.wait_ge(raw_free, b * U + UM + e + 1)
                        sp.dma_start(raw[:, e % 2, 0:WE], a["w_exp"][e]).then_inc(raw_loaded[e % 2], 16)
                token_blocks(sp, of_block)

            @block.gpsimd
            def _(pool):
                ln.pool_rstd(pool)

            @block.scalar
            def _(act):
                act.sem_inc(silu_ready, START)
                act.sem_inc(route_done, 1)
                act.wait_ge(small_in, 80)
                nc.scalar.activation(wq[:, 0], wq_raw[:], ACT.Copy).then_inc(q_high, 1)
                nc.scalar.activation(select[:], select_raw[:], ACT.Copy).then_inc(q_high, 1)
                ln.act_high(act, 0)
                for m in range(AHEAD):
                    act.wait_ge(raw_loaded[m % 2], 16 * (m // 2 + 1))
                    nc.scalar.activation(w[:, m, 0, :], raw[:, m % 2, :], ACT.Copy).then_inc(w_high, 1)

                def of_query(b):
                    for half in range(2):
                        act.wait_ge(q_done, b * 2 + half + 1)
                        nc.scalar.activation(query[:, bass.ds(b * BLK, BLK), half], gu[half][0:RD, :],
                                             ACT.Copy).then_inc(query_ready, 1)
                    ln.act_high(act, b + 1)
                with act.Fori(0, NBLK) as b:
                    of_query(b)

                def of_block(b, last):
                    def of_unit(g, m):
                        n = b * U + g * SLOTS + m
                        act.wait_ge(g_done, n + 1)
                        act.wait_ge(hid_step, START + n - 1)
                        nc.scalar.activation(act_out[:, m % 2, :], gu[0][:], ACT.Silu).then_inc(silu_ready, 1)
                        unit = units_ahead(b, g, m, last)
                        if unit is not None:
                            nn, slot, cols = unit
                            par = slot % 2
                            base = b * (U // 2) + g * (SLOTS // 2) + (m + AHEAD) // 2 + 1
                            act.wait_ge(raw_loaded[par], base * 16)
                            act.wait_ge(unit_used, nn + 1)
                            nc.scalar.activation(w[:, slot, 0, 0:cols], raw[:, par, 0:cols], ACT.Copy).then_inc(w_high, 1)

                    def of_group(g):
                        for m in range(SLOTS):
                            of_unit(g, m)

                    def of_mlp_group(g):
                        act.wait_ge(route_done, b * BT + g + 1)
                        flat = query[:].rearrange("p t s -> p (t s)").rearrange("p (i n) -> p i n", i=2)
                        nc.scalar.activation(tile_query[:], flat[:, :, bass.ds((b * BT + g) * P, P)],
                                             ACT.Copy).then_inc(queries_ready, 1)
                        of_group(g)
                    mlp_groups(act, of_mlp_group)
                    act.wait_ge(pair_in, b + 1)
                    nc.scalar.activation(pair_exp[:], pair[:].rearrange("p t x y -> p t (x y)"),
                                         ACT.Exp).then_inc(pair_exp_ready, 1)
                    act.wait_ge(rows_turned, b * 2 + 1)
                    nc.scalar.activation(rowsT[:, 0], turn[0:ROWS, :], ACT.Copy).then_inc(rows_high, 1)
                    act.wait_ge(rows_turned, b * 2 + 2)
                    nc.scalar.activation(rankT[:], gu[2][0:ROWS, :], ACT.Copy).then_inc(rank_ready, 1)
                    for e in range(UE):
                        act.wait_ge(mix_done, b * UE + e + 1)
                        if e >= 2:
                            act.wait_ge(mix_ready, b * UE + e - 1)
                        nc.scalar.activation(expo[:, e % 2, :], expo_ps[e % 2][:], ACT.Exp).then_inc(expo_ready, 1)
                    for g in range(UM // SLOTS, U // SLOTS):
                        of_group(g)
                    if not last:
                        ln.act_high(act, NBLK + 1 + b)
                token_blocks(act, of_block)

            @block.vector
            def _(dve):
                dve.sem_inc(hid_step, START)
                dve.sem_inc(raw_free, 2)
                dve.memset(rows[:], 0.0).then_inc(q_split, 1)
                ln.dve_scale(dve, 0, 0, first=True)
                dve.wait_ge(q_high, 1)
                dve.tensor_tensor(wq[:, 1], wq_raw[:], wq[:, 0].bitcast(F32), ALU.subtract).then_inc(q_split, 1)
                ln.dve_low(dve, 0)

                def split_low(n, slot, cols):
                    dve.wait_ge(w_high, n + 1)
                    dve.tensor_tensor(w[:, slot, 1, 0:cols], raw[:, slot % 2, 0:cols], w[:, slot, 0, 0:cols].bitcast(F32),
                                      ALU.subtract).then_inc(w_ready, 1)
                    dve.wait_ge(w_ready, n + 1)
                    dve.sem_inc(raw_free, 1)

                for m in range(AHEAD):
                    split_low(m, m, WM)
                with dve.Fori(0, NBLK - 1) as b:
                    ln.dve_scale(dve, b + 1, b + 1)
                    ln.dve_low(dve, b + 1)
                ln.dve_scale(dve, NBLK, 0)
                ln.dve_low(dve, NBLK)

                def last_steps(b):
                    step = [0]

                    def chain(ins):
                        step[0] += 1
                        ins.then_inc(block_step, 1)
                        dve.wait_ge(block_step, b * BSTEPS + step[0])

                    dve.wait_ge(pair_exp_ready, b + 1)
                    e4 = pair_exp[:].rearrange("p t (x y) -> p t x y", x=TOP)
                    chain(dve.tensor_tensor(pair_exp[:].rearrange("p t q -> p (t q)"), pair_exp[:].rearrange("p t q -> p (t q)"),
                                            chosen[:].rearrange("p t x y -> p (t x y)"), ALU.mult))
                    chain(dve.tensor_reduce(row_sum[:], e4, AX.X, ALU.add))
                    chain(dve.tensor_reduce(inv_total[:], row_sum[:], AX.X, ALU.add))
                    chain(dve.reciprocal(inv_total[:], inv_total[:]))
                    chain(dve.tensor_scalar(clamped[:], best_pos[:, :, 0, :], XK - 0.5, None, ALU.is_gt))
                    chain(dve.tensor_tensor(clamped[:], clamped[:], row_sum[:], ALU.mult))
                    dve.tensor_reduce(rows[:, :, 0, ROWS - 1], clamped[:], AX.X, ALU.add).then_inc(rows_ready, 1)

                def route_part(b, g, m):
                    base = (b * BT + g) * TSTEPS
                    step = [(0, 4, 10, 13)[m]]

                    def chain(ins, wait=True):
                        step[0] += 1
                        ins.then_inc(route_step, 1)
                        if wait:
                            dve.wait_ge(route_step, base + step[0])

                    def alone():
                        dve.sem_inc(passed, 1)

                    t = bass.ds(g, 1) if not isinstance(g, int) else slice(g, g + 1)

                    def tile(x, pattern):
                        return x.rearrange(pattern)
                    if m == 0:
                        dve.wait_ge(route_done, b * BT + g + 2)
                        chain(dve.tensor_copy(route[:].rearrange("p s k -> p (s k)"), gu[2][:, 0:2 * KEYS]))
                        alone()
                        for i in range(2):
                            chain(dve.max(best[:, i, :], route[:, i, :]), wait=i == 1)
                        alone()
                        chain(dve.max_index(best_at[:, 0, :], best[:, 0, :], route[:, 0, :]))
                    if m == 1:
                        alone()
                        chain(dve.max_index(best_at[:, 1, :], best[:, 1, :], route[:, 1, :]))
                        chain(dve.tensor_copy(tile(best_pos[:, t], "p o s k -> p (o s k)"), best_at[:].rearrange("p s k -> p (s k)")), wait=False)
                        chain(dve.tensor_tensor(pair_now[:],
                                                best[:, 0, :].rearrange("p (k o) -> p k o", o=1).broadcast_to([P, TOP, TOP]),
                                                best[:, 1, :].rearrange("p (o k) -> p o k", o=1).broadcast_to([P, TOP, TOP]), ALU.add))
                        flat = pair_now[:].rearrange("p x y -> p (x y)")
                        alone()
                        chain(dve.max(pair_best[:], flat))
                        alone()
                        chain(dve.match_replace(marked[:].rearrange("p x y -> p (x y)"), pair_best[:], flat, -3.0e38))
                        chain(dve.tensor_tensor(tile(chosen[:, t], "p o x y -> p (o x y)"), marked[:].rearrange("p x y -> p (x y)"),
                                                flat, ALU.not_equal))
                    if m == 2:
                        chain(dve.tensor_reduce(count[:], tile(chosen[:, t], "p o x y -> p (o x) y"), AX.X, ALU.add), wait=False)
                        chain(dve.tensor_tensor(hit[:, :, 0:XK], iota[:, 0:XK].rearrange("p (o k) -> p o k", o=1).broadcast_to([P, TOP, XK]),
                                                tile(best_pos[:, t, 0, :], "p o k -> p k o").broadcast_to([P, TOP, XK]), ALU.is_equal))
                        chain(dve.tensor_tensor(hit[:, :, 0:XK], hit[:, :, 0:XK],
                                                count[:].rearrange("p (k o) -> p k o", o=1).broadcast_to([P, TOP, XK]), ALU.mult))
                        dve.tensor_reduce(tile(rows[:, t, 1, KEYS:KEYS + XK], "p o k -> p (o k)"),
                                          hit[:, :, 0:XK].rearrange("p k x -> p x k"), AX.X, ALU.add)
                        for i, (c0, n) in enumerate(((KEYS, XK), (0, KEYS))):
                            dve.tensor_scalar(tile(rows[:, t, 0, c0:c0 + n], "p o k -> p (o k)"), route[:, i, 0:n],
                                              best[:, i, 0:1], None, ALU.subtract)
                    if m == 3:
                        chain(dve.tensor_tensor(hit[:], iota[:].rearrange("p (o k) -> p o k", o=1).broadcast_to([P, TOP, KEYS]),
                                                tile(best_pos[:, t, 1, :], "p o k -> p k o").broadcast_to([P, TOP, KEYS]), ALU.is_equal))
                        chain(dve.tensor_tensor(hit[:], hit[:], ysteps[:].rearrange("p (k o) -> p k o", o=1).broadcast_to([P, TOP, KEYS]),
                                                ALU.mult))
                        dve.tensor_reduce(tile(rows[:, t, 1, 0:KEYS], "p o k -> p (o k)"), hit[:].rearrange("p k y -> p y k"), AX.X,
                                          ALU.add)
                        chain(dve.tensor_scalar(tile(pair[:, t], "p o x y -> p (o x y)"), pair_now[:].rearrange("p x y -> p (x y)"),
                                                pair_best[:, 0:1], None, ALU.subtract))

                def of_block(b, last):
                    def of_unit(g, m, mlp):
                        n = b * U + g * SLOTS + m
                        dve.wait_ge(silu_ready, START + n + 1)
                        if mlp:
                            dve.wait_ge(u_done, b * UM + g * SLOTS + m + 1)
                        dve.wait_ge(hid_ready, START + n)
                        other = gu[1][:] if mlp else mix[:, g * SLOTS + m - UM, :]
                        dve.tensor_tensor(hid[:], act_out[:, m % 2, :], other, ALU.mult).then_inc(hid_step, 1)
                        dve.wait_ge(hid_step, START + n + 1)
                        dve.wait_ge(unit_used, SLOTS + n - 1)
                        dve.tensor_copy(hidT[:, m % 2, 0], hid[:]).then_inc(hid_high, 1)
                        dve.wait_ge(hid_high, n + 1)
                        dve.tensor_tensor(hidT[:, m % 2, 1], hid[:], hidT[:, m % 2, 0].bitcast(F32),
                                          ALU.subtract).then_inc(hid_ready, 1)
                        unit = units_ahead(b, g, m, last)
                        if unit is not None:
                            split_low(*unit)

                    def of_group(g):
                        for m in range(SLOTS):
                            of_unit(g, m, True)
                            route_part(b, g, m)
                            if m == SLOTS - 1 and isinstance(g, int) and g == 0 and not last:
                                ln.dve_scale(dve, NBLK + 1 + b, b + 1)
                    mlp_groups(dve, of_group)
                    dve.wait_ge(route_step, (b + 1) * BT * TSTEPS)
                    dve.sem_inc(pair_in, 1)
                    last_steps(b)
                    for t in range(BT):
                        if t < BT - 1:
                            dve.wait_ge(out_done, b * 2 * (BT - 1) + t + 1)
                        else:
                            dve.wait_ge(unit_used, SLOTS + b * U + UM)
                        dve.tensor_tensor(h[:, b * BT + t, :], h[:, b * BT + t, :], out_ps[t][:],
                                          ALU.add).then_inc(out_free, 1)
                    dve.wait_ge(rows_high, b + 1)
                    dve.tensor_tensor(rowsT[:, 1], turn[0:ROWS, :], rowsT[:, 0].bitcast(F32), ALU.subtract).then_inc(rows_low, 1)
                    for e in range(UE):
                        dve.wait_ge(expo_ready, b * UE + e + 1)
                        dve.scalar_tensor_tensor(out=mix[:, e, :], in0=rank_ps[e % 2][:], scalar=TOP + 0.5, in1=expo[:, e % 2, :],
                                                 op0=ALU.is_gt, op1=ALU.mult).then_inc(mix_ready, 1)
                    dve.wait_ge(extra_done, b + 1)
                    dve.wait_ge(mix_ready, (b + 1) * UE)
                    dve.tensor_tensor(mix[:, UE - 1, :], mix[:, UE - 1, :], gu[1][:], ALU.add).then_inc(mix_whole, 1)
                    dve.wait_ge(mix_whole, b + 1)
                    for g in range(UM // SLOTS, U // SLOTS):
                        for m in range(SLOTS):
                            of_unit(g, m, False)
                    if not last:
                        ln.dve_low(dve, NBLK + 1 + b)
                    for t in range(BT):
                        if t < BT - 1:
                            dve.wait_ge(out_done, (b * 2 + 1) * (BT - 1) + t + 1)
                        else:
                            dve.wait_ge(unit_used, SLOTS + (b + 1) * U)
                        dve.wait_ge(out_free, BT + b * 2 * BT + t + 1)
                        dve.scalar_tensor_tensor(out=h[:, b * BT + t, :], in0=out_ps[t][:], scalar=inv_total[:, t:t + 1],
                                                 in1=h[:, b * BT + t, :], op0=ALU.mult, op1=ALU.add).then_inc(out_free, 1)
                token_blocks(dve, of_block)

            @block.tensor
            def _(pe):
                pe.sem_inc(unit_used, SLOTS)
                pe.sem_inc(hid_ready, START)
                pe.sem_inc(out_free, BT)
                ln.pe_turn(pe, 0, first=True)
                pe.wait_ge(q_split, 2)
                pe.wait_ge(q_high, 2)
                with pe.Fori(0, NBLK) as b:
                    pe.wait_ge(ln.xT_ready, (b + 1) * DC)
                    for half in range(2):
                        for k in range(DC):
                            ins = product(pe, gu[half][0:RD, :], [wq[:, i, k * P + half * RD:k * P + half * RD + RD] for i in range(2)],
                                          [ln.xT[:, i, k, :] for i in range(2)], k == 0, k == DC - 1)
                        ins.then_inc(q_done, 1)
                    ln.pe_turn(pe, b + 1)
                    pe.wait_ge(query_ready, (b + 1) * 2)

                def of_block(b, last):
                    pe.wait_ge(ln.xT_ready, (NBLK + 1 + b) * DC)

                    def first_product(g, m, mlp):
                        n = b * U + g * SLOTS + m
                        pe.wait_ge(w_ready, n + 1)
                        pe.wait_ge(silu_ready, START + n)
                        for k in range(DC):
                            ins = product(pe, gu[0][:], [w[:, m, i, k * P:(k + 1) * P] for i in range(2)],
                                          [ln.xT[:, i, k, :] for i in range(2)], k == 0, k == DC - 1)
                        ins.then_inc(g_done, 1)
                        if mlp:
                            pe.wait_ge(hid_step, START + n)
                            for k in range(DC):
                                ins = product(pe, gu[1][:], [w[:, m, i, (DC + k) * P:(DC + k + 1) * P] for i in range(2)],
                                              [ln.xT[:, i, k, :] for i in range(2)], k == 0, k == DC - 1)
                            ins.then_inc(u_done, 1)

                    def second_product(g, m, mlp, start, stop):
                        n = b * U + g * SLOTS + m
                        pe.wait_ge(hid_ready, START + n + 1)
                        c0 = 2 * DC * P if mlp else DC * P
                        for t in range(BT):
                            if start:
                                pe.wait_ge(out_free, (b * 2 + (0 if mlp else 1)) * BT + t + 1)
                            ins = product(pe, out_ps[t][:], [hidT[:, m % 2, i, t * P:(t + 1) * P] for i in range(2)],
                                          [w[:, m, i, c0:c0 + D] for i in range(2)], start, stop)
                            if t == BT - 1:
                                ins.then_inc(unit_used, 1)
                            elif stop:
                                ins.then_inc(out_done, 1)

                    def of_group(g):
                        if not isinstance(g, int) or g:
                            pe.wait_ge(route_step, (b * BT + g) * TSTEPS - TSTEPS + 1)
                        pe.wait_ge(queries_ready, b * BT + g + 1)
                        for i in range(2):
                            ins = pe.matmul(gu[2][:, i * KEYS:(i + 1) * KEYS], tile_query[:, i, :], keys[:, i, :],
                                            start=True, stop=True)
                        ins.then_inc(route_done, 1)
                        for m in range(SLOTS):
                            first_product(g, m, True)
                            if m:
                                second_product(g, m - 1, True, isinstance(g, int) and g == 0 and m == 1, False)
                            elif not (isinstance(g, int) and g == 0):
                                second_product(g - 1, SLOTS - 1, True, False, False)
                    mlp_groups(pe, of_group)
                    second_product(UM // SLOTS - 1, SLOTS - 1, True, False, True)

                    pe.wait_ge(rows_ready, b + 1)
                    for i, out in enumerate((turn, gu[2])):
                        for t in range(BT):
                            ins = pe.transpose(out[0:ROWS, t * P:(t + 1) * P], rows[:, t, i, :], ident[:])
                        ins.then_inc(rows_turned, 1)
                    pe.wait_ge(rows_low, b + 1)
                    pe.wait_ge(rank_ready, b + 1)
                    pe.wait_ge(silu_ready, START + b * U + UM)
                    for e in range(UE):
                        if e >= 2:
                            pe.wait_ge(expo_ready, b * UE + e - 1)
                            pe.wait_ge(mix_ready, b * UE + e - 1)
                        lhs = select[:, e * P:(e + 1) * P]
                        for i in range(2):
                            pe.matmul(expo_ps[e % 2][:], lhs, rowsT[:, i], start=i == 0, stop=i == 1)
                        pe.matmul(rank_ps[e % 2][:], lhs, rankT[:], start=True, stop=True).then_inc(mix_done, 1)
                    pe.wait_ge(expo_ready, b * UE + UE)
                    pe.wait_ge(mix_ready, b * UE + UE)
                    for i in range(2):
                        ins = pe.matmul(gu[1][:], select[:, EXP:EXP + P], rowsT[:, i], start=i == 0, stop=i == 1)
                    ins.then_inc(extra_done, 1)

                    for g in range(UM // SLOTS, U // SLOTS):
                        for m in range(SLOTS):
                            first_product(g, m, False)
                            if (g, m) != (UM // SLOTS, 0):
                                pg, pm = (g, m - 1) if m else (g - 1, SLOTS - 1)
                                second_product(pg, pm, False, (pg, pm) == (UM // SLOTS, 0), False)
                    if not last:
                        ln.pe_turn(pe, NBLK + 1 + b)
                    second_product(U // SLOTS - 1, SLOTS - 1, False, False, True)
                    pe.wait_ge(mix_whole, b + 1)
                token_blocks(pe, of_block)


def rotary_attention_stage(nc, h, ident, a):
    HD, KV = 64, 8
    CAP, SCALE = 50.0, 256.0 ** -0.5
    UNITS = 16
    PAIR = 2
    DENSE = 3
    MM = BT + DC * DENSE + BT
    PARTS = 2 * BT
    WQ, WK, WV, WO = 0, 2, 3, 4
    SLOTS = 2
    PE_AT = {4 * c - 2 + i: [(c + 1, i)] for c in range(DC - 1) for i in range(DENSE)}
    ACT_AT = {**{u: x for u, x in PE_AT.items() if u > 0}, 1: [(1, 2)]}
    DVE_AT = {**{u + 1: x for u, x in PE_AT.items() if u > 0}, 1: [(1, 0), (1, 1)], 2: [(1, 2)]}
    START = 2
    with Stage(nc, "at1") as s:
        mm = [s.ps(f"mm{i}", [P, BLK]) for i in range(2)]
        score = [s.ps(f"score{i}", [P, PAIR, 2, P]) for i in range(4)]
        spare = [s.ps(f"spare{i}", [P, BLK]) for i in range(2)]
        o_ps = [x[:, 0:PAIR * 2 * (HD + 1)].rearrange("p (t i d) -> p t i d", t=PAIR, i=2) for x in spare]
        ln = Norm(s, nc, h, ident, mm[0])
        w = Resident(s, nc, 6, 2)
        cos = s.sb("cos", [P, CLIP])
        sin = s.sb("sin", [P, CLIP])
        mask = s.sb("mask", [P, P])
        qT = s.sb("qT", [P, 2, 2, BLK])
        kT = s.sb("kT", [P, 2, BLK])
        swapped = s.sb("swapped", [P, 2, BLK])
        v = s.sb("v", [P, BT, KV, HD + 1])
        probT = s.sb("probT", [P, SLOTS, PAIR, 2, P])
        inv_sum = s.sb("inv_sum", [P, 2, PAIR, 2])
        o = w.raw[:].rearrange("p a (b n) -> p (a b) n", b=2)
        oT = s.sb("oT", [P, 2, 2, DC, P], F32R)

        small_in = s.sem("small_in")
        ones_ready = s.sem("ones_ready")
        mm_done = s.sem("mm_done")
        mm_taken = [s.sem(f"mm_taken{i}") for i in range(2)]
        swap_loaded = [s.sem(f"swap_loaded{i}") for i in range(2)]
        rope_step = s.sem("rope_step")
        rope_ready = s.sem("rope_ready")
        score_done = s.sem("score_done")
        tanh_ready = s.sem("tanh_ready")
        exp_ready = s.sem("exp_ready")
        probT_ready = s.sem("probT_ready")
        o_done = s.sem("o_done")
        inv_ready = s.sem("inv_ready")
        o_ready = s.sem("o_ready")
        o_turned = s.sem("o_turned")
        oT_high = s.sem("oT_high")
        oT_ready = s.sem("oT_ready")
        part_half = s.sem("part_half")
        passed = s.sem("passed")

        def task(c, i):
            return (BT if c else 0) + c * DENSE + i

        def where(c, i):
            return kT[:, c % 2, :] if i == 0 else qT[:, c % 2, i - 1, :]

        with s.block() as block:

            @block.sync
            def _(sp):
                for dst, src in ((cos, "cos"), (sin, "sin"), (mask, "maskT")):
                    sp.dma_start(dst[:], a[src]).then_inc(small_in, 16)
                w.load(sp, a["w_at1"])

                def of_block(b, last):
                    for c in range(DC):
                        for i in range(DENSE):
                            j, d = task(c, i), c * DENSE + i
                            sp.wait_ge(mm_taken[j % 2], b * (MM // 2) + j // 2 + 2)
                            sp.sem_inc(passed, 1)
                            sp.wait_ge(rope_ready, START + b * DC * DENSE + d - 1)
                            for r in range(4):
                                src = slice((r ^ 1) * 32, (r ^ 1) * 32 + 32)
                                sp.dma_start(swapped[r * 32:r * 32 + 32, d % 2, :],
                                             where(c, i)[src]).then_inc(swap_loaded[d % 2], 16)
                token_blocks(sp, of_block)

            @block.gpsimd
            def _(pool):
                ln.pool_start(pool)
                ln.pool_rstd_block(pool, 0, first=True)
                w.split_late(pool)
                for b in range(1, NBLK):
                    ln.pool_rstd_block(pool, b)

            @block.scalar
            def _(act):
                w.split_high(act, range(2))
                ln.act_high(act, 0)
                w.split_high(act, range(2, w.early))

                def of_block(b, last):
                    def take(c, i):
                        j = task(c, i)
                        act.wait_ge(mm_done, b * MM + j + 1)
                        if c >= 2:
                            act.wait_ge(score_done, b * UNITS + (c - 1) * 4)
                        nc.scalar.activation(where(c, i), mm[j % 2][:], ACT.Copy).then_inc(mm_taken[j % 2], 1)

                    for i in range(DENSE):
                        take(0, i)
                    act.wait_ge(ones_ready, 1)
                    for t in range(BT):
                        j = DENSE + t
                        act.wait_ge(mm_done, b * MM + j + 1)
                        nc.scalar.activation(v[:, t, :, 0:HD], mm[j % 2][:].rearrange("p (j d) -> p j d", j=KV),
                                             ACT.Copy).then_inc(mm_taken[j % 2], 1)
                    take(1, 0)
                    take(1, 1)
                    for u in range(UNITS):
                        n = b * UNITS + u
                        act.wait_ge(score_done, n + 1)
                        if u >= SLOTS:
                            act.wait_ge(o_done, n - SLOTS + 1)
                        bank = score[2 * (u % 4 // 2) + u % 2]
                        nc.scalar.activation(probT[:, u % SLOTS], bank[:], ACT.Tanh, scale=SCALE / CAP).then_inc(tanh_ready, 1)
                        act.wait_ge(tanh_ready, n + 1)
                        nc.scalar.activation(probT[:, u % SLOTS], probT[:, u % SLOTS], ACT.Exp, scale=CAP).then_inc(exp_ready, 1)
                        for c, i in ACT_AT.get(u, ()):
                            take(c, i)
                        if u >= UNITS - 4 and not last:
                            ln.act_high_chunk(act, b + 1, u - UNITS + 4)
                    for i in range(PARTS):
                        act.wait_ge(o_turned, b * PARTS + i + 1)
                        if i >= 2:
                            if i % 2 == 0:
                                act.wait_ge(part_half, b * BT + i // 2)
                            else:
                                act.wait_ge(mm_done, b * MM + MM - BT + i // 2)
                        nc.scalar.activation(oT[:, i % 2, 0], spare[i % 2][:].rearrange("p (c q) -> p c q", c=DC),
                                             ACT.Copy).then_inc(oT_high, 1)
                token_blocks(act, of_block)

            @block.vector
            def _(dve):
                dve.sem_inc(rope_ready, START)
                dve.memset(v[:, :, :, HD:], 1.0).then_inc(ones_ready, 1)
                ln.dve_scale(dve, 0, 0, first=True)
                w.split_low(dve, range(2))
                ln.dve_low(dve, 0)
                w.split_low(dve, range(2, w.early))
                dve.wait_ge(small_in, 48)

                def of_block(b, last):
                    def rope(c, i):
                        d = c * DENSE + i
                        n = b * DC * DENSE + d
                        dve.wait_ge(swap_loaded[d % 2], (b * (DC * DENSE // 2) + d // 2 + 1) * 64)
                        clips = BLK // CLIP
                        x = where(c, i).rearrange("p (n t) -> p n t", n=clips)
                        y = swapped[:, d % 2, :].rearrange("p (n t) -> p n t", n=clips)
                        table = [z[:].rearrange("p (o t) -> p o t", o=1).broadcast_to([P, clips, CLIP]) for z in (cos, sin)]
                        dve.tensor_tensor(x, x, table[0], ALU.mult).then_inc(rope_step, 1)
                        dve.tensor_tensor(y, y, table[1], ALU.mult).then_inc(rope_step, 1)
                        dve.wait_ge(rope_step, n * 2 + 2)
                        dve.tensor_tensor(x, x, y, ALU.add).then_inc(rope_ready, 1)

                    for i in range(DENSE):
                        rope(0, i)

                    dve.wait_ge(w.late_ready, 2)

                    def take_o(u):
                        n = b * UNITS + u
                        t0 = u % 2 * PAIR
                        c0 = u // 2 * P
                        dve.wait_ge(o_done, n + 1)
                        dve.reciprocal(inv_sum[:, u % 2], o_ps[u % 2][:, :, :, HD]).then_inc(inv_ready, 1)
                        dve.wait_ge(inv_ready, n + 1)
                        dve.tensor_tensor(o[:, t0:t0 + PAIR, c0:c0 + P].rearrange("p t (i d) -> p t i d", i=2),
                                          o_ps[u % 2][:, :, :, 0:HD],
                                          inv_sum[:, u % 2].rearrange("p t (i o) -> p t i o", o=1).broadcast_to([P, PAIR, 2, HD]),
                                          ALU.mult).then_inc(o_ready, 1)

                    for u in range(UNITS):
                        n = b * UNITS + u
                        dve.wait_ge(exp_ready, n + 1)
                        dve.tensor_tensor(probT[:, u % SLOTS].rearrange("p t i q -> p (t i) q"),
                                          probT[:, u % SLOTS].rearrange("p t i q -> p (t i) q"),
                                          mask[:].rearrange("p (o q) -> p o q", o=1).broadcast_to([P, PAIR * 2, P]),
                                          ALU.mult).then_inc(probT_ready, 1)
                        if u:
                            take_o(u - 1)
                        for c, i in DVE_AT.get(u, ()):
                            rope(c, i)
                        if u == 3 and not last:
                            ln.dve_scale(dve, b + 1, b + 1)
                        if u >= UNITS - 4 and not last:
                            ln.dve_low_chunk(dve, b + 1, u - UNITS + 4)
                    take_o(UNITS - 1)

                    def low(i):
                        dve.wait_ge(oT_high, b * PARTS + i + 1)
                        dve.tensor_tensor(oT[:, i % 2, 1], spare[i % 2][:].rearrange("p (c q) -> p c q", c=DC),
                                          oT[:, i % 2, 0].bitcast(F32), ALU.subtract).then_inc(oT_ready, 1)

                    def add(t):
                        j = MM - BT + t
                        dve.wait_ge(mm_done, b * MM + j + 1)
                        dve.tensor_tensor(h[:, b * BT + t, :], h[:, b * BT + t, :], mm[j % 2][:],
                                          ALU.add).then_inc(mm_taken[j % 2], 1)
                    for i in range(PARTS):
                        low(i)
                        if i >= 3 and i % 2:
                            add(i // 2 - 1)
                    add(BT - 1)
                token_blocks(dve, of_block)

            @block.tensor
            def _(pe):
                pe.sem_inc(mm_taken[0], 1)
                pe.sem_inc(mm_taken[1], 1)
                ln.pe_turn(pe, 0, first=True)
                pe.wait_ge(w.ready, w.early)

                def of_block(b, last):
                    pe.wait_ge(ln.xT_ready, b * DC + DC)

                    def take_mm(j):
                        pe.wait_ge(mm_taken[j % 2], b * (MM // 2) + j // 2 + 1)
                        return mm[j % 2][:]

                    def dense(c, i):
                        out = take_mm(task(c, i))
                        piece, col = (WK, c * P) if i == 0 else (WQ + (2 * c + i - 1) // DC, (2 * c + i - 1) % DC * P)
                        for k in range(DC):
                            ins = product(pe, out, w.pair(piece, k, col, col + P),
                                          [ln.xT[:, x, k, :] for x in range(2)], k == 0, k == DC - 1)
                        ins.then_inc(mm_done, 1)

                    for i in range(DENSE):
                        dense(0, i)
                    for t in range(BT):
                        out = take_mm(DENSE + t)
                        for k in range(DC):
                            ins = product(pe, out, [ln.xT[:, x, k, t * P:(t + 1) * P] for x in range(2)],
                                          w.pair(WV, k, 0, D), k == 0, k == DC - 1)
                        ins.then_inc(mm_done, 1)

                    def scores(u):
                        n = b * UNITS + u
                        c, r, t0 = u // 4, u % 4 // 2, u % 2 * PAIR
                        if u % 4 == 0:
                            pe.wait_ge(rope_ready, START + b * DC * DENSE + (c + 1) * DENSE)
                        if u >= 4:
                            pe.wait_ge(tanh_ready, n - 3)
                        rows = slice(r * HD, (r + 1) * HD)
                        for t in range(PAIR):
                            cols = slice((t0 + t) * P, (t0 + t + 1) * P)
                            ins = pe.matmul(score[2 * r + u % 2][:, t, :, :], kT[rows, c % 2, cols], qT[rows, c % 2, :, cols],
                                            start=True, stop=True)
                        ins.then_inc(score_done, 1)

                    def heads(u):
                        n = b * UNITS + u
                        t0 = u % 2 * PAIR
                        if u == 0:
                            for j in (DENSE + BT - 2, DENSE + BT - 1):
                                pe.wait_ge(mm_taken[j % 2], b * (MM // 2) + j // 2 + 2)
                        pe.wait_ge(probT_ready, n + 1)
                        if u >= 2:
                            pe.wait_ge(o_ready, n - 1)
                        for t in range(PAIR):
                            for i in range(2):
                                ins = pe.matmul(o_ps[u % 2][:, t, i, :], probT[:, u % SLOTS, t, i, :], v[:, t0 + t, u // 2, :],
                                                start=True, stop=True)
                        ins.then_inc(o_done, 1)

                    for u in range(-2, UNITS + 1):
                        if u == 0:
                            scores(0)
                            scores(1)
                        if u >= 1:
                            heads(u - 1)
                        for c, i in PE_AT.get(u, ()):
                            dense(c, i)
                        if UNITS - 4 <= u < UNITS and not last:
                            if u == UNITS - 4:
                                pe.wait_ge(mm_taken[0], b * (MM // 2) + (MM - BT) // 2 + 1)
                            ln.pe_turn_chunk(pe, b + 1, u - UNITS + 4)
                        if 0 <= u < UNITS - 2:
                            scores(u + 2)

                    def turn_part(i):
                        t, half = i // 2, i % 2
                        if i == 0:
                            pe.wait_ge(o_ready, (b + 1) * UNITS)
                        if i >= 2:
                            pe.wait_ge(oT_ready, b * PARTS + i - 1)
                        for c in range(DC):
                            col = (half * DC + c) * P
                            ins = pe.transpose(spare[i % 2][:, c * P:(c + 1) * P], o[:, t, col:col + P], ident[:])
                        ins.then_inc(o_turned, 1)

                    def project(i):
                        t, half = i // 2, i % 2
                        j = MM - BT + t
                        if half == 0:
                            take_mm(j)
                        pe.wait_ge(oT_ready, b * PARTS + i + 1)
                        for c in range(DC):
                            ins = product(pe, mm[j % 2][:], [oT[:, i % 2, x, c, :] for x in range(2)],
                                          w.pair(WO + half, c, 0, D), i % 2 == 0 and c == 0, i % 2 == 1 and c == DC - 1)
                        ins.then_inc(mm_done if half else part_half, 1)

                    turn_part(0)
                    turn_part(1)
                    pe.wait_ge(w.late_ready, 2)
                    if not last:
                        pe.wait_ge(ln.xT_ready, (b + 2) * DC)
                    for i in range(PARTS):
                        project(i)
                        if i + 2 < PARTS:
                            turn_part(i + 2)
                token_blocks(pe, of_block)


def ternary_mlp_stage(nc, h, ident, a, out):
    INNER = 1408
    FC = INNER // P
    COLS = FC * D
    W1, W2, W3 = range(3)
    PARTS = 4
    CUT = [FC * i // PARTS for i in range(PARTS + 1)]
    with Stage(nc, "ter") as s:
        turn = [s.ps(f"turn{i}", [P, BLK]) for i in range(2)]
        x1_ps = [s.ps(f"x1_{i}", [P, BLK]) for i in range(2)]
        x2_ps = [s.ps(f"x2_{i}", [P, BLK]) for i in range(2)]
        out_ps = [s.ps(f"out{i}", [P, D]) for i in range(2)]
        ln = Norm(s, nc, h, ident, turn)
        raw = s.sb("raw", [P, COLS])
        w = s.sb("w", [P, 3, COLS], F32R)
        size = s.sb("size", [P, D])
        size_sum = s.sb("size_sum", [P, 3, FC])
        size_total = s.sb("size_total", [P, 3])
        ones = s.sb("ones", [P, P])
        bound = s.sb("bound", [P, 3, 2])
        sig = s.sb("sig", [P, 2, BLK])
        hid = s.sb("hid", [P, 2, BLK])
        hidT = s.sb("hidT", [P, FC, 2, BLK], F32R)

        raw_loaded = [s.sem(f"raw_loaded{i}") for i in range(PARTS)]
        ones_ready = s.sem("ones_ready")
        size_ready = s.sem("size_ready")
        total_ready = s.sem("total_ready")
        mean_done = s.sem("mean_done")
        bound_ready = s.sem("bound_ready")
        above_ready = s.sem("above_ready")
        w_ready = s.sem("w_ready")
        x1_done = s.sem("x1_done")
        x2_done = s.sem("x2_done")
        sig_ready = s.sem("sig_ready")
        hid_step = s.sem("hid_step")
        hid_high = s.sem("hid_high")
        hid_ready = s.sem("hid_ready")
        out_done = s.sem("out_done")
        h_ready = s.sem("h_ready")
        stored = s.sem("stored")
        START = 2

        with s.block() as block:

            @block.sync
            def _(sp):
                for n in range(3):
                    for i in range(PARTS):
                        if n:
                            sp.wait_ge(w_ready, (n - 1) * PARTS + i + 1)
                        cols = slice(CUT[i] * D, CUT[i + 1] * D)
                        sp.dma_start(raw[:, cols], a["w_ter"][n][:, cols]).then_inc(raw_loaded[i], 16)
                with sp.Fori(0, TILES) as t:
                    sp.wait_ge(h_ready, START + t + 1)
                    sp.dma_start(out[t], h[:, t, :]).then_inc(stored, 16)
                sp.wait_ge(stored, TILES * 16)

            @block.gpsimd
            def _(pool):
                pool.memset(ones[:], 1.0).then_inc(ones_ready, 1)
                ln.pool_rstd(pool)

            @block.scalar
            def _(act):
                act.sem_inc(sig_ready, START)
                for n in range(3):
                    for f in range(FC):
                        if f in CUT:
                            act.wait_ge(raw_loaded[CUT.index(f)], 16 * n + 16)
                        if n or f:
                            act.wait_ge(size_ready, n * FC + f)
                        nc.scalar.activation(size[:], raw[:, f * D:(f + 1) * D], ACT.Abs,
                                             accum_out=size_sum[:, n, f:f + 1]).then_inc(size_ready, 1)
                    if n == 0:
                        ln.act_high(act, 0)

                def of_block(b, last):
                    for f in range(FC):
                        n = b * FC + f
                        act.wait_ge(x1_done, n + 1)
                        act.wait_ge(hid_step, START + n - (1 if f else 0))
                        nc.scalar.activation(sig[:, f % 2, :], x1_ps[f % 2][:], ACT.Sigmoid,
                                             scale=-1.0).then_inc(sig_ready, 1)
                    if not last:
                        ln.act_high(act, b + 1)
                token_blocks(act, of_block)

            @block.vector
            def _(dve):
                dve.sem_inc(hid_step, START)
                dve.sem_inc(h_ready, START)
                ln.dve_scale(dve, 0, 0, first=True)
                for n in range(3):
                    dve.wait_ge(size_ready, (n + 1) * FC)
                    dve.tensor_reduce(size_total[:, n:n + 1], size_sum[:, n, :], AX.X, ALU.add).then_inc(total_ready, 1)
                    if n == 0:
                        ln.dve_low(dve, 0)
                    dve.wait_ge(mean_done, n + 1)
                    for i, sign in enumerate((0.5, -0.5)):
                        dve.tensor_scalar(bound[:, n, i:i + 1], out_ps[0][:, 0:1], sign / (INNER * D), sign * 1e-8,
                                          ALU.mult, ALU.add).then_inc(bound_ready, 1)
                    dve.wait_ge(bound_ready, 2 * n + 2)
                    for i in range(PARTS):
                        cols = slice(CUT[i] * D, CUT[i + 1] * D)
                        dve.tensor_scalar(w[:, n, cols], raw[:, cols], bound[:, n, 0:1], None, ALU.is_gt).then_inc(above_ready, 1)
                        dve.wait_ge(above_ready, n * PARTS + i + 1)
                        dve.scalar_tensor_tensor(out=w[:, n, cols], in0=raw[:, cols], scalar=bound[:, n, 1:2],
                                                 in1=w[:, n, cols].bitcast(F32), op0=ALU.is_lt,
                                                 op1=ALU.subtract).then_inc(w_ready, 1)

                def of_block(b, last):
                    for f in range(FC):
                        n = b * FC + f
                        dve.wait_ge(x2_done, n + 1)
                        dve.wait_ge(sig_ready, START + n + 1)
                        dve.tensor_tensor(hid[:, f % 2, :], sig[:, f % 2, :], x2_ps[f % 2][:],
                                          ALU.mult).then_inc(hid_step, 1)
                        dve.wait_ge(hid_step, START + n + 1)
                        dve.tensor_copy(hidT[:, f, 0, :], hid[:, f % 2, :]).then_inc(hid_high, 1)
                        dve.wait_ge(hid_high, n + 1)
                        dve.tensor_tensor(hidT[:, f, 1, :], hid[:, f % 2, :], hidT[:, f, 0, :].bitcast(F32),
                                          ALU.subtract).then_inc(hid_ready, 1)
                        if f == 1 and not last:
                            ln.dve_scale(dve, b + 1, b + 1)
                    if not last:
                        ln.dve_low(dve, b + 1)
                    for t in range(BT):
                        dve.wait_ge(out_done, b * BT + t + 1)
                        dve.tensor_tensor(h[:, b * BT + t, :], h[:, b * BT + t, :], out_ps[t % 2][:],
                                          ALU.add).then_inc(h_ready, 1)
                token_blocks(dve, of_block)

            @block.tensor
            def _(pe):
                pe.sem_inc(hid_ready, START)
                pe.wait_ge(ones_ready, 1)
                ln.pe_turn(pe, 0, first=True)
                for n in range(3):
                    pe.wait_ge(total_ready, n + 1)
                    if n:
                        pe.wait_ge(bound_ready, 2 * n)
                    pe.matmul(out_ps[0][:, 0:1], ones[:], size_total[:, n:n + 1], start=True, stop=True).then_inc(mean_done, 1)

                def of_block(b, last):
                    pe.wait_ge(ln.xT_ready, b * DC + DC)
                    for f in range(FC):
                        n = b * FC + f
                        for m, bank, done in ((W1, x1_ps, x1_done), (W2, x2_ps, x2_done)):
                            pe.wait_ge(w_ready, (m + 1) * PARTS)
                            pe.wait_ge(sig_ready if m == W1 else hid_step, START + n - (1 if f else 0))
                            for k in range(DC):
                                lhs = w[:, m, (f * DC + k) * P:(f * DC + k + 1) * P]
                                for x in range(2):
                                    ins = pe.matmul(bank[f % 2][:], lhs, ln.xT[:, x, k, :], start=k == 0 and x == 0,
                                                    stop=k == DC - 1 and x == 1)
                            ins.then_inc(done, 1)
                    if not last:
                        ln.pe_turn(pe, b + 1)
                    pe.wait_ge(w_ready, 3 * PARTS)
                    pe.wait_ge(hid_ready, START + (b + 1) * FC)
                    for t in range(BT):
                        pe.wait_ge(h_ready, START + b * BT + t - 1)
                        for f in range(FC):
                            for x in range(2):
                                ins = pe.matmul(out_ps[t % 2][:], hidT[:, f, x, t * P:(t + 1) * P], w[:, W3, f * D:(f + 1) * D],
                                                start=f == 0 and x == 0, stop=f == FC - 1 and x == 1)
                        ins.then_inc(out_done, 1)
                token_blocks(pe, of_block)


def program(nc, a, out):
    with ExitStack() as ctx:
        h = ctx.enter_context(nc.sbuf_tensor("h", [P, TILES, D], F32))
        ident = ctx.enter_context(nc.sbuf_tensor("ident", [P, P], F32))
        ident_loaded = ctx.enter_context(nc.semaphore("ident_loaded"))
        with nc.Block() as block:

            @block.sync
            def _(sp):
                sp.dma_start(ident[:], a["ident"]).then_inc(ident_loaded, 16)
                sp.wait_ge(ident_loaded, 16)
        token_stage(nc, h, ident, a)
        attention_stage(nc, h, ident, a)
        memory_mlp_stage(nc, h, ident, a)
        rotary_attention_stage(nc, h, ident, a)
        ternary_mlp_stage(nc, h, ident, a, out)



def lay_token(lay, f):
    lay["x"] = f["x"].reshape(NBLK, BT, P, PACK).transpose(0, 2, 1, 3)
    lay["norm_w"] = f["L0_tok_norm_w"].reshape(PC, P).T
    lay["router"] = f["L0_tok_router_w"].reshape(EXPERTS, PC, P).transpose(2, 1, 0).reshape(P, PC * EXPERTS)
    w1 = np.concatenate([f["L0_tok_w1"], f["L0_tok_sw1"][None]])
    w2 = np.concatenate([f["L0_tok_w2"], f["L0_tok_sw2"][None]])
    w1 = w1.reshape(MLPS, HC, P, PC, P).transpose(0, 1, 4, 3, 2).reshape(MLPS * HC, P, PC * P)
    w2 = w2.reshape(MLPS, D, HC, P).transpose(0, 2, 3, 1).reshape(MLPS * HC, P, D)
    lay["w_units"] = np.concatenate([w1, w2], axis=2)
    lay["b1"] = np.concatenate([f["L0_tok_b1"], f["L0_tok_sb1"][None]]).reshape(MLPS, HC, P).transpose(2, 0, 1)
    lay["b2"] = np.concatenate([f["L0_tok_b2"], f["L0_tok_sb2"][None]])


def lay_attention(lay, f):
    def rows(w):
        return w.reshape(DC, P, -1).transpose(1, 0, 2).reshape(P, -1)
    lay["w_at0"] = np.stack([rows(f[f"L0_attn_{k}"]) for k in ("Wq", "Wk", "Wv", "Wp")])
    for k in ("bq", "bk"):
        lay[k] = f[f"L0_attn_{k}"].reshape(DC, P).T
    for k in ("bv", "bp"):
        lay[k] = f[f"L0_attn_{k}"]
    q, k = np.arange(P)[:, None], np.arange(P)[None, :]
    lay["mask"] = np.where((q // CLIP == k // CLIP) & (k <= q), 0.0, BIG).astype(np.float32)


def lay_memory_mlp(lay, f):
    DM, KEYS, XK = 512, 64, 16
    lay["w_ret"] = f["L0_ffn_W_q"].reshape(DC, P, P).transpose(1, 0, 2).reshape(P, -1)
    lay["keys"] = f["L0_ffn_keys"].transpose(1, 0, 2)

    def chunks(w):
        return w.reshape(DC, P, -1, P).transpose(2, 1, 0, 3).reshape(-1, P, DC * P)
    lay["w_mlp"] = np.concatenate([chunks(f["L0_ffn_gate_w"]), chunks(f["L0_ffn_up_w"]),
                                   f["L0_ffn_down_w"].reshape(-1, P, D)], axis=2)
    lay["w_exp"] = np.concatenate([chunks(f["L0_ffn_down_embed"].T), f["L0_ffn_up_embed"].reshape(-1, P, D)], axis=2)
    lay["iota"] = np.tile(np.arange(KEYS, dtype=np.float32), (P, 1))
    lay["ysteps"] = np.tile(np.arange(8, 0, -1, dtype=np.float32), (P, 1))
    e = np.arange(1024)
    select = np.zeros((KEYS + XK + 1, 1024 + P), np.float32)
    select[e % KEYS, e] = 1.0
    select[KEYS + e // KEYS, e] = 1.0
    select[KEYS + XK, 1024 + P - 1] = 1.0
    lay["select"] = select


def lay_rotary_attention(lay, f):
    HD, KV = 64, 8

    def rows(w):
        return w.reshape(-1, P, D).transpose(1, 0, 2).reshape(P, -1)
    order = [4 * c + i + 2 * r for c in range(4) for i in range(2) for r in range(2)]
    wq = f["L1_attn_Wq"].reshape(D, 16, HD)[:, order].reshape(D, 16 * HD)
    wo = f["L1_attn_Wo"]
    lay["w_at1"] = np.stack([rows(wq[:, :D]), rows(wq[:, D:]), rows(f["L1_attn_Wk"]), rows(f["L1_attn_Wv"]),
                             rows(wo[:D]), rows(wo[D:])])
    freq = np.float32(1.0) / np.power(np.float32(10000.0), np.arange(0, HD, 2).astype(np.float32) / np.float32(HD))
    angle = np.tile(freq, 4)[:, None].astype(np.float32) * np.arange(CLIP, dtype=np.float32)[None, :]
    sign = np.where(np.arange(P) % HD < HD // 2, -1.0, 1.0).astype(np.float32)[:, None]
    lay["cos"] = np.cos(angle).astype(np.float32)
    lay["sin"] = (sign * np.sin(angle)).astype(np.float32)
    k, q = np.arange(P)[:, None], np.arange(P)[None, :]
    lay["maskT"] = ((q // CLIP == k // CLIP) & (k <= q)).astype(np.float32)


def lay_ternary_mlp(lay, f):
    def left(w):
        return w.reshape(-1, P, DC, P).transpose(3, 0, 2, 1).reshape(P, -1)
    lay["w_ter"] = np.stack([left(f["L1_ffn_w1"]), left(f["L1_ffn_w2"]),
                             f["L1_ffn_w3"].T.reshape(-1, P, D).transpose(1, 0, 2).reshape(P, -1)])


def kernel(**inputs):
    import concourse.bacc as bacc
    from concourse.bass_utils import run_bass_kernel_spmd

    f = {k: np.ascontiguousarray(v) for k, v in inputs.items()}
    lay = {"ident": np.eye(P, dtype=np.float32)}
    for fill in (lay_token, lay_attention, lay_memory_mlp, lay_rotary_attention, lay_ternary_mlp):
        fill(lay, f)
    lay = {k: np.ascontiguousarray(v) for k, v in lay.items()}
    nc = bacc.Bacc("TRN2", target_bir_lowering=False, num_devices=1)
    a = {k: nc.dram_tensor(f"in_{k}", v.shape, F32, kind="ExternalInput").ap() for k, v in lay.items()}
    out = nc.dram_tensor("out", (TILES, P, D), F32, kind="ExternalOutput").ap()
    program(nc, a, out)
    r = run_bass_kernel_spmd(nc, [{f"in_{k}": v for k, v in lay.items()}], core_ids=[0])
    return r.results[0]["out"].reshape(CLIPS, CLIP, D)
```
